# Optimizing a Trainium2 kernel written in Bass

```python
import numpy as np
import jax
import jax.numpy as jnp

def _softmax(x, axis=-1):
    return jax.nn.softmax(x, axis=axis)

def _gelu(x):
    return jax.nn.gelu(x, approximate=True)

def _silu(x):
    return jax.nn.silu(x)

def _sigmoid(x):
    return jax.nn.sigmoid(x)

def _layernorm(x, axis=-1, eps=1e-05):
    m = jnp.mean(x, axis=axis, keepdims=True)
    v = jnp.var(x, axis=axis, keepdims=True)
    return (x - m) / jnp.sqrt(v + eps)

def _scatter_add(tgt, idx, src, axis=0):
    return tgt.at[idx].add(src)

def _segment_sum(src, seg, n):
    return jax.ops.segment_sum(src, seg, n)
kernel_name = 'mk_adaln_d2_jaxref_r8_f75b19'

def setup_inputs(seed: int=0):
    np.random.seed(seed)
    _w = jnp.asarray

    def _L0_attn_setup():
        import jax, jax.numpy as jnp
        import numpy as np
        B_, L_, DM = (2, 512, 128)
        DST, KCONV, EXP, HD = (128, 4, 2, 64)
        DIN = EXP * DM
        DSSM = DIN
        NH = DSSM // HD
        CONV_DIM = DSSM + 2 * DST
        D_IN_PROJ = 2 * DIN + 2 * DST + NH
        CHUNK = 32
        EPS = 1e-12

        def _forward(u, W_in, b_in, conv_w, conv_b, dt_bias, A_log, D, norm_w, W_out, b_out):
            b, l, _ = u.shape
            zxbcdt = u @ W_in.T + b_in
            z = zxbcdt[..., :DSSM]
            xBC = zxbcdt[..., DSSM:DSSM + CONV_DIM]
            dt_raw = zxbcdt[..., DSSM + CONV_DIM:]
            xp = jnp.pad(xBC, ((0, 0), (KCONV - 1, 0), (0, 0)))
            acc = conv_b
            for k in range(KCONV):
                acc = acc + xp[:, k:k + l, :] * conv_w[:, k]
            xBC = jax.nn.silu(acc)
            x = xBC[..., :DSSM]
            Bm = xBC[..., DSSM:DSSM + DST]
            Cm = xBC[..., DSSM + DST:]
            dt = jax.nn.softplus(dt_raw + dt_bias)
            A = -jnp.exp(A_log)
            nc = l // CHUNK
            xc = x.reshape(b, nc, CHUNK, NH, HD)
            dtc = dt.reshape(b, nc, CHUNK, NH)
            Bc = Bm.reshape(b, nc, CHUNK, DST)
            Cc = Cm.reshape(b, nc, CHUNK, DST)
            dA = dtc * A
            dA_cs = jnp.cumsum(dA, axis=2)
            seg = dA_cs[:, :, :, None, :] - dA_cs[:, :, None, :, :]
            mask = jnp.tril(jnp.ones((CHUNK, CHUNK), bool))[None, None, :, :, None]
            Lmat = jnp.exp(jnp.where(mask, seg, -jnp.inf))
            Y_diag = jnp.einsum('bcin,bcjn,bcijh,bcjh,bcjhp->bcihp', Cc, Bc, Lmat, dtc, xc)
            decay_states = jnp.exp(dA_cs[:, :, -1:, :] - dA_cs)
            states = jnp.einsum('bcln,bclh,bclhp->bchpn', Bc, decay_states * dtc, xc)
            chunk_decay = jnp.exp(dA_cs[:, :, -1, :])

            def step(carry, inp):
                dec, st = inp
                return (dec[:, :, None, None] * carry + st, carry)
            init = jnp.zeros((b, NH, HD, DST), x.dtype)
            _, prev_states = jax.lax.scan(step, init, (jnp.moveaxis(chunk_decay, 1, 0), jnp.moveaxis(states, 1, 0)))
            prev_states = jnp.moveaxis(prev_states, 0, 1)
            Y_off = jnp.einsum('bcln,bchpn,bclh->bclhp', Cc, prev_states, jnp.exp(dA_cs))
            Y = Y_diag + Y_off + D[None, None, None, :, None] * xc
            y = Y.reshape(b, l, DSSM)
            y = y * jax.nn.silu(z)
            y = y * jax.lax.rsqrt(jnp.mean(y * y, axis=-1, keepdims=True) + EPS) * norm_w
            return y @ W_out.T + b_out
        key = jax.random.key(seed)
        ks = jax.random.split(key, 8)
        u = jax.random.normal(ks[0], (B_, L_, DM), jnp.float32)
        W_in = jax.random.normal(ks[1], (D_IN_PROJ, DM), jnp.float32) / np.sqrt(DM).astype(np.float32)
        b_in = jnp.zeros((D_IN_PROJ,), jnp.float32)
        conv_w = jax.random.normal(ks[2], (CONV_DIM, KCONV), jnp.float32) / np.sqrt(KCONV).astype(np.float32)
        conv_b = jnp.zeros((CONV_DIM,), jnp.float32)
        dt = jnp.exp(jax.random.uniform(ks[3], (NH,)) * (np.log(0.1) - np.log(0.001)) + np.log(0.001))
        dt = jnp.clip(dt, 0.0001)
        dt_bias = dt + jnp.log(-jnp.expm1(-dt))
        A_log = jnp.log(jax.random.uniform(ks[4], (NH,), minval=1.0, maxval=16.0))
        D = jnp.ones((NH,), jnp.float32)
        norm_w = jnp.ones((DSSM,), jnp.float32)
        W_out = jax.random.normal(ks[5], (DM, DIN), jnp.float32) / np.sqrt(DIN).astype(np.float32)
        b_out = jnp.zeros((DM,), jnp.float32)
        return dict(u=u, W_in=W_in, b_in=b_in, conv_w=conv_w, conv_b=conv_b, dt_bias=dt_bias, A_log=A_log, D=D, norm_w=norm_w, W_out=W_out, b_out=b_out)
    _L0_attn_in = _L0_attn_setup()

    def _L0_ffn_setup():
        import jax, jax.numpy as jnp
        import numpy as np
        B, S, D, F, E = (4, 256, 128, 512, 8)
        LN_EPS = 1e-05
        key = jax.random.key(seed)
        ks = jax.random.split(key, 6)
        sc = 0.02
        return {'x': jax.random.normal(ks[0], (B, S, D), dtype=jnp.float32), 'Wr': jax.random.normal(ks[1], (D, E), dtype=jnp.float32) * sc, 'br': jnp.zeros((E,), jnp.float32), 'ln_g': jnp.ones((D,), jnp.float32), 'ln_b': jnp.zeros((D,), jnp.float32), 'W1': jax.random.normal(ks[2], (E, D, F), dtype=jnp.float32) * sc, 'b1': jnp.zeros((E, F), jnp.float32), 'W2': jax.random.normal(ks[3], (E, F, D), dtype=jnp.float32) * sc, 'b2': jnp.zeros((E, D), jnp.float32)}
    _L0_ffn_in = _L0_ffn_setup()
    _L0_c = _w((lambda *s: np.random.randn(*s).astype(np.float32) * 0.05)(16, 128))
    _L0_wmod = _w((lambda *s: np.random.randn(*s).astype(np.float32) * 0.05)(128, 6 * 128) * 128 ** (-0.5))

    def _L1_attn_setup():
        import math
        import jax, jax.numpy as jnp
        import numpy as np
        N_HEAD = 16

        def _reference_tuple_inner(x, W_dq, W_uq, W_dkv, W_uk, W_uv, W_o):
            B, T, C = x.shape
            nh = N_HEAD
            hs = C // nh
            kvl = W_dkv.shape[0]
            k_eff = (W_dq.T @ W_uq.T @ W_uk).reshape(nh, hs, kvl)
            v_eff = (W_uv.T @ W_o.T).reshape(kvl, nh, hs).transpose(1, 0, 2)
            c_kv = x @ W_dkv.T
            q = (x @ W_dq.T @ W_uq.T).reshape(B, T, nh, hs).transpose(0, 2, 1, 3)
            q_lat = jnp.einsum('bhtd,hdl->bhtl', q, k_eff)
            attn = jnp.einsum('bhtl,bsl->bhts', q_lat, c_kv) / math.sqrt(hs)
            causal_mask = jnp.triu(jnp.ones((T, T), bool), k=1)
            attn = jnp.where(causal_mask[None, None], -jnp.inf, attn)
            attn = jax.nn.softmax(attn, axis=-1)
            ctx = jnp.einsum('bhts,bsl->bhtl', attn, c_kv)
            y = jnp.einsum('bhtl,hld->bhtd', ctx, v_eff).transpose(0, 2, 1, 3).reshape(B, T, C)
            return (y, c_kv)
        key = jax.random.key(seed)
        ks = jax.random.split(key, 7)
        B, T, C = (4, 256, 128)
        QL, KVL = (32, 32)
        s = 0.02
        return {'x': jax.random.normal(ks[0], (B, T, C), jnp.float32), 'W_dq': jax.random.normal(ks[1], (QL, C), jnp.float32) * s, 'W_uq': jax.random.normal(ks[2], (C, QL), jnp.float32) * s, 'W_dkv': jax.random.normal(ks[3], (KVL, C), jnp.float32) * s, 'W_uk': jax.random.normal(ks[4], (C, KVL), jnp.float32) * s, 'W_uv': jax.random.normal(ks[5], (C, KVL), jnp.float32) * s, 'W_o': jax.random.normal(ks[6], (C, C), jnp.float32) * s}
    _L1_attn_in = _L1_attn_setup()

    def _L1_ffn_setup():
        import jax, jax.numpy as jnp
        import numpy as np
        TOP_K = 2
        key = jax.random.key(seed)
        ks = jax.random.split(key, 6)
        B, T, H, E, F = (2, 256, 128, 8, 512)
        s = 0.02
        return {'hidden_states': jax.random.normal(ks[0], (B, T, H), dtype=jnp.float32), 'router_w': jax.random.normal(ks[1], (E, H), dtype=jnp.float32) * s, 'w1': jax.random.normal(ks[2], (E, F, H), dtype=jnp.float32) * s, 'b1': jax.random.normal(ks[3], (E, F), dtype=jnp.float32) * s, 'w2': jax.random.normal(ks[4], (E, H, F), dtype=jnp.float32) * s, 'b2': jax.random.normal(ks[5], (E, H), dtype=jnp.float32) * s}
    _L1_ffn_in = _L1_ffn_setup()
    _L1_c = _w((lambda *s: np.random.randn(*s).astype(np.float32) * 0.05)(16, 128))
    _L1_wmod = _w((lambda *s: np.random.randn(*s).astype(np.float32) * 0.05)(128, 6 * 128) * 128 ** (-0.5))
    _d = {'L0_attn_u': _L0_attn_in['u'], 'L0_attn_W_in': _L0_attn_in['W_in'], 'L0_attn_b_in': _L0_attn_in['b_in'], 'L0_attn_conv_w': _L0_attn_in['conv_w'], 'L0_attn_conv_b': _L0_attn_in['conv_b'], 'L0_attn_dt_bias': _L0_attn_in['dt_bias'], 'L0_attn_A_log': _L0_attn_in['A_log'], 'L0_attn_D': _L0_attn_in['D'], 'L0_attn_norm_w': _L0_attn_in['norm_w'], 'L0_attn_W_out': _L0_attn_in['W_out'], 'L0_attn_b_out': _L0_attn_in['b_out'], 'L0_ffn_Wr': _L0_ffn_in['Wr'], 'L0_ffn_br': _L0_ffn_in['br'], 'L0_ffn_ln_g': _L0_ffn_in['ln_g'], 'L0_ffn_ln_b': _L0_ffn_in['ln_b'], 'L0_ffn_W1': _L0_ffn_in['W1'], 'L0_ffn_b1': _L0_ffn_in['b1'], 'L0_ffn_W2': _L0_ffn_in['W2'], 'L0_ffn_b2': _L0_ffn_in['b2'], 'L0_c': _L0_c, 'L0_wmod': _L0_wmod, 'L1_attn_W_dq': _L1_attn_in['W_dq'], 'L1_attn_W_uq': _L1_attn_in['W_uq'], 'L1_attn_W_dkv': _L1_attn_in['W_dkv'], 'L1_attn_W_uk': _L1_attn_in['W_uk'], 'L1_attn_W_uv': _L1_attn_in['W_uv'], 'L1_attn_W_o': _L1_attn_in['W_o'], 'L1_ffn_router_w': _L1_ffn_in['router_w'], 'L1_ffn_w1': _L1_ffn_in['w1'], 'L1_ffn_b1': _L1_ffn_in['b1'], 'L1_ffn_w2': _L1_ffn_in['w2'], 'L1_ffn_b2': _L1_ffn_in['b2'], 'L1_c': _L1_c, 'L1_wmod': _L1_wmod}
    _x0 = _d['L0_attn_u']
    _d['L0_attn_u'] = jax.random.normal(jax.random.fold_in(jax.random.key(seed), 1), (16, 256, 128), dtype=_x0.dtype)
    del _x0
    return _d

def reference(L0_attn_u, L0_attn_W_in, L0_attn_b_in, L0_attn_conv_w, L0_attn_conv_b, L0_attn_dt_bias, L0_attn_A_log, L0_attn_D, L0_attn_norm_w, L0_attn_W_out, L0_attn_b_out, L0_ffn_Wr, L0_ffn_br, L0_ffn_ln_g, L0_ffn_ln_b, L0_ffn_W1, L0_ffn_b1, L0_ffn_W2, L0_ffn_b2, L0_c, L0_wmod, L1_attn_W_dq, L1_attn_W_uq, L1_attn_W_dkv, L1_attn_W_uk, L1_attn_W_uv, L1_attn_W_o, L1_ffn_router_w, L1_ffn_w1, L1_ffn_b1, L1_ffn_w2, L1_ffn_b2, L1_c, L1_wmod):

    def _L0_attn_ref(u, W_in, b_in, conv_w, conv_b, dt_bias, A_log, D, norm_w, W_out, b_out):
        import jax, jax.numpy as jnp
        import numpy as np
        B_, L_, DM = (2, 512, 128)
        DST, KCONV, EXP, HD = (128, 4, 2, 64)
        DIN = EXP * DM
        DSSM = DIN
        NH = DSSM // HD
        CONV_DIM = DSSM + 2 * DST
        D_IN_PROJ = 2 * DIN + 2 * DST + NH
        CHUNK = 32
        EPS = 1e-12

        def _forward(u, W_in, b_in, conv_w, conv_b, dt_bias, A_log, D, norm_w, W_out, b_out):
            b, l, _ = u.shape
            zxbcdt = u @ W_in.T + b_in
            z = zxbcdt[..., :DSSM]
            xBC = zxbcdt[..., DSSM:DSSM + CONV_DIM]
            dt_raw = zxbcdt[..., DSSM + CONV_DIM:]
            xp = jnp.pad(xBC, ((0, 0), (KCONV - 1, 0), (0, 0)))
            acc = conv_b
            for k in range(KCONV):
                acc = acc + xp[:, k:k + l, :] * conv_w[:, k]
            xBC = jax.nn.silu(acc)
            x = xBC[..., :DSSM]
            Bm = xBC[..., DSSM:DSSM + DST]
            Cm = xBC[..., DSSM + DST:]
            dt = jax.nn.softplus(dt_raw + dt_bias)
            A = -jnp.exp(A_log)
            nc = l // CHUNK
            xc = x.reshape(b, nc, CHUNK, NH, HD)
            dtc = dt.reshape(b, nc, CHUNK, NH)
            Bc = Bm.reshape(b, nc, CHUNK, DST)
            Cc = Cm.reshape(b, nc, CHUNK, DST)
            dA = dtc * A
            dA_cs = jnp.cumsum(dA, axis=2)
            seg = dA_cs[:, :, :, None, :] - dA_cs[:, :, None, :, :]
            mask = jnp.tril(jnp.ones((CHUNK, CHUNK), bool))[None, None, :, :, None]
            Lmat = jnp.exp(jnp.where(mask, seg, -jnp.inf))
            Y_diag = jnp.einsum('bcin,bcjn,bcijh,bcjh,bcjhp->bcihp', Cc, Bc, Lmat, dtc, xc)
            decay_states = jnp.exp(dA_cs[:, :, -1:, :] - dA_cs)
            states = jnp.einsum('bcln,bclh,bclhp->bchpn', Bc, decay_states * dtc, xc)
            chunk_decay = jnp.exp(dA_cs[:, :, -1, :])

            def step(carry, inp):
                dec, st = inp
                return (dec[:, :, None, None] * carry + st, carry)
            init = jnp.zeros((b, NH, HD, DST), x.dtype)
            _, prev_states = jax.lax.scan(step, init, (jnp.moveaxis(chunk_decay, 1, 0), jnp.moveaxis(states, 1, 0)))
            prev_states = jnp.moveaxis(prev_states, 0, 1)
            Y_off = jnp.einsum('bcln,bchpn,bclh->bclhp', Cc, prev_states, jnp.exp(dA_cs))
            Y = Y_diag + Y_off + D[None, None, None, :, None] * xc
            y = Y.reshape(b, l, DSSM)
            y = y * jax.nn.silu(z)
            y = y * jax.lax.rsqrt(jnp.mean(y * y, axis=-1, keepdims=True) + EPS) * norm_w
            return y @ W_out.T + b_out
        return _forward(u, W_in, b_in, conv_w, conv_b, dt_bias, A_log, D, norm_w, W_out, b_out)

    def _L0_ffn_ref(x, Wr, br, ln_g, ln_b, W1, b1, W2, b2):
        import jax, jax.numpy as jnp
        import numpy as np
        B, S, D, F, E = (4, 256, 128, 512, 8)
        LN_EPS = 1e-05
        tokens_shape = x.shape[:-1]
        xt = x.reshape(-1, x.shape[-1])
        router_logits = xt @ Wr + br
        router_probs = jax.nn.softmax(router_logits, axis=-1)
        gates = jnp.max(router_probs, axis=-1, keepdims=True)
        idx = jnp.argmax(router_probs, axis=-1)
        onehot = jax.nn.one_hot(idx, E, dtype=xt.dtype)
        mu = jnp.mean(xt, axis=-1, keepdims=True)
        var = jnp.mean(jnp.square(xt - mu), axis=-1, keepdims=True)
        xn = (xt - mu) * jax.lax.rsqrt(var + LN_EPS) * ln_g + ln_b
        h = jnp.einsum('te,td,edf->tf', onehot, xn, W1) + b1[idx]
        h = jax.nn.relu(h)
        y = jnp.einsum('te,tf,efd->td', onehot, h, W2) + b2[idx]
        y = y * gates
        return y.reshape(tokens_shape + (y.shape[-1],))

    def _L1_attn_ref(x, W_dq, W_uq, W_dkv, W_uk, W_uv, W_o):
        import math
        import jax, jax.numpy as jnp
        import numpy as np
        N_HEAD = 16

        def _reference_tuple_inner(x, W_dq, W_uq, W_dkv, W_uk, W_uv, W_o):
            B, T, C = x.shape
            nh = N_HEAD
            hs = C // nh
            kvl = W_dkv.shape[0]
            k_eff = (W_dq.T @ W_uq.T @ W_uk).reshape(nh, hs, kvl)
            v_eff = (W_uv.T @ W_o.T).reshape(kvl, nh, hs).transpose(1, 0, 2)
            c_kv = x @ W_dkv.T
            q = (x @ W_dq.T @ W_uq.T).reshape(B, T, nh, hs).transpose(0, 2, 1, 3)
            q_lat = jnp.einsum('bhtd,hdl->bhtl', q, k_eff)
            attn = jnp.einsum('bhtl,bsl->bhts', q_lat, c_kv) / math.sqrt(hs)
            causal_mask = jnp.triu(jnp.ones((T, T), bool), k=1)
            attn = jnp.where(causal_mask[None, None], -jnp.inf, attn)
            attn = jax.nn.softmax(attn, axis=-1)
            ctx = jnp.einsum('bhts,bsl->bhtl', attn, c_kv)
            y = jnp.einsum('bhtl,hld->bhtd', ctx, v_eff).transpose(0, 2, 1, 3).reshape(B, T, C)
            return (y, c_kv)
        return _reference_tuple_inner(x, W_dq, W_uq, W_dkv, W_uk, W_uv, W_o)[0]

    def _L1_ffn_ref(hidden_states, router_w, w1, b1, w2, b2):
        import jax, jax.numpy as jnp
        import numpy as np
        TOP_K = 2
        x = hidden_states
        router_logits = jnp.einsum('bth,eh->bte', x, router_w)
        topk_values, topk_indices = jax.lax.top_k(router_logits, TOP_K)
        topk_weights = jax.nn.softmax(topk_values.astype(jnp.float32), axis=-1).astype(x.dtype)
        h1 = jnp.einsum('bth,efh->btef', x, w1) + b1
        h1 = jax.nn.gelu(h1, approximate=False)
        expert_outputs = jnp.einsum('btef,ehf->bteh', h1, w2) + b2
        gather_idx = topk_indices[..., None]
        topk_expert_outputs = jnp.take_along_axis(expert_outputs, gather_idx, axis=2)
        mixed_output = jnp.sum(topk_expert_outputs * topk_weights[..., None], axis=2)
        return mixed_output
    x = L0_attn_u
    mod = (_silu(L0_c) @ L0_wmod).reshape(L0_c.shape[0], 6, 1, -1)
    sa, ca, ga, sb, cb, gb = (mod[:, 0], mod[:, 1], mod[:, 2], mod[:, 3], mod[:, 4], mod[:, 5])
    ga = (2 * (ga >= 0) - 1) * jnp.maximum(jnp.abs(ga), 0.25)
    gb = (2 * (gb >= 0) - 1) * jnp.maximum(jnp.abs(gb), 0.25)
    h = _layernorm(x, axis=-1) * (1 + ca) + sa
    x = x + ga * _L0_attn_ref(h, L0_attn_W_in, L0_attn_b_in, L0_attn_conv_w, L0_attn_conv_b, L0_attn_dt_bias, L0_attn_A_log, L0_attn_D, L0_attn_norm_w, L0_attn_W_out, L0_attn_b_out)
    h = _layernorm(x, axis=-1) * (1 + cb) + sb
    x = x + gb * _L0_ffn_ref(h, L0_ffn_Wr, L0_ffn_br, L0_ffn_ln_g, L0_ffn_ln_b, L0_ffn_W1, L0_ffn_b1, L0_ffn_W2, L0_ffn_b2)
    mod = (_silu(L1_c) @ L1_wmod).reshape(L1_c.shape[0], 6, 1, -1)
    sa, ca, ga, sb, cb, gb = (mod[:, 0], mod[:, 1], mod[:, 2], mod[:, 3], mod[:, 4], mod[:, 5])
    ga = (2 * (ga >= 0) - 1) * jnp.maximum(jnp.abs(ga), 0.25)
    gb = (2 * (gb >= 0) - 1) * jnp.maximum(jnp.abs(gb), 0.25)
    h = _layernorm(x, axis=-1) * (1 + ca) + sa
    x = x + ga * _L1_attn_ref(h, L1_attn_W_dq, L1_attn_W_uq, L1_attn_W_dkv, L1_attn_W_uk, L1_attn_W_uv, L1_attn_W_o)
    h = _layernorm(x, axis=-1) * (1 + cb) + sb
    x = x + gb * _L1_ffn_ref(h, L1_ffn_router_w, L1_ffn_w1, L1_ffn_b1, L1_ffn_w2, L1_ffn_b2)
    return x

_drawn_inputs = setup_inputs


def setup_inputs(seed=0):
    import zlib

    import numpy as np

    out = dict(_drawn_inputs(seed))
    spreads = {'L0_attn_b_in': (0.0, 0.1),
     'L0_attn_conv_b': (0.0, 0.1),
     'L0_attn_D': (1.0, 0.6),
     'L0_attn_norm_w': (1.0, 0.2),
     'L0_attn_b_out': (0.0, 0.351),
     'L0_ffn_br': (0.0, 0.8),
     'L0_ffn_ln_g': (1.0, 0.6),
     'L0_ffn_ln_b': (0.0, 0.8),
     'L0_ffn_b1': (0.0, 0.8),
     'L0_ffn_b2': (0.0, 0.8)}
    factors = {'L0_ffn_Wr': 8.0,
     'L0_ffn_W1': 8.0,
     'L0_ffn_W2': 8.0,
     'L1_attn_W_dq': 8.0,
     'L1_attn_W_uq': 8.0,
     'L1_attn_W_dkv': 8.0,
     'L1_attn_W_uk': 8.0,
     'L1_attn_W_uv': 8.0,
     'L1_attn_W_o': 8.0,
     'L1_ffn_router_w': 6.558,
     'L1_ffn_w1': 6.255,
     'L1_ffn_b1': 8.0,
     'L1_ffn_w2': 6.148,
     'L1_ffn_b2': 25.499,
     'L1_c': 5.699,
     'L1_wmod': 5.773}
    for name, (base, spread) in spreads.items():
        noise = np.random.default_rng([zlib.crc32(name.encode()), seed]).standard_normal(out[name].shape)
        drawn = base * np.exp(spread * noise) if base else spread * noise
        out[name] = jnp.asarray(drawn.astype(out[name].dtype))
    for name, factor in factors.items():
        out[name] = (out[name] * factor).astype(out[name].dtype)
    return out
```

```python
from contextlib import ExitStack

import concourse.bass as bass
from concourse import mybir

F32 = mybir.dt.float32
BF16 = mybir.dt.bfloat16
I32 = mybir.dt.int32
U32 = mybir.dt.uint32
ALU = mybir.AluOpType
ACT = mybir.ActivationFunctionType
AX = mybir.AxisListType

P = 128
SEQS = 16
SEQ_LEN = 256
D = 128
TILES = SEQS * SEQ_LEN // P
TOKENS = TILES * P
PAIRS = SEQS // 2
PT = TILES // PAIRS
PW = PT * P
E = 8
FF = 512
FB = FF // P
DSSM = 256
HEADS0 = 4
HD0 = 64
HEADS1 = 16
HD1 = 8
LAT = 32
EPS_LN = 1e-5
EPS_RMS = 1e-12
ROW = 132
REGION = TOKENS + P
XPAD = SEQ_LEN + 3
SHIFT, SCALE, GATE = 0, 1, 2
MASKED = -1.0e30
WEIGHT_PARTS = 4
WEIGHT_LOADS = 16 * (2 * WEIGHT_PARTS + 2)


def after(engine, sem, value):
    if isinstance(value, int) and value <= 0:
        return
    engine.wait_ge(sem, value)


def after_then(engine, sem, value, passed):
    after(engine, sem, value)
    engine.wait_ge(passed, 1)
    engine.nop(nofuse=True)


class Chain:

    def __init__(self, engine, sem):
        self.engine, self.sem, self.n = engine, sem, 0

    def restart(self):
        if self.n:
            self.engine.wait_ge(self.sem, self.n)
            self.engine.nop(nofuse=True)
            self.engine.sem_clear(self.sem)
            self.n = 0

    def link(self, instruction):
        self.n += 1
        instruction.then_inc(self.sem, 1)
        self.engine.wait_ge(self.sem, self.n)

    def announce(self, instruction, sem, value):
        instruction.then_inc(sem, 1)
        self.engine.wait_ge(sem, value)


def bc_last(ap, n):
    return ap.unsqueeze(2).broadcast_to([ap.shape[0], ap.shape[1], n])


def pipeline(engine, step, first, last, full_from, full_to):
    for k in range(first, full_from):
        step(k, k % 2, k)
    n = (full_to - full_from) // 2
    if n > 0:
        with engine.Fori(0, n) as i:
            for h in range(2):
                step(2 * i + (full_from + h), (full_from + h) % 2, None)
    for k in range(full_from + 2 * n, last + 1):
        step(k, k % 2, k)


def expert_tiles(layer):
    return ((layer + 1) * TOKENS + E * (P - 1)) // P


def build(nc, t, out, stop=5):
    top = ExitStack()
    with top:
        def sb_in(ctx, phase=""):
            return lambda name, shape, dt=F32: ctx.enter_context(nc.sbuf_tensor(phase + name, shape, dt))

        def ps_in(ctx, phase=""):
            return lambda name, shape, dt=F32: ctx.enter_context(nc.psum_tensor(phase + name, shape, dt))

        def sem(name):
            return top.enter_context(nc.semaphore(name))

        def phase_semaphores(ctx, of_phase):
            def phase_sem(name, kept=False):
                if kept:
                    return sem(name)
                of_phase.append(ctx.enter_context(nc.semaphore(name)))
                return of_phase[-1]
            return phase_sem

        def clear(of_phase):
            with nc.Block() as block:
                @block.sync
                def _(sp):
                    for used in of_phase:
                        sp.sem_clear(used)

        sb = sb_in(top)
        c = {}
        c["X"] = sb("X", [P, TILES, D])
        c["ident"] = sb("ident", [P, P])
        c["identb"] = sb("identb", [P, P], BF16)
        c["upto"] = sb("upto", [P, P])
        c["beyond"] = sb("beyond", [P, P])
        c["before"] = sb("before", [P, P])
        c["ones"] = sb("ones", [P, P])
        c["minus_half"] = sb("minus_half", [P, PT])
        c["iota8"] = sb("iota8", [P, E])
        c["region0"] = sb("region0", [P, E])
        c["token_id"] = sb("token_id", [P, TILES])
        c["gates"] = sb("gates", [P, 2, TILES])
        c["counts"] = sb("counts", [P, E])
        c["modT"] = [sb(f"modT{l}", [P, 3, SEQS]) for l in range(2)]
        c["pad_rows"] = sb("pad_rows", [P, ROW])
        c["W1"] = sb("W1", [P, E * FF])
        c["W2"] = sb("W2", [P, E * FB * D])
        c["b1"] = sb("b1", [P, E * FB])
        c["b2"] = sb("b2", [P, E * D])
        c["s_w"] = [sem(f"expert_weights{l}") for l in range(2)]
        c["mod_dram"] = [nc.dram_tensor(f"mod_rows{l}", (SEQS, 6 * D), F32).ap() for l in range(2)]
        c["routed"] = [nc.dram_tensor(f"routed{l}", (E * REGION, ROW), F32).ap() for l in range(2)]
        c["answers"] = [nc.dram_tensor(f"answers{l}", ((l + 1) * TOKENS + expert_tiles(l) * P, D), F32).ap()
                        for l in range(2)]
        c["parts_dram"] = nc.dram_tensor("qk_parts_dram", (3, P, 3, 2 * SEQ_LEN), BF16).ap()
        w = {}
        setup(nc, t, c, w, sb, sem)
        phases = (lambda sb, ps, sem: mamba(nc, t, c, w, sb, ps, sem),
                  lambda sb, ps, sem: experts(nc, c, sb, ps, sem, 0),
                  lambda sb, ps, sem: attention(nc, t, c, w, sb, ps, sem),
                  lambda sb, ps, sem: experts(nc, c, sb, ps, sem, 1),
                  lambda sb, ps, sem: finish(nc, c, out, sb, sem))
        for i, phase in enumerate(phases[:stop]):
            with ExitStack() as ctx:
                of_phase = []
                phase(sb_in(ctx, f"{i}_"), ps_in(ctx, f"{i}_"), phase_semaphores(ctx, of_phase))
                if i < len(phases) - 1:
                    clear(of_phase)
        if stop < 4:
            s_dbg = sem("s_dbg")
            with nc.Block() as block:
                @block.sync
                def _(sp):
                    sp.dma_start(out.rearrange("s (j p) d -> p (s j) d", p=P), c["X"][:, :, :]).then_inc(s_dbg, 16)
                    sp.wait_ge(s_dbg, 16)


def setup(nc, t, c, w, sb, sem):
    s_x = sem("s_x")
    s_small = sem("s_small")
    s_mod = sem("s_mod")
    s_modw = sem("s_modw")
    s_memset = sem("s_memset")
    s_masks = sem("s_masks")
    s_tanh = sem("s_tanh")
    s_silu = sem("s_silu")
    s_modps = sem("s_modps")
    s_v = sem("s_setup_chain")
    s_wps = sem("s_wps")
    s_wcp = sem("s_wcp")
    w["WinT"] = sb("WinT", [P, 772])
    w["WoT"] = sb("WoT", [P, 2, D])
    w["bin_ch"] = sb("bin_ch", [P, 6])
    w["conv_w"] = sb("conv_w", [P, 4, 4])
    w["conv_b"] = sb("conv_b", [P, 4])
    w["tap_bias"] = sb("tap_bias", [P, 4])
    w["D_ch"] = sb("D_ch", [P, 2])
    w["norm_ch"] = sb("norm_ch", [P, 2])
    w["heads_bc"] = sb("heads_bc", [P, 3, HEADS0])
    w["dt_bias"] = sb("dt_bias", [P, HEADS0])
    w["A"] = sb("A", [P, HEADS0])
    w["bout_bc"] = sb("bout_bc", [P, D])
    w["ln_bc"] = sb("ln_bc", [P, 2, D])
    w["br_bc"] = sb("br_bc", [P, E])
    w["Wr"] = [sb(f"Wr{l}", [P, E]) for l in range(2)]
    w["Wqkv"] = sb("Wqkv", [P, 3, D])
    with ExitStack() as ctx:
        sbx, psx = (lambda n, s, dt=F32: ctx.enter_context(nc.sbuf_tensor(n, s, dt))), \
                   (lambda n, s, dt=F32: ctx.enter_context(nc.psum_tensor(n, s, dt)))
        cT = sbx("cT", [P, 2, SEQS])
        th = sbx("th", [P, 2, SEQS])
        wmod = sbx("wmod", [P, 2, 6 * D])
        rows = sbx("mod_rows", [SEQS, 2, 6 * D])
        tmp = sbx("mod_tmp", [SEQS, 2, 2, D])
        sg = sbx("mod_sign", [SEQS, 2, 2, D])
        iop = sbx("iop", [P, P], I32)
        wdq = sbx("wdq", [LAT, D])
        wuqT = sbx("wuqT", [LAT, D])
        wdkv = sbx("wdkv", [LAT, D])
        wuk = sbx("wuk", [P, LAT])
        wuv = sbx("wuv", [P, LAT])
        woT = sbx("woT", [P, D])
        wqT = sbx("wqT", [P, D])
        keT = sbx("keT", [LAT, D])
        ve = sbx("ve", [LAT, D])
        mps = psx("mod_ps", [P, 2, 6, SEQS])
        rps = psx("row_ps", [P, 2, 2, 512])
        wps = psx("w_ps", [P, 3, D])
        wps2 = psx("w_ps2", [P, 3, D])
        block = ctx.enter_context(nc.Block())
        small = [
            (cT[:, 0, :], t["L0_c"]), (cT[:, 1, :], t["L1_c"]),
            (wmod[:, 0, :], t["L0_wmod"]), (wmod[:, 1, :], t["L1_wmod"]),
            (wdq[:, :], t["L1_attn_W_dq"]), (wuqT[:, :], t["L1_attn_W_uq"]), (wdkv[:, :], t["L1_attn_W_dkv"]),
            (wuk[:, :], t["L1_attn_W_uk"]), (wuv[:, :], t["L1_attn_W_uv"]), (woT[:, :], t["L1_attn_W_o"]),
            (w["WinT"][:, :], t["L0_attn_W_in"]),
            (w["WoT"][:, :, :], t["L0_attn_W_out"].rearrange("(b p) d -> p b d", p=P)),
            (w["bin_ch"][:, :], t["b_in_ch"]),
            (w["conv_w"][:, :, :], t["L0_attn_conv_w"]),
            (w["conv_b"][:, :], t["L0_attn_conv_b"]),
            (w["norm_ch"][:, :], t["L0_attn_norm_w"]),
            (w["heads_bc"][:, 0, :], t["b_in_dt"].partition_broadcast(P)),
            (w["heads_bc"][:, 1, :], t["L0_attn_dt_bias"].partition_broadcast(P)),
            (w["heads_bc"][:, 2, :], t["L0_attn_A_log"].partition_broadcast(P)),
            (w["bout_bc"][:, :], t["L0_attn_b_out"].partition_broadcast(P)),
            (w["ln_bc"][:, 0, :], t["L0_ffn_ln_g"].partition_broadcast(P)),
            (w["ln_bc"][:, 1, :], t["L0_ffn_ln_b"].partition_broadcast(P)),
            (w["br_bc"][:, :], t["L0_ffn_br"].partition_broadcast(P)),
            (w["Wr"][0][:, :], t["L0_ffn_Wr"]), (w["Wr"][1][:, :], t["L1_ffn_router_w"]),
        ]
        for h in range(HEADS0):
            small.append((w["D_ch"][HD0 * (h % 2):HD0 * (h % 2) + HD0, h // 2:h // 2 + 1],
                          t["L0_attn_D"][:, h:h + 1].partition_broadcast(HD0)))

        @block.sync
        def _(sp):
            for dst, src in small:
                sp.dma_start(dst, src).then_inc(s_small, 16)
            sp.wait_ge(s_mod, 1)
            for l in range(2):
                sp.dma_start(c["mod_dram"][l], rows[:, l, :]).then_inc(s_modw, 16)
            sp.wait_ge(s_modw, 32)

        @block.scalar
        def _(act):
            xv = t["L0_attn_u"].rearrange("s (j p) d -> p (s j) d", p=P)
            for q in range(4):
                act.dma_start(c["X"][:, 8 * q:8 * q + 8, :], xv[:, 8 * q:8 * q + 8, :]).then_inc(s_x, 16)
            act.wait_ge(s_small, 16 * len(small))
            nc.scalar.activation(th[:, :, :], cT[:, :, :], ACT.Tanh, scale=0.5).then_inc(s_tanh, 1)
            nc.scalar.activation(w["A"][:, :], w["heads_bc"][:, 2, :], ACT.Exp).then_inc(s_tanh, 1)
            act.wait_ge(s_x, 64)

        @block.gpsimd
        def _(pool):
            g = nc.gpsimd
            g.memset(c["ones"][:, :], 1.0).then_inc(s_memset, 1)
            for m in ("ident", "upto", "beyond", "before"):
                g.memset(c[m][:, :], 0.0 if m == "ident" else 1.0).then_inc(s_memset, 1)
            g.memset(c["identb"][:, :], 0.0).then_inc(s_memset, 1)
            g.memset(c["pad_rows"][:, :], 0.0).then_inc(s_memset, 1)
            g.memset(c["minus_half"][:, :], -0.5).then_inc(s_masks, 1)
            pool.wait_ge(s_memset, 7)
            for m, op, fill, sign in (("ident", ALU.not_equal, 1.0, 1), ("identb", ALU.not_equal, 1.0, 1),
                                      ("upto", ALU.is_ge, 0.0, -1), ("beyond", ALU.is_gt, 0.0, 1),
                                      ("before", ALU.is_gt, 0.0, -1)):
                g.affine_select(out=c[m][:, :], in_=c[m][:, :], compare_op=op, fill=fill, base=0,
                                pattern=[[-sign, P]], channel_multiplier=sign).then_inc(s_masks, 1)
            g.iota(c["iota8"][:, :], pattern=[[1, E]], base=0, channel_multiplier=0,
                   allow_small_or_imprecise_dtypes=True).then_inc(s_masks, 1)
            g.iota(c["region0"][:, :], pattern=[[REGION, E]], base=0, channel_multiplier=0,
                   allow_small_or_imprecise_dtypes=True).then_inc(s_masks, 1)
            g.iota(c["token_id"][:, :], pattern=[[P, TILES]], base=0, channel_multiplier=1,
                   allow_small_or_imprecise_dtypes=True).then_inc(s_masks, 1)

        @block.tensor
        def _(pe):
            pe.wait_ge(s_silu, 1)
            for l in range(2):
                for m in range(3):
                    nc.tensor.matmul(mps[:, l, m, :], wmod[:, l, m * D:(m + 1) * D], cT[:, l, :], start=True, stop=True)
                for h, (a, b) in enumerate(((0, 512), (512, 768))):
                    last = nc.tensor.matmul(rps[0:SEQS, l, h, 0:b - a], cT[:, l, :], wmod[:, l, a:b],
                                            start=True, stop=True)
            last.then_inc(s_modps, 1)
            nc.tensor.matmul(wps[:, 0, :], wdq[:, :], wuqT[:, :], start=True, stop=True)
            nc.tensor.matmul(wps[:, 1, :], wuqT[:, :], wdq[:, :], start=True, stop=True)
            nc.tensor.matmul(wps[0:LAT, 2, :], wuv[:, :], woT[:, :], start=True, stop=True).then_inc(s_wps, 1)
            pe.wait_ge(s_wcp, 3)
            nc.tensor.matmul(wps2[0:LAT, 0, :], wuk[:, :], wqT[:, :], start=True, stop=True).then_inc(s_wps, 1)
            pe.wait_ge(s_wcp, 4)
            nc.tensor.matmul(wps2[:, 1, :], wdkv[:, :], keT[:, :], start=True, stop=True)
            nc.tensor.matmul(wps2[:, 2, :], wdkv[:, :], ve[:, :], start=True, stop=True).then_inc(s_wps, 1)

        @block.vector
        def _(dve):
            v = Chain(dve, s_v)
            V = nc.vector
            dve.wait_ge(s_tanh, 2)
            v.link(V.tensor_scalar(cT[:, :, :], cT[:, :, :], 0.5, None, ALU.mult))
            V.scalar_tensor_tensor(cT[:, :, :], th[:, :, :], 1.0, cT[:, :, :], ALU.add, ALU.mult).then_inc(s_silu, 1)
            v.link(V.tensor_tensor(w["dt_bias"][:, :], w["heads_bc"][:, 0, :], w["heads_bc"][:, 1, :], ALU.add))
            v.link(V.tensor_scalar(w["A"][:, :], w["A"][:, :], -1.0, None, ALU.mult))
            v.link(V.tensor_scalar(w["conv_w"][:, :, :], w["conv_w"][:, :, :], 0.5, None, ALU.mult))
            v.link(V.tensor_scalar(w["conv_b"][:, :], w["conv_b"][:, :], 0.5, None, ALU.mult))
            v.link(V.tensor_tensor(w["tap_bias"][:, :], w["bin_ch"][:, 2:6], w["conv_w"][:, :, 3], ALU.mult))
            v.link(V.tensor_tensor(w["tap_bias"][:, :], w["tap_bias"][:, :], w["conv_b"][:, :], ALU.add))
            v.link(V.tensor_scalar(w["bin_ch"][:, 0:2], w["bin_ch"][:, 0:2], 0.5, None, ALU.mult))
            for b in range(2):
                v.link(V.tensor_scalar(w["WoT"][:, b, :], w["WoT"][:, b, :], w["norm_ch"][:, b:b + 1], None, ALU.mult))
            dve.wait_ge(s_wps, 1)
            V.tensor_copy(w["Wqkv"][:, 0, :], wps[:, 0, :]).then_inc(s_wcp, 1)
            V.tensor_copy(wqT[:, :], wps[:, 1, :]).then_inc(s_wcp, 1)
            V.tensor_copy(ve[:, :], wps[0:LAT, 2, :]).then_inc(s_wcp, 1)
            dve.wait_ge(s_wps, 2)
            V.tensor_copy(keT[:, :], wps2[0:LAT, 0, :]).then_inc(s_wcp, 1)
            dve.wait_ge(s_wps, 3)
            v.link(V.tensor_copy(w["Wqkv"][:, 1:3, :], wps2[:, 1:3, :]))
            dve.wait_ge(s_modps, 1)
            for l in range(2):
                v.link(V.tensor_copy(c["modT"][l][:, :, :], mps[:, l, 0:3, :]))
                v.link(V.tensor_scalar(c["modT"][l][:, SCALE, :], c["modT"][l][:, SCALE, :], 1.0, None, ALU.add))
                v.link(V.tensor_copy(rows[:, l, 0:512], rps[0:SEQS, l, 0, :]))
                v.link(V.tensor_copy(rows[:, l, 512:768], rps[0:SEQS, l, 1, 0:256]))
            r6 = rows[:, :, :].rearrange("s l (m d) -> s l m d", d=D)
            for g in range(2):
                m = 3 * g + GATE
                v.link(V.scalar_tensor_tensor(tmp[:, :, g, :], r6[:, :, m, :], -1.0, r6[:, :, m, :],
                                              ALU.mult, ALU.max))
                v.link(V.tensor_scalar(tmp[:, :, g, :], tmp[:, :, g, :], 0.25, None, ALU.max))
                v.link(V.tensor_scalar(sg[:, :, g, :], r6[:, :, m, :], 0.0, 2.0, ALU.is_ge, ALU.mult))
                v.link(V.tensor_scalar(sg[:, :, g, :], sg[:, :, g, :], -1.0, None, ALU.add))
                v.link(V.tensor_tensor(r6[:, :, m, :], tmp[:, :, g, :], sg[:, :, g, :], ALU.mult))
            v.link(V.tensor_scalar(r6[:, :, 3 + SCALE, :], r6[:, :, 3 + SCALE, :], 1.0, None, ALU.add))
            V.tensor_scalar(r6[:, :, SCALE, :], r6[:, :, SCALE, :], 1.0, None, ALU.add).then_inc(s_mod, 1)


def moments(V, v, x, stats, mv, tiles):
    for n in range(tiles):
        last = V.bn_stats(stats[:, n, :], x(n))
    v.link(last)
    for n in range(tiles):
        last = V.bn_aggr(mv[:, n, :], stats[:, n, :])
    return last


def normalize(V, x, xhat, mv, rstd, tiles):
    for n in range(tiles):
        last = V.tensor_scalar(xhat(n), x(n), mv[:, n, 0:1], rstd[:, n:n + 1], ALU.subtract, ALU.mult)
    return last


def inverse_root(G, ch, c, out, tmp, x, eps):
    ch.link(G.tensor_scalar(tmp, x, eps, None, ALU.add))
    return G.tensor_tensor(out, tmp, c["minus_half"][:, 0:tmp.shape[-1]], ALU.pow)


def tile_at(x, n):
    return x[:, n, :] if isinstance(n, int) else x[:, bass.ds(n, 1), :].rearrange("p o d -> p (o d)")


def cols(n, size):
    return slice(n, n + size) if isinstance(n, int) else bass.ds(n, size)


def route(V, v, c, logits, r, tiles, layer):
    top, idx, idxf, pick = r["top"], r["idx"], r["idxf"], r["pick"]
    for n in range(tiles):
        last = V.max(top[:, n, :], logits[:, n, :])
    v.link(last)
    for n in range(tiles):
        last = V.max_index(idx[:, n, :], top[:, n, :], logits[:, n, :])
    v.link(last)
    v.link(V.tensor_copy(idxf[:, :, :], idx[:, :, 0:2]))
    for k in range(layer + 1):
        last = V.tensor_tensor(pick[:, k, :, :], c["iota8"][:, :].unsqueeze(1).broadcast_to([P, tiles, E]),
                               bc_last(idxf[:, :, k], E), ALU.is_equal)
    return last


def place_rows(V, v, c, r, rank, total, tiles, layer):
    pick, slot, acc, base = r["pick"], r["slot"], r["acc"], r["base"]
    for n in range(tiles):
        v.link(V.tensor_tensor(base[:, n, :], c["counts"][:, :], c["region0"][:, :], ALU.add))
        v.link(V.tensor_tensor(c["counts"][:, :], c["counts"][:, :], total[:, n, :], ALU.add))
    v.link(V.tensor_tensor(base[:, :, :], base[:, :, :], rank, ALU.add))
    for k in range(layer + 1):
        v.link(V.tensor_tensor(acc[:, :, :], base[:, :, :], pick[:, k, :, :], ALU.mult))
        v.link(V.tensor_reduce(slot[:, k, :], acc[:, :, :], AX.X, ALU.add))


def mamba(nc, t, c, w, sb, ps, sem):
    X = c["X"]
    V, A, T = nc.vector, nc.scalar, nc.tensor
    hT = sb("hT", [P, PW])
    xpad = sb("xpad", [P, 4, 2, XPAD])
    acc = sb("acc", [P, 4, PW])
    th = sb("tanh_conv", [P, 4, PW])
    xs = [sb(f"xs{u}", [P, 4, PW]) for u in range(2)]
    zh = sb("zh", [P, 2, PW])
    thz = sb("tanh_z", [P, 2, PW])
    zs = [sb(f"zs{u}", [P, 2, PW]) for u in range(2)]
    xhat = sb("xhat", [P, PT, D])
    stats = sb("stats", [P, PT, 6])
    mv0, rstd0, rtmp = sb("mv0", [P, TILES, 2]), sb("rstd0", [P, TILES]), sb("rtmp", [P, 4, PT])
    mv1, rstd1 = sb("mv1", [P, PT, 2]), sb("rstd1", [P, PT])
    mv2, rstd2 = sb("mv2", [P, PT, 2]), sb("rstd2", [P, PT])
    sqs = sb("mean_square", [P, PT])
    dtr = sb("dt_raw", [P, PT, HEADS0])
    dte = sb("dt_exp", [P, PT, HEADS0])
    dtl = sb("dt_log", [P, PT, HEADS0])
    dtv = [sb(f"dt{u}", [P, PT, HEADS0]) for u in range(2)]
    dA = [sb(f"dA{u}", [P, PT, HEADS0]) for u in range(2)]
    uz = sb("dA_upto", [P, PT, HEADS0, P])
    L = [sb(f"decay{u}", [P, 2, 3, HEADS0, P]) for u in range(2)]
    sfx = sb("decay_to_end", [P, 2, HEADS0])
    cbm = sb("cb_masked", [P, 2, 3, P])
    mask3 = sb("mask3", [P, 3, P])
    xdt = [sb(f"x_dt{u}", [P, PT, HEADS0, HD0]) for u in range(2)]
    xde = [sb(f"x_dt_end{u}", [P, 2, HEADS0, HD0]) for u in range(2)]
    yg = sb("y_gated", [P, 2, PW])
    ysq = sb("y_square", [P, 2, PW])
    rms = sb("rms", [P, PT])
    res = sb("res", [P, PT, D])
    modbc = [sb(f"modbc{u}", [P, 2, 3, D]) for u in range(2)]
    h2 = sb("h2", [P, PT, D])
    h2T = sb("h2T", [P, PT, P])
    rows = [sb(f"rows{u}", [P, PT, ROW]) for u in range(2)]
    logits = sb("logits", [P, PT, E])
    diff = sb("logit_diff", [P, TILES, E])
    gsum = sb("gate_sum", [P, TILES])
    r = dict(top=sb("top", [P, PT, E]), idx=sb("idx", [P, PT, E], U32), idxf=sb("idxf", [P, PT, 2]),
             pick=sb("pick", [P, 1, PT, E]), slot=sb("slot", [P, 1, PT]), acc=sb("pick_acc", [P, PT, E]),
             base=sb("slot_base", [P, PT, E]))
    slot_i = [sb(f"slot_i{u}", [P, PT], I32) for u in range(2)]

    pT = ps("pT", [P, 512])
    pX = [ps(f"pX{i}", [P, 512]) for i in range(2)]
    pS = [ps(f"pS{i}", [P, HEADS0, P]) for i in range(2)]
    pC = ps("pC", [P, 512])
    pY = [ps(f"pY{i}", [P, 2, 2, P]) for i in range(2)]
    pCB = pC[:, 0:384].rearrange("p (k t) -> p k t", t=P)
    p_dt = pC[:, 384:400].rearrange("p (t h) -> p t h", h=HEADS0)
    p_ss = pC[:, 400:404]
    p_lg = pC[:, 404:436].rearrange("p (t e) -> p t e", e=E)
    p_rk = pC[:, 436:468].rearrange("p (t e) -> p t e", e=E)
    p_tot = pC[:, 468:500].rearrange("p (t e) -> p t e", e=E)

    names = ("zeroed xhat hT_ps hT x_ps x_free xpad_free conv tanh_c tanh_z xs zs dt_ps dt_in dt_e dt_l dA uz seg_ps "
             "decay cb_ps cbm xv_ps xv sfx M_pool M y_ps yg ysq out_ps x1 mod router_in h2T_ps h2T lg_ps pick rk_ps "
             "slot diff gate_e lg_read mv0 rstd0 mv1 rstd1 mv2 rstd2 ss_ps sqs rms").split()
    s = {n: sem("m_" + n) for n in names}
    s_mod = [sem(f"m_modbc{u}") for u in range(2)]
    s_scat = [sem(f"m_scatter{u}", kept=True) for u in range(2)]
    s_v, s_a, s_g = sem("m_dve"), sem("m_act"), sem("m_pool")

    def run_stages(k, static, stages):
        for lag, stage, u in stages:
            if static is None or 0 <= static - lag < PAIRS:
                stage(k - lag, u)

    def clip(value, most):
        return min(value, most) if isinstance(value, int) else value

    with nc.Block() as block:
        @block.sync
        def _(sp):
            load_expert_weights(sp, t, c, 0)
            def step(k, h, static):
                if static is None or static - 1 < PAIRS and static >= 1:
                    p, u = k - 1, (h + 1) % 2
                    after(sp, s["router_in"], p - 1)
                    src = c["mod_dram"][0].rearrange("s (m d) -> s m d", d=D)[bass.ds(2 * p, 2), 2:5, :]
                    sp.dma_start(modbc[u][:, :, :, :], src.partition_broadcast(P)).then_inc(s_mod[u], 16)

            pipeline(sp, step, 1, PAIRS, 4, 8)

        @block.gpsimd
        def _(pool):
            g = nc.gpsimd
            ch = Chain(pool, s_g)
            for b in range(4):
                ch.link(g.memset(xpad[:, b, :, 0:3], 0.0))
            for u in range(2):
                ch.link(g.memset(rows[u][:, :, :], 0.0))
            g.memset(mask3[:, 1, :], 1.0).then_inc(s["zeroed"], 1)
            for k in (0, 2):
                g.tensor_copy(mask3[:, k, :], c["upto"][:, :]).then_inc(s["zeroed"], 1)

            for n in range(PAIRS):
                pool.wait_ge(s["mv0"], n + 1)
                inverse_root(g, ch, c, rstd0[:, PT * n:PT * n + PT], rtmp[:, 0, :], mv0[:, PT * n:PT * n + PT, 1],
                             EPS_LN).then_inc(s["rstd0"], 1)
                pool.wait_ge(s["rstd0"], n + 1)

            def decay(p, u):
                after(pool, s["dA"], p + 1)
                after(pool, s["seg_ps"], 6 * p)
                for n in range(PT):
                    g.tensor_tensor(uz[:, n, :, :], bc_last(dA[u][:, n, :], P),
                                    c["upto"][:, :].unsqueeze(1).broadcast_to([P, HEADS0, P]),
                                    ALU.mult).then_inc(s["uz"], 1)

            def experts_norm(p, u):
                after_then(pool, s["mv2"], p + 1, s["rstd0"])
                inverse_root(g, ch, c, rstd2[:, :], rtmp[:, 2, :], mv2[:, :, 1], EPS_LN).then_inc(s["rstd2"], 1)

            def weigh(p, u):
                for q in range(2):
                    after(pool, s["sfx"], 2 * p + q + 1)
                    after(pool, s["cbm"], 2 * p + q + 1)
                    g.tensor_tensor(L[u][:, q, 0, :, :], L[u][:, q, 0, :, :],
                                    cbm[:, q, 0, :].unsqueeze(1).broadcast_to([P, HEADS0, P]),
                                    ALU.mult).then_inc(s["M_pool"], 1)

            def squares(p, u):
                after_then(pool, s["sqs"], p + 1, s["rstd0"])
                inverse_root(g, ch, c, rms[:, :], rtmp[:, 3, :], sqs[:, :], EPS_RMS).then_inc(s["rms"], 1)

            def scatter(p, u):
                after_then(pool, s["slot"], p + 1, s["rstd0"])
                for n in range(PT):
                    pool.indirect_dma_start(c["routed"][0], bass.IndirectOffsetOnAxis(ap=slot_i[u][:, n:n + 1], axis=0),
                                            rows[u][:, n, :], None).then_inc(s_scat[u], 16)

            def router_norm(p, u):
                after_then(pool, s["mv1"], p + 1, s["rstd0"])
                inverse_root(g, ch, c, rstd1[:, :], rtmp[:, 1, :], mv1[:, :, 1], EPS_LN).then_inc(s["rstd1"], 1)

            def step(k, h, static):
                ch.restart()
                run_stages(k, static, ((1, decay, 1 - h), (3, experts_norm, 1 - h), (1, weigh, 1 - h), (2, squares, h),
                                       (3, scatter, 1 - h), (2, router_norm, h)))
                ch.restart()

            pipeline(pool, step, 0, PAIRS + 2, 4, 8)
            for u in range(2):
                pool.wait_ge(s_scat[u], 16 * PT * PAIRS // 2)

        @block.scalar
        def _(act):
            def project(p, u):
                after(act, s["hT_ps"], p + 1)
                after(act, s["dt_ps"], p)
                for q in range(2):
                    seq = cols(2 * p + q, 1)
                    A.activation(hT[:, q * 256:q * 256 + 256], pT[:, q * 256:q * 256 + 256], ACT.Identity,
                                 bias=c["modT"][0][:, SHIFT, seq], scale=c["modT"][0][:, SCALE, seq])\
                        .then_inc(s["hT"], 1)
                for b in range(4):
                    after(act, s["x_ps"], 6 * p + b + 1)
                    after(act, s["conv"], 4 * p)
                    A.activation(xpad[:, b, :, 3:XPAD], pX[b % 2][:, :].rearrange("p (q t) -> p q t", q=2),
                                 ACT.Identity, bias=w["bin_ch"][:, 2 + b:3 + b]).then_inc(s["xpad_free"], 1)
                    after(act, s["xs"], 2 * p)
                    A.activation(acc[:, b, :], pX[b % 2][:, :], ACT.Identity, bias=w["tap_bias"][:, b:b + 1],
                                 scale=w["conv_w"][:, b, 3:4]).then_inc(s["x_free"], 1)
                for b in range(2):
                    after(act, s["x_ps"], 6 * p + b + 5)
                    after(act, s["zs"], p)
                    A.activation(zh[:, b, :], pX[b % 2][:, :], ACT.Identity, bias=w["bin_ch"][:, b:b + 1],
                                 scale=0.5).then_inc(s["x_free"], 1)
                after(act, s["x_free"], 6 * (p + 1))
                A.activation(thz[:, :, :], zh[:, :, :], ACT.Tanh).then_inc(s["tanh_z"], 1)
                for b in range(2):
                    after(act, s["conv"], 4 * p + 2 * b + 2)
                    A.activation(th[:, 2 * b:2 * b + 2, :], acc[:, 2 * b:2 * b + 2, :], ACT.Tanh)\
                        .then_inc(s["tanh_c"], 1)
                after(act, s["dt_in"], p + 1)
                A.activation(dte[:, :, :], dte[:, :, :], ACT.Exp).then_inc(s["dt_e"], 1)
                after(act, s["dt_e"], p + 1)
                A.activation(dtl[:, :, :], dte[:, :, :], ACT.Ln, bias=1.0).then_inc(s["dt_l"], 1)

            def decay(p, u):
                for n in range(6):
                    after(act, s["seg_ps"], 6 * p + n + 1)
                    after(act, s["y_ps"], 2 * (p - 1))
                    A.activation(L[u][:, n // 3, n % 3, :, :], pS[n % 2][:, :, :], ACT.Exp).then_inc(s["decay"], 1)

            def mixed(p, u):
                after(act, s["yg"], p + 1)
                after(act, s["ss_ps"], p)
                A.activation(ysq[:, :, :], yg[:, :, :], ACT.Square).then_inc(s["ysq"], 1)

            def router(p, u):
                after(act, s["h2T_ps"], p + 1)
                after(act, s["lg_ps"], p)
                A.activation(h2T[:, :, :], pT[:, :].rearrange("p (n t) -> p n t", t=P), ACT.Copy)\
                    .then_inc(s["h2T"], 1)

            def step(k, h, static):
                run_stages(k, static, ((2, mixed, h), (3, router, 1 - h), (1, decay, 1 - h), (0, project, h)))

            pipeline(act, step, 0, PAIRS + 2, 4, 8)
            act.wait_ge(s["diff"], PAIRS)
            A.activation(diff[:, :, :], diff[:, :, :], ACT.Exp).then_inc(s["gate_e"], 1)

        @block.tensor
        def _(pe):
            def project(p, u):
                after(pe, s["xhat"], p + 1)
                after(pe, s["xv"], 2 * p)
                after(pe, s["x1"], p - 2)
                for n in range(PT):
                    last = T.transpose(pT[:, n * P:n * P + P], xhat[:, n, :], c["ident"][:, :])
                last.then_inc(s["hT_ps"], 1)
                pe.wait_ge(s["hT"], 2 * (p + 1))
                for b in range(6):
                    col = (b + 2) % 6 * P
                    after(pe, s["x_free"], 6 * p + b - 1)
                    T.matmul(pX[b % 2][:, :], w["WinT"][:, col:col + P], hT[:, :], start=True, stop=True)\
                        .then_inc(s["x_ps"], 1)
                after(pe, s["slot"], p - 2)
                after(pe, s["sqs"], p - 1)
                after(pe, s["cbm"], 2 * p)
                for n in range(PT):
                    last = T.matmul(p_dt[:, n, :], hT[:, n * P:n * P + P], w["WinT"][:, 6 * P:6 * P + HEADS0],
                                    start=True, stop=True)
                last.then_inc(s["dt_ps"], 1)

            def decay(p, u):
                after(pe, s["xs"], 2 * p + 2)
                for q in range(2):
                    if q == 0:
                        after(pe, s["h2T"], p - 1)
                    else:
                        pe.wait_ge(s["xv"], 2 * p + 1)
                    for n in range(2):
                        for b in range(2):
                            last = T.transpose(pT[:, (2 * n + b) * P:(2 * n + b + 1) * P],
                                               xs[u][:, b, (2 * q + n) * P:(2 * q + n + 1) * P], c["ident"][:, :])
                    last.then_inc(s["xv_ps"], 1)
                    after(pe, s["cbm"], 2 * p + q)
                    if q == 0:
                        after(pe, s["lg_read"], p - 1)
                        after(pe, s["dt_in"], p + 1)
                    t0 = q * SEQ_LEN
                    T.matmul(pC[:, 0:256], xs[u][:, 2, t0:t0 + P], xs[u][:, 3, t0:t0 + 256], start=True, stop=True)
                    T.matmul(pC[:, 256:384], xs[u][:, 2, t0 + P:t0 + 256], xs[u][:, 3, t0 + P:t0 + 256],
                             start=True, stop=True).then_inc(s["cb_ps"], 1)
                    for k in range(3):
                        n = 3 * q + k
                        tile = 2 * q + (k > 0)
                        after(pe, s["uz"], PT * p + tile + 1)
                        after(pe, s["decay"], 6 * p + n - 1)
                        T.matmul(pS[n % 2][:, :, :], c["ones"][:, :] if k == 1 else c["beyond"][:, :],
                                 uz[:, tile, :, :], start=True, stop=True).then_inc(s["seg_ps"], 1)

            def mixed(p, u):
                after(pe, s["M_pool"], 2 * p + 2)
                after(pe, s["M"], 2 * p + 2)
                after(pe, s["yg"], p)
                for b in range(2):
                    for q in range(2):
                        for e in range(2):
                            h = 2 * b + e
                            o = slice(HD0 * e, HD0 * e + HD0)
                            T.matmul(pY[b][o, q, 0, :], xdt[u][:, 2 * q, h, :], L[u][:, q, 0, h, :],
                                     start=True, stop=True)
                            T.matmul(pY[b][o, q, 1, :], xde[u][:, q, h, :], L[u][:, q, 1, h, :],
                                     start=True, stop=False)
                            last = T.matmul(pY[b][o, q, 1, :], xdt[u][:, 2 * q + 1, h, :], L[u][:, q, 2, h, :],
                                            start=False, stop=True)
                    last.then_inc(s["y_ps"], 1)

            def output(p, u):
                pe.wait_ge(s["yg"], p + 1)
                after(pe, s["hT"], clip(2 * p + 6, 2 * PAIRS))
                after(pe, s["xv"], clip(2 * p + 4, 2 * PAIRS))
                after(pe, s["h2T"], p)
                for n in range(PT):
                    for b in range(2):
                        last = T.matmul(pT[:, n * P:n * P + P], yg[:, b, n * P:n * P + P], w["WoT"][:, b, :],
                                        start=(b == 0), stop=(b == 1))
                last.then_inc(s["out_ps"], 1)

            def squares(p, u):
                pe.wait_ge(s["ysq"], p + 1)
                after(pe, s["cbm"], clip(2 * p + 4, 2 * PAIRS))
                after(pe, s["lg_read"], p)
                for n in range(PT):
                    for b in range(2):
                        last = T.matmul(p_ss[:, n:n + 1], ysq[:, b, n * P:n * P + P], c["ones"][:, 0:1],
                                        start=(b == 0), stop=(b == 1))
                last.then_inc(s["ss_ps"], 1)

            def router(p, u):
                pe.wait_ge(s["router_in"], p + 1)
                for n in range(PT):
                    last = T.transpose(pT[:, n * P:n * P + P], h2[:, n, :], c["ident"][:, :])
                last.then_inc(s["h2T_ps"], 1)
                pe.wait_ge(s["h2T"], p + 1)
                after(pe, s["dt_in"], clip(p + 3, PAIRS))
                after(pe, s["slot"], p)
                for n in range(PT):
                    last = T.matmul(p_lg[:, n, :], h2T[:, n, :], w["Wr"][0][:, :], start=True, stop=True)
                last.then_inc(s["lg_ps"], 1)

            def ranks(p, u):
                pe.wait_ge(s["pick"], p + 1)
                after(pe, s["sqs"], clip(p + 2, PAIRS))
                T.matmul(p_rk, c["before"][:, :], r["pick"][:, 0, :, :], start=True, stop=True)
                T.matmul(p_tot, c["ones"][:, :], r["pick"][:, 0, :, :], start=True, stop=True).then_inc(s["rk_ps"], 1)

            def step(k, h, static):
                run_stages(k, static, ((2, mixed, h), (3, router, 1 - h), (1, decay, 1 - h), (2, squares, h),
                                       (3, ranks, 1 - h), (0, project, h), (2, output, h)))

            pipeline(pe, step, 0, PAIRS + 2, 4, 8)

        @block.vector
        def _(dve):
            v = Chain(dve, s_v)
            v.link(V.memset(c["counts"][:, :], 0.0))
            for n in range(PAIRS):
                moments(V, v, lambda i: X[:, PT * n + i, :], stats, mv0[:, PT * n:PT * n + PT, :], PT)\
                    .then_inc(s["mv0"], 1)
                dve.wait_ge(s["mv0"], n + 1)
            dve.wait_ge(s["rstd0"], PAIRS)
            dve.wait_ge(s["zeroed"], 3)
            def project(p, u):
                after(dve, s["hT_ps"], p)
                m, r0 = mv0[:, cols(PT * p, PT), :], rstd0[:, cols(PT * p, PT)]
                normalize(V, lambda n: tile_at(X, PT * p + n), lambda n: xhat[:, n, :], m, r0, PT)\
                    .then_inc(s["xhat"], 1)
                dve.wait_ge(s["xhat"], p + 1)
                for b in range(4):
                    after(dve, s["x_free"], 6 * p + b + 1)
                    a2 = acc[:, b, :].rearrange("p (q t) -> p q t", q=2)
                    for k in range(2):
                        v.link(V.scalar_tensor_tensor(a2, xpad[:, b, :, k:k + SEQ_LEN], w["conv_w"][:, b, k:k + 1], a2,
                                                      ALU.mult, ALU.add))
                    V.scalar_tensor_tensor(a2, xpad[:, b, :, 2:2 + SEQ_LEN], w["conv_w"][:, b, 2:3], a2,
                                           ALU.mult, ALU.add).then_inc(s["conv"], 1)
                    dve.wait_ge(s["conv"], 4 * p + b + 1)
                dve.wait_ge(s["dt_ps"], p + 1)
                v.link(V.tensor_tensor(dtr[:, :, :], p_dt,
                                       w["dt_bias"][:, :].unsqueeze(1).broadcast_to([P, PT, HEADS0]), ALU.add))
                V.scalar_tensor_tensor(dte[:, :, :], dtr[:, :, :], -1.0, dtr[:, :, :], ALU.mult, ALU.min).then_inc(s["dt_in"], 1)
                dve.wait_ge(s["dt_in"], p + 1)
                dve.wait_ge(s["tanh_z"], p + 1)
                after(dve, s["yg"], p - 1)
                V.scalar_tensor_tensor(zs[u][:, :, :], thz[:, :, :], 1.0, zh[:, :, :], ALU.add, ALU.mult)\
                    .then_inc(s["zs"], 1)
                dve.wait_ge(s["zs"], p + 1)
                for b in range(2):
                    dve.wait_ge(s["tanh_c"], 2 * p + b + 1)
                    V.scalar_tensor_tensor(xs[u][:, 2 * b:2 * b + 2, :], th[:, 2 * b:2 * b + 2, :], 1.0,
                                           acc[:, 2 * b:2 * b + 2, :], ALU.add, ALU.mult).then_inc(s["xs"], 1)
                    dve.wait_ge(s["xs"], 2 * p + b + 1)
                dve.wait_ge(s["dt_l"], p + 1)
                v.link(V.scalar_tensor_tensor(dtv[u][:, :, :], dtr[:, :, :], 0.0, dtl[:, :, :], ALU.max, ALU.add))
                V.tensor_tensor(dA[u][:, :, :], dtv[u][:, :, :],
                                w["A"][:, :].unsqueeze(1).broadcast_to([P, PT, HEADS0]), ALU.mult)\
                    .then_inc(s["dA"], 1)
                dve.wait_ge(s["dA"], p + 1)

            def decay(p, u):
                for q in range(2):
                    dve.wait_ge(s["cb_ps"], 2 * p + q + 1)
                    after(dve, s["M_pool"], 2 * p + q - 1)
                    V.tensor_tensor(cbm[:, q, :, :], pCB, mask3[:, :, :], ALU.mult).then_inc(s["cbm"], 1)
                    dve.wait_ge(s["cbm"], 2 * p + q + 1)
                    dve.wait_ge(s["xv_ps"], 2 * p + q + 1)
                    V.tensor_tensor(xdt[u][:, 2 * q:2 * q + 2, :, :].rearrange("p n h d -> p (n h) d"),
                                    pT[:, :].rearrange("p (n d) -> p n d", d=HD0),
                                    bc_last(dtv[u][:, 2 * q:2 * q + 2, :].rearrange("p n h -> p (n h)"), HD0),
                                    ALU.mult).then_inc(s["xv"], 1)
                    dve.wait_ge(s["xv"], 2 * p + q + 1)
                    dve.wait_ge(s["decay"], 6 * p + 3 * q + 1)
                    V.tensor_copy(sfx[:, q, :], L[u][:, q, 0, :, P - 1]).then_inc(s["sfx"], 1)
                    dve.wait_ge(s["sfx"], 2 * p + q + 1)
                    dve.wait_ge(s["sfx"], 2 * p + q + 1)
                    dve.wait_ge(s["xv"], 2 * p + q + 1)
                    v.link(V.tensor_tensor(xde[u][:, q, :, :], xdt[u][:, 2 * q, :, :], bc_last(sfx[:, q, :], HD0),
                                           ALU.mult))
                    dve.wait_ge(s["cbm"], 2 * p + q + 1)
                    for k in (1, 2):
                        dve.wait_ge(s["decay"], 6 * p + 3 * q + k + 1)
                        last = V.tensor_tensor(L[u][:, q, k, :, :], L[u][:, q, k, :, :],
                                               cbm[:, q, k, :].unsqueeze(1).broadcast_to([P, HEADS0, P]), ALU.mult)
                        v.link(last) if k == 1 else v.announce(last, s["M"], 2 * p + q + 1)

            def mixed(p, u):
                for b in range(2):
                    dve.wait_ge(s["y_ps"], 2 * p + b + 1)
                    v.link(V.scalar_tensor_tensor(yg[:, b, :], xs[u][:, b, :], w["D_ch"][:, b:b + 1],
                                                  pY[b][:, :, :, :].rearrange("p q k t -> p (q k t)"),
                                                  ALU.mult, ALU.add))
                V.tensor_tensor(yg[:, :, :], yg[:, :, :], zs[u][:, :, :], ALU.mult).then_inc(s["yg"], 1)
                dve.wait_ge(s["yg"], p + 1)

            def squares(p, u):
                dve.wait_ge(s["ss_ps"], p + 1)
                V.tensor_scalar(sqs[:, :], p_ss, 1.0 / DSSM, None, ALU.mult).then_inc(s["sqs"], 1)
                dve.wait_ge(s["sqs"], p + 1)

            def output(p, u):
                dve.wait_ge(s["out_ps"], p + 1)
                dve.wait_ge(s["rms"], p + 1)
                v.link(V.tensor_tensor(res[:, :, :], pT[:, :].rearrange("p (n d) -> p n d", d=D),
                                       bc_last(rms[:, :], D), ALU.mult))
                v.link(V.tensor_tensor(res[:, :, :], res[:, :, :],
                                       w["bout_bc"][:, :].unsqueeze(1).broadcast_to([P, PT, D]), ALU.add))
                after(dve, s_mod[u], 8 * p + (16 - 8 * u))
                for q in range(2):
                    last = V.tensor_tensor(res[:, 2 * q:2 * q + 2, :], res[:, 2 * q:2 * q + 2, :],
                                           modbc[u][:, q, 0, :].unsqueeze(1).broadcast_to([P, 2, D]), ALU.mult)
                v.link(last)
                x = X[:, cols(PT * p, PT), :]
                V.tensor_tensor(x, x, res[:, :, :], ALU.add).then_inc(s["x1"], 1)
                after_then(dve, s["x1"], p + 1, s["rstd0"])
                moments(V, v, lambda n: tile_at(X, PT * p + n), stats, mv1, PT).then_inc(s["mv1"], 1)
                dve.wait_ge(s["mv1"], p + 1)

            def router(p, u):
                dve.wait_ge(s["rstd1"], p + 1)
                v.link(normalize(V, lambda n: tile_at(X, PT * p + n), lambda n: h2[:, n, :], mv1, rstd1, PT))
                for m, op in ((2, ALU.mult), (1, ALU.add)):
                    for q in range(2):
                        last = V.tensor_tensor(h2[:, 2 * q:2 * q + 2, :], h2[:, 2 * q:2 * q + 2, :],
                                               modbc[u][:, q, m, :].unsqueeze(1).broadcast_to([P, 2, D]), op)
                    if m == 2:
                        v.link(last)
                last.then_inc(s["router_in"], 1)
                after_then(dve, s["router_in"], p + 1, s["rstd0"])
                moments(V, v, lambda n: h2[:, n, :], stats, mv2, PT).then_inc(s["mv2"], 1)
                dve.wait_ge(s["mv2"], p + 1)
                dve.wait_ge(s["lg_ps"], p + 1)
                v.announce(V.tensor_tensor(logits[:, :, :], p_lg,
                                         w["br_bc"][:, :].unsqueeze(1).broadcast_to([P, PT, E]), ALU.add),
                         s["lg_read"], p + 1)
                dve.wait_ge(s["rstd0"], 1)
                dve.nop(nofuse=True)
                route(V, v, c, logits, r, PT, 0).then_inc(s["pick"], 1)
                dve.wait_ge(s["pick"], p + 1)
                V.tensor_tensor(diff[:, cols(PT * p, PT), :], logits[:, :, :], bc_last(r["top"][:, :, 0], E),
                                ALU.subtract).then_inc(s["diff"], 1)
                dve.wait_ge(s["diff"], p + 1)

            def place(p, u):
                dve.wait_ge(s["rstd2"], p + 1)
                after(dve, s_scat[1 - u], 32 * p + 32 * u)
                v.link(normalize(V, lambda n: h2[:, n, :], lambda n: rows[u][:, n, 0:D], mv2, rstd2, PT))
                for m, op in ((0, ALU.mult), (1, ALU.add)):
                    v.link(V.tensor_tensor(rows[u][:, :, 0:D], rows[u][:, :, 0:D],
                                           w["ln_bc"][:, m, :].unsqueeze(1).broadcast_to([P, PT, D]), op))
                V.tensor_copy(rows[u][:, :, D], c["token_id"][:, cols(PT * p, PT)])
                dve.wait_ge(s["rk_ps"], p + 1)
                place_rows(V, v, c, r, p_rk, p_tot, PT, 0)
                V.tensor_copy(slot_i[u][:, :], r["slot"][:, 0, :]).then_inc(s["slot"], 1)
                dve.wait_ge(s["slot"], p + 1)

            def step(k, h, static):
                for lag, stage, u in ((2, mixed, h), (3, router, 1 - h), (1, decay, 1 - h), (2, squares, h),
                                      (3, place, 1 - h), (0, project, h), (2, output, h)):
                    if static is None or 0 <= static - lag < PAIRS:
                        v.restart()
                        stage(k - lag, u)
                v.restart()

            pipeline(dve, step, 0, PAIRS + 2, 4, 8)
            dve.wait_ge(s["gate_e"], 1)
            v.link(V.tensor_reduce(gsum[:, :], diff[:, :, :], AX.X, ALU.add))
            v.link(V.reciprocal(c["gates"][:, 0, :], gsum[:, :]))


class Turn:

    def __init__(self, k, first, lap0, static, rings):
        self.k, self.first, self.lap0, self.static, self.rings = k, first, lap0, static, rings

    def unit(self, lag):
        return self.k - lag

    def ring(self, lag):
        return (self.first - lag) % self.rings

    def lap(self, lag):
        return self.lap0 + (self.first - lag) // self.rings

    def has(self, lag, units):
        return self.static is None or 0 <= self.static - lag < units


def turns(engine, rings, step, last, full_from, full_to):
    for k in range(full_from):
        step(Turn(k, k % rings, k // rings, k, rings))
    n = (full_to - full_from) // rings
    with engine.Fori(0, n) as i:
        for h in range(rings):
            step(Turn(rings * i + (full_from + h), h, i + full_from // rings, None, rings))
    for k in range(full_from + rings * n, last + 1):
        step(Turn(k, k % rings, k // rings, k, rings))


def attention(nc, t, c, w, sb, ps, sem):
    X = c["X"]
    V, A, T = nc.vector, nc.scalar, nc.tensor
    S2 = SEQ_LEN // P
    H, KR = HEADS1, 6 * HD1
    a0 = [sb(f"a0_{u}", [P, S2, D]) for u in range(3)]
    gbc = [sb(f"gate0_bc{u}", [P, D]) for u in range(3)]
    modbc = [sb(f"modbc{u}", [P, 3, D]) for u in range(3)]
    mv0, rstd0 = [sb(f"mv0_{u}", [P, S2, 2]) for u in range(3)], [sb(f"rstd0_{u}", [P, S2]) for u in range(3)]
    mv1, rstd1 = [sb(f"mv1_{u}", [P, S2, 2]) for u in range(3)], [sb(f"rstd1_{u}", [P, S2]) for u in range(3)]
    stats, rtmp = sb("stats", [P, S2, 6]), sb("rtmp", [P, 2, S2])
    res = sb("res", [P, S2, D])
    xhat = sb("xhat", [P, S2, D])
    hT = sb("hT", [P, SEQ_LEN])
    parts = [sb(f"qk_parts{u}", [P, 3, 2 * SEQ_LEN], BF16) for u in range(3)]
    rest = sb("qk_rest", [P, 2 * SEQ_LEN])
    vv = [sb(f"v_ones{u}", [P, S2, H, LAT]) for u in range(3)]
    Q = [sb(f"q_rows{u}", [P, H, SEQ_LEN], BF16) for u in range(3)]
    K = [sb(f"k_rows{u}", [P, H, SEQ_LEN], BF16) for u in range(3)]
    maskq, maskk = sb("mask_q", [P, 4, P], BF16), sb("mask_k", [P, 4, P], BF16)
    mx = sb("row_max", [P, 3, H])
    nm = sb("neg_max", [P, S2, H])
    mT = sb("max_parts", [H, 2, SEQ_LEN], BF16)
    pr = [sb(f"probs{i}", [P, 4, P]) for i in range(6)]
    oT = sb("out_T", [P, 4, SEQ_LEN])
    rden = sb("rden", [P, H])
    yv = sb("y_tok", [P, S2, H, HD1])
    h2T = sb("h2T", [P, S2, P])
    rows = [sb(f"rows{u}", [P, 2, S2, ROW]) for u in range(3)]
    top2 = sb("top2", [P, TILES, 2])
    logits = sb("logits", [P, S2, E])
    r = dict(top=sb("top", [P, S2, E]), idx=sb("idx", [P, S2, E], U32), idxf=sb("idxf", [P, S2, 2]),
             pick=sb("pick", [P, 2, S2, E]), slot=sb("slot", [P, 2, S2]),
             acc=sb("pick_acc", [P, S2, E]), base=sb("slot_base", [P, S2, E]))
    both = sb("pick_both", [P, S2, E])
    slot_i = [sb(f"slot_i{u}", [P, 2, S2], I32) for u in range(3)]
    gexp = sb("gate_exp", [P, TILES])

    pT, pP = ps("pT", [P, 512]), ps("pP", [P, 512])
    pS = [ps(f"pS{i}", [P, 4, P]) for i in range(4)]
    pO = ps("pO", [P, 4, SEQ_LEN])
    p_lg = pT[:, 0:S2 * E].rearrange("p (n e) -> p n e", e=E)
    p_rk = pT[:, 0:S2 * E].rearrange("p (n e) -> p n e", e=E)
    p_tot = pT[:, S2 * E:2 * S2 * E].rearrange("p (n e) -> p n e", e=E)

    names = ("zeroed x2 mv0 rstd0 xhat hT_ps hT qk_ps part1 rest1 part2 parts v_ps v scores max neg mT_ps m1 m2 "
             "probs_ps probs pv oT yT_ps yT x3 mv1 rstd1 h2 h2T_ps h2T lg_ps lg_read pick rk_ps slot gexp").split()
    s = {n: sem("a_" + n) for n in names}
    s_a0, s_mod, s_dram, s_qk, s_m = ([sem(f"a_{n}{u}") for u in range(3)] for n in
                                      ("answers", "modbc", "parts_dram", "packed", "max_rows"))
    s_scat = [sem(f"a_scatter{u}", kept=True) for u in range(3)]
    s_v, s_g = sem("a_dve"), sem("a_pool")
    ZEROED = 12

    def clip(value, most):
        return min(value, most) if isinstance(value, int) else value

    def bank_free(engine, turn, users):
        for name, value, most in users[:1] if turn.static is None else users:
            after(engine, s[name], clip(value, most))

    UNITS = [(g, m) for g in range(4) for m in range(3)]
    TILE_PAIR = ((0, 0), (0, 1), (1, 1))

    with nc.Block() as block:
        @block.sync
        def _(sp):
            load_expert_weights(sp, t, c, 1)
            qp = c["parts_dram"]

            def load(p, u, lap):
                after(sp, s["x2"], p - 2)
                sp.dma_start(a0[u][:, :, :], c["answers"][0][cols(2 * P * p, 2 * P), :]
                             .rearrange("(n p) d -> p n d", p=P)).then_inc(s_a0[u], 16)
                m0 = c["mod_dram"][0].rearrange("s (m d) -> s m d", d=D)[cols(p, 1), 5:6, :]
                sp.dma_start(gbc[u][:, :], m0.rearrange("s m d -> (s m) d").rearrange("a d -> (a d)").partition_broadcast(P))\
                    .then_inc(s_a0[u], 16)

            def modulation(p, u, lap):
                after(sp, s["h2"], p - 2)
                m1 = c["mod_dram"][1].rearrange("s (m d) -> s m d", d=D)[cols(p, 1), 2:5, :]
                sp.dma_start(modbc[u][:, :, :], m1.rearrange("s m d -> (s m) d").partition_broadcast(P))\
                    .then_inc(s_mod[u], 16)

            def pack(p, u, lap):
                after(sp, s["parts"], p + 1)
                sp.dma_start(qp[u], parts[u][:, :, :]).then_inc(s_dram[u], 16)
                after(sp, s_dram[u], 16 * lap + 16)
                after(sp, s["probs_ps"], 12 * (p - 2))
                v = qp[u].rearrange("(h d) i t -> i d h t", d=HD1)
                for r6, (a, b) in enumerate(((0, 0), (1, 0), (2, 0), (0, 1), (1, 1), (0, 2))):
                    sp.dma_start(Q[u][r6 * HD1:r6 * HD1 + HD1, :, :], v[a][:, :, 0:SEQ_LEN]).then_inc(s_qk[u], 16)
                    sp.dma_start(K[u][r6 * HD1:r6 * HD1 + HD1, :, :], v[b][:, :, SEQ_LEN:2 * SEQ_LEN])\
                        .then_inc(s_qk[u], 16)
                sp.dma_start(Q[u][KR:KR + 2, :, :], Q[u][P - 2:P, :, :]).then_inc(s_qk[u], 16)

            def max_rows(p, u, lap):
                after(sp, s["m2"], p + 1)
                after(sp, s["scores"], 12 * p + 12)
                for i in range(2):
                    sp.dma_start(Q[u][KR + i:KR + i + 1, :, :], mT[:, i, :]).then_inc(s_m[u], 16)

            def step(tn):
                for lag, stage in ((4, max_rows), (2, pack), (0, load), (4, modulation)):
                    if tn.has(lag, SEQS):
                        stage(tn.unit(lag), tn.ring(lag), tn.lap(lag))

            sp.wait_ge(s["zeroed"], ZEROED)
            turns(sp, 3, step, SEQS + 3, 9, SEQS)

        @block.gpsimd
        def _(pool):
            g = nc.gpsimd
            ch = Chain(pool, s_g)
            for u in range(3):
                g.memset(Q[u][:, :, :], 0.0).then_inc(s["zeroed"], 1)
                ch.link(g.memset(K[u][:, :, :], 1.0))
                g.affine_select(out=K[u][:, :, :], in_=K[u][:, :, :], compare_op=ALU.is_ge, fill=0.0,
                                base=KR + 1, pattern=[[0, H * SEQ_LEN]], channel_multiplier=-1)\
                    .then_inc(s["zeroed"], 1)
                ch.link(g.memset(vv[u][:, :, :, :], 0.0))
                ch.link(g.memset(rows[u][:, :, :, :], 0.0))
                g.memset(vv[u][:, :, :, HD1:HD1 + 1], 1.0).then_inc(s["zeroed"], 1)
            for n, (m, sign) in enumerate(((maskq, 1), (maskk, -1))):
                ch.link(g.memset(m[:, :, :], 0.0))
                g.affine_select(out=m[:, :, :], in_=m[:, :, :], compare_op=ALU.is_ge, fill=MASKED, base=0,
                                pattern=[[0, 4], [-sign, P]], channel_multiplier=sign).then_inc(s["zeroed"], 1)
            g.memset(rtmp[:, :, :], 0.0).then_inc(s["zeroed"], 1)
            pool.wait_ge(s["zeroed"], ZEROED)

            def load(p, u):
                after_then(pool, s["mv0"], p + 1, s["zeroed"])
                inverse_root(g, ch, c, rstd0[u][:, :], rtmp[:, 0, :], mv0[u][:, :, 1], EPS_LN).then_inc(s["rstd0"], 1)

            def output(p, u):
                after_then(pool, s["mv1"], p + 1, s["zeroed"])
                inverse_root(g, ch, c, rstd1[u][:, :], rtmp[:, 1, :], mv1[u][:, :, 1], EPS_LN)\
                    .then_inc(s["rstd1"], 1)

            def scatter(p, u):
                after_then(pool, s["slot"], p + 1, s["zeroed"])
                for k in range(2):
                    for n in range(S2):
                        pool.indirect_dma_start(c["routed"][1],
                                                bass.IndirectOffsetOnAxis(ap=slot_i[u][:, k, n:n + 1], axis=0),
                                                rows[u][:, k, n, :], None).then_inc(s_scat[u], 16)

            def step(tn):
                ch.restart()
                for lag, stage in ((6, scatter), (5, output), (0, load)):
                    if tn.has(lag, SEQS):
                        stage(tn.unit(lag), tn.ring(lag))
                ch.restart()

            turns(pool, 3, step, SEQS + 5, 9, SEQS)
            for u in range(3):
                pool.wait_ge(s_scat[u], 16 * 4 * len(range(u, SEQS, 3)))

        @block.scalar
        def _(act):
            def project(p, u, lap):
                after(act, s["hT_ps"], p + 1)
                after(act, s["v_ps"], p)
                A.activation(hT[:, :], pT[:, 0:SEQ_LEN], ACT.Identity, bias=c["modT"][1][:, SHIFT, cols(p, 1)],
                             scale=c["modT"][1][:, SCALE, cols(p, 1)]).then_inc(s["hT"], 1)

            def router(p, u, lap):
                after(act, s["h2T_ps"], p + 1)
                after(act, s["lg_ps"], p)
                A.activation(h2T[:, :, :], pP[:, 0:SEQ_LEN].rearrange("p (n t) -> p n t", t=P), ACT.Copy)\
                    .then_inc(s["h2T"], 1)

            def split(p, u, lap):
                after(act, s["qk_ps"], p + 1)
                after(act, s_dram[u], 16 * lap)
                A.activation(parts[u][:, 0, :], pP[:, :], ACT.Copy).then_inc(s["part1"], 1)
                after(act, s["rest1"], p + 1)
                A.activation(parts[u][:, 1, :], rest[:, :], ACT.Copy).then_inc(s["part2"], 1)

            def mix(p, u, lap):
                for i in range(12):
                    after(act, s["probs_ps"], 12 * p + i + 1)
                    after(act, s["pv"], 4 * p + i // 3 - 1)
                    A.activation(pr[i % 6][:, :, :], pS[i % 4][:, :, :], ACT.Exp, scale=HD1 ** -0.5)\
                        .then_inc(s["probs"], 1)
                after(act, s["pv"], 4 * p + 4)
                after(act, s["yT_ps"], 2 * p)
                A.activation(oT[:, :, :], pO[:, :, :], ACT.Copy).then_inc(s["oT"], 1)

            def maxima(p, u, lap):
                after(act, s["mT_ps"], p + 1)
                if tn_static[0] is None or p >= 1:
                    before, blap = (u - 1) % 3, lap if u else lap - 1
                    after(act, s_m[before], 32 * blap + 32)
                A.activation(mT[:, 0, :], pT[0:H, 0:SEQ_LEN], ACT.Copy).then_inc(s["m1"], 1)

            tn_static = [0]

            def step(tn):
                tn_static[0] = tn.static
                for lag, stage in ((1, project), (6, router), (1, split), (4, mix), (3, maxima)):
                    if tn.has(lag, SEQS):
                        stage(tn.unit(lag), tn.ring(lag), tn.lap(lag))

            turns(act, 3, step, SEQS + 5, 9, SEQS)
            act.wait_ge(s["gexp"], 1)
            A.activation(gexp[:, :], gexp[:, :], ACT.Exp).then_inc(s["gexp"], 1)

        @block.tensor
        def _(pe):
            def turn_input(tn):
                p = tn.unit(1)
                after(pe, s["xhat"], p + 1)
                bank_free(pe, tn, [("m2", p - 2, SEQS), ("slot", p - 5, SEQS), ("hT", p, SEQS)])
                for n in range(S2):
                    last = T.transpose(pT[:, n * P:n * P + P], xhat[:, n, :], c["ident"][:, :])
                last.then_inc(s["hT_ps"], 1)

            def turn_router(tn):
                p = tn.unit(6)
                after(pe, s["h2"], p + 1)
                bank_free(pe, tn, [("v", p + 5, SEQS), ("yT", 2 * p + 2, 2 * SEQS)])
                for n in range(S2):
                    last = T.transpose(pP[:, n * P:n * P + P], rows[tn.ring(6)][:, 0, n, 0:D], c["ident"][:, :])
                last.then_inc(s["h2T_ps"], 1)

            def maxima(tn, units):
                p, u = tn.unit(3), tn.ring(3)
                if units[0] == 0:
                    after(pe, s_qk[u], 16 * 13 * tn.lap(3) + 16 * 13)
                for i in units:
                    g, m = UNITS[i]
                    kt, qt = TILE_PAIR[m]
                    if i < 4:
                        after(pe, s["probs"], 12 * (p - 1) - 3 + i)
                    else:
                        after(pe, s["max"], 12 * p + i - 3)
                    if kt == qt:
                        T.matmul(pS[i % 4][:, :, :], c["identb"][:, :], maskq[:, :, :], start=True, stop=False)
                    for h in range(4):
                        last = T.matmul(pS[i % 4][:, h, :], Q[u][:, 4 * g + h, qt * P:qt * P + P],
                                        K[u][:, 4 * g + h, kt * P:kt * P + P], start=(kt != qt),
                                        stop=(kt != qt or h == 3))
                    last.then_inc(s["scores"], 1)

            def logits_(tn):
                p = tn.unit(6)
                after(pe, s["h2T"], p + 1)
                bank_free(pe, tn, [("hT", p + 6, SEQS), ("m2", p + 3, SEQS), ("slot", p, SEQS)])
                for n in range(S2):
                    last = T.matmul(p_lg[:, n, :], h2T[:, n, :], w["Wr"][1][:, :], start=True, stop=True)
                last.then_inc(s["lg_ps"], 1)

            def queries_keys(tn):
                p = tn.unit(1)
                after(pe, s["hT"], p + 1)
                bank_free(pe, tn, [("h2T", p - 4, SEQS), ("v", p, SEQS), ("yT", 2 * (p - 4), 2 * SEQS)])
                for i in range(2):
                    last = T.matmul(pP[:, i * SEQ_LEN:i * SEQ_LEN + SEQ_LEN], w["Wqkv"][:, i, :], hT[:, :],
                                    start=True, stop=True)
                last.then_inc(s["qk_ps"], 1)

            def ranks(tn):
                p = tn.unit(6)
                after(pe, s["pick"], p + 1)
                after(pe, s["lg_read"], p + 1)
                T.matmul(p_rk, c["before"][:, :], both[:, :, :], start=True, stop=True)
                T.matmul(p_tot, c["ones"][:, :], both[:, :, :], start=True, stop=True).then_inc(s["rk_ps"], 1)

            def mix(tn, g):
                p, u = tn.unit(4), tn.ring(4)
                if g == 0:
                    after(pe, s_m[u], 32 * tn.lap(4) + 32)
                if g < 4:
                    for m, (kt, qt) in enumerate(TILE_PAIR):
                        i = 3 * g + m
                        if i < 4:
                            after(pe, s["max"], clip(12 * (p + 1) + 9 + i, 12 * SEQS))
                            after(pe, s["probs"], 12 * p - 3 + i) if tn.static is not None else None
                        else:
                            after(pe, s["probs"], 12 * p + i - 3)
                        if kt == qt:
                            T.matmul(pS[i % 4][:, :, :], c["identb"][:, :], maskk[:, :, :], start=True, stop=False)
                        for h in range(4):
                            last = T.matmul(pS[i % 4][:, h, :], K[u][:, 4 * g + h, kt * P:kt * P + P],
                                            Q[u][:, 4 * g + h, qt * P:qt * P + P], start=(kt != qt),
                                            stop=(kt != qt or h == 3))
                        last.then_inc(s["probs_ps"], 1)
                if g > 0:
                    g = g - 1
                    if g == 0:
                        after(pe, s["v"], p + 1)
                        after(pe, s["oT"], p)
                    for m, (kt, qt) in enumerate(TILE_PAIR):
                        i = 3 * g + m
                        after(pe, s["probs"], 12 * p + i + 1)
                        for h in range(4):
                            last = T.matmul(pO[32 * h:32 * h + 32, g, qt * P:qt * P + P], vv[u][:, kt, 4 * g + h, :],
                                            pr[i % 6][:, h, :], start=(m != 2), stop=(m != 1))
                    last.then_inc(s["pv"], 1)

            def turn_output(tn, n):
                p = tn.unit(5)
                after(pe, s["oT"], p + 1)
                bank_free(pe, tn, [("yT", 2 * p + 1, 2 * SEQS)] if n else
                          [("rest1", p + 5, SEQS), ("v", p + 4, SEQS), ("yT", 2 * p, 2 * SEQS)])
                for g in range(4):
                    last = T.transpose(pP[:, g * P:g * P + P], oT[:, g, n * P:n * P + P], c["ident"][:, :])
                last.then_inc(s["yT_ps"], 1)

            def turn_max(tn):
                p = tn.unit(3)
                after(pe, s["neg"], p + 1)
                bank_free(pe, tn, [("slot", p - 2, SEQS), ("hT", p + 3, SEQS), ("m2", p, SEQS)])
                for n in range(S2):
                    last = T.transpose(pT[0:H, n * P:n * P + P], nm[:, n, :], c["ident"][:, :])
                last.then_inc(s["mT_ps"], 1)

            def values(tn):
                p = tn.unit(1)
                bank_free(pe, tn, [("yT", 2 * (p - 3), 2 * SEQS), ("rest1", p + 1, SEQS), ("h2T", p - 4, SEQS)])
                for n in range(S2):
                    last = T.matmul(pP[:, n * P:n * P + P], hT[:, n * P:n * P + P], w["Wqkv"][:, 2, :],
                                    start=True, stop=True)
                last.then_inc(s["v_ps"], 1)

            def step(tn):
                for lag, stage, *rest_ in (
                        (1, turn_input), (6, turn_router), (3, maxima, range(0, 4)), (6, logits_),
                        (3, maxima, range(4, 8)), (1, queries_keys), (3, maxima, range(8, 12)), (6, ranks),
                        (4, mix, 0), (4, mix, 1), (5, turn_output, 0), (4, mix, 2), (4, mix, 3),
                        (5, turn_output, 1), (4, mix, 4), (3, turn_max), (1, values)):
                    if tn.has(lag, SEQS):
                        stage(tn, *rest_)

            pe.wait_ge(s["zeroed"], ZEROED)
            turns(pe, 3, step, SEQS + 5, 9, SEQS)

        @block.vector
        def _(dve):
            v = Chain(dve, s_v)
            dve.wait_ge(s["zeroed"], ZEROED)
            v.link(V.memset(c["counts"][:, :], 0.0))

            def second_max(tn):
                p = tn.unit(4)
                dve.wait_ge(s["m1"], p + 1)
                v.announce(V.tensor_tensor(mT[:, 1, :], pT[0:H, 0:SEQ_LEN], mT[:, 0, :], ALU.subtract), s["m2"], p + 1)

            def norm_input(tn):
                p, u = tn.unit(1), tn.ring(1)
                after(dve, s["hT_ps"], p)
                dve.wait_ge(s["rstd0"], p + 1)
                v.announce(normalize(V, lambda n: tile_at(X, 2 * p + n), lambda n: xhat[:, n, :], mv0[u], rstd0[u], S2),
                         s["xhat"], p + 1)

            def router_input(tn):
                p, u = tn.unit(6), tn.ring(6)
                after(dve, s_scat[u], 64 * tn.lap(6))
                dve.wait_ge(s["rstd1"], p + 1)
                v.link(normalize(V, lambda n: tile_at(X, 2 * p + n), lambda n: res[:, n, :], mv1[u], rstd1[u], S2))
                after(dve, s_mod[u], 16 * tn.lap(6) + 16)
                v.link(V.tensor_tensor(res[:, :, :], res[:, :, :],
                                       modbc[u][:, 2, :].unsqueeze(1).broadcast_to([P, S2, D]), ALU.mult))
                for k in range(2):
                    last = V.tensor_tensor(rows[u][:, k, :, 0:D], res[:, :, :],
                                           modbc[u][:, 1, :].unsqueeze(1).broadcast_to([P, S2, D]), ALU.add)
                v.announce(last, s["h2"], p + 1)
                for k in range(2):
                    last = V.tensor_scalar(rows[u][:, k, :, D], c["token_id"][:, cols(2 * p, S2)],
                                           float(k * TOKENS), None, ALU.add)
                v.link(last)

            def maxima(tn, units):
                p = tn.unit(3)
                for i in units:
                    g, m = UNITS[i]
                    dve.wait_ge(s["scores"], 12 * p + i + 1)
                    V.tensor_reduce(mx[:, m, 4 * g:4 * g + 4], pS[i % 4][:, :, :], AX.X, ALU.max)\
                        .then_inc(s["max"], 1)

            def choose(tn):
                p = tn.unit(6)
                dve.wait_ge(s["lg_ps"], p + 1)
                v.announce(V.tensor_copy(logits[:, :, :], p_lg), s["lg_read"], p + 1)
                dve.wait_ge(s["zeroed"], 1)
                dve.nop(nofuse=True)
                v.link(route(V, v, c, logits, r, S2, 1))
                v.announce(V.tensor_tensor(both[:, :, :], r["pick"][:, 0, :, :], r["pick"][:, 1, :, :], ALU.add),
                         s["pick"], p + 1)
                v.link(V.tensor_copy(top2[:, cols(2 * p, S2), :], r["top"][:, :, 0:2]))

            def split(tn):
                p, u = tn.unit(1), tn.ring(1)
                dve.wait_ge(s["part1"], p + 1)
                v.announce(V.tensor_tensor(rest[:, :], pP[:, :], parts[u][:, 0, :], ALU.subtract), s["rest1"], p + 1)

            def third_part(tn):
                p, u = tn.unit(1), tn.ring(1)
                dve.wait_ge(s["part2"], p + 1)
                v.announce(V.tensor_tensor(parts[u][:, 2, :], rest[:, :], parts[u][:, 1, :], ALU.subtract),
                         s["parts"], p + 1)

            def place(tn):
                p, u = tn.unit(6), tn.ring(6)
                dve.wait_ge(s["rk_ps"], p + 1)
                place_rows(V, v, c, r, p_rk, p_tot, S2, 1)
                v.announce(V.tensor_copy(slot_i[u][:, :, :], r["slot"][:, :, :]), s["slot"], p + 1)

            def negate(tn):
                p = tn.unit(3)
                dve.wait_ge(s["max"], 12 * p + 12)
                after(dve, s["mT_ps"], p)
                v.link(V.tensor_tensor(mx[:, 1, :], mx[:, 1, :], mx[:, 2, :], ALU.max))
                v.announce(V.tensor_scalar(nm[:, :, :], mx[:, 0:2, :], -1.0, None, ALU.mult), s["neg"], p + 1)

            def tokens(tn, n):
                p = tn.unit(5)
                dve.wait_ge(s["yT_ps"], 2 * p + n + 1)
                y = pP[:, :].rearrange("p (h l) -> p h l", l=LAT)
                v.link(V.reciprocal(rden[:, :], y[:, :, HD1]))
                v.announce(V.tensor_tensor(yv[:, n, :, :], y[:, :, 0:HD1], bc_last(rden[:, :], HD1), ALU.mult),
                         s["yT"], 2 * p + n + 1)

            def output(tn):
                p, u = tn.unit(5), tn.ring(5)
                after(dve, s_mod[u], 16 * tn.lap(5) + 16)
                v.link(V.tensor_tensor(res[:, :, :], yv[:, :, :, :].rearrange("p n h d -> p n (h d)"),
                                       modbc[u][:, 0, :].unsqueeze(1).broadcast_to([P, S2, D]), ALU.mult))
                x = X[:, cols(2 * p, S2), :]
                v.link(V.tensor_tensor(x, x, res[:, :, :], ALU.add))
                v.announce(moments(V, v, lambda n: tile_at(X, 2 * p + n), stats, mv1[u], S2), s["mv1"], p + 1)

            def load(tn):
                p, u = tn.unit(0), tn.ring(0)
                after(dve, s_a0[u], 32 * tn.lap(0) + 32)
                v.link(V.tensor_tensor(a0[u][:, :, :], a0[u][:, :, :],
                                       bc_last(c["gates"][:, 0, cols(2 * p, S2)], D), ALU.mult))
                v.link(V.tensor_tensor(a0[u][:, :, :], a0[u][:, :, :],
                                       gbc[u][:, :].unsqueeze(1).broadcast_to([P, S2, D]), ALU.mult))
                x = X[:, cols(2 * p, S2), :]
                v.announce(V.tensor_tensor(x, x, a0[u][:, :, :], ALU.add), s["x2"], p + 1)
                dve.wait_ge(s["zeroed"], 1)
                dve.nop(nofuse=True)
                v.announce(moments(V, v, lambda n: tile_at(X, 2 * p + n), stats, mv0[u], S2), s["mv0"], p + 1)

            def values(tn):
                p, u = tn.unit(1), tn.ring(1)
                dve.wait_ge(s["v_ps"], p + 1)
                after(dve, s["pv"], 4 * (p - 2))
                v.announce(V.tensor_copy(vv[u][:, :, :, 0:HD1],
                                       pP[:, 0:SEQ_LEN].rearrange("p (n h d) -> p n h d", n=S2, d=HD1)),
                         s["v"], p + 1)

            def step(tn):
                v.restart()
                for lag, stage, *rest_ in (
                        (4, second_max), (1, norm_input), (6, router_input), (3, maxima, range(0, 6)), (6, choose),
                        (3, maxima, range(6, 9)), (1, split), (3, maxima, range(9, 12)), (1, third_part),
                        (6, place), (3, negate), (5, tokens, 0), (5, tokens, 1), (5, output), (0, load),
                        (1, values)):
                    if tn.has(lag, SEQS):
                        stage(tn, *rest_)
                v.restart()

            turns(dve, 3, step, SEQS + 5, 9, SEQS)
            v.link(V.tensor_copy(gexp[:, :], top2[:, :, 1]))
            v.announce(V.tensor_tensor(gexp[:, :], gexp[:, :], top2[:, :, 0], ALU.subtract), s["gexp"], 1)
            dve.wait_ge(s["gexp"], 2)
            v.link(V.tensor_scalar(c["gates"][:, 0, :], gexp[:, :], 1.0, None, ALU.add))
            v.link(V.reciprocal(c["gates"][:, 0, :], c["gates"][:, 0, :]))
            v.link(V.tensor_tensor(c["gates"][:, 1, :], gexp[:, :], c["gates"][:, 0, :], ALU.mult))


def finish(nc, c, out, sb, sem):
    V = nc.vector
    S2 = SEQ_LEN // P
    a = [sb(f"fin{u}", [P, 2, S2, D]) for u in range(2)]
    gbc = [sb(f"gate1_bc{u}", [P, D]) for u in range(2)]
    s_in = [sem(f"f_in{u}") for u in range(2)]
    s_done, s_v = sem("f_done"), sem("f_dve")
    s_out = sem("f_out")
    X = c["X"]

    with nc.Block() as block:
        @block.sync
        def _(sp):
            def load(p, u):
                after(sp, s_done, p - 1)
                for k in range(2):
                    sp.dma_start(a[u][:, k, :, :], c["answers"][1][cols(2 * P * p + k * TOKENS, 2 * P), :]
                                 .rearrange("(n p) d -> p n d", p=P)).then_inc(s_in[u], 16)
                m = c["mod_dram"][1].rearrange("s (m d) -> s m d", d=D)[cols(p, 1), 5:6, :]
                sp.dma_start(gbc[u][:, :], m.rearrange("s m d -> (s m d)").partition_broadcast(P))\
                    .then_inc(s_in[u], 16)

            pipeline(sp, lambda k, h, static: load(k, h), 0, SEQS - 1, 2, SEQS)

        @block.scalar
        def _(act):
            def store(p, u):
                after(act, s_done, p + 1)
                act.dma_start(out[cols(p, 1), :, :].rearrange("s (n p) d -> p (s n) d", p=P),
                              X[:, cols(2 * p, S2), :]).then_inc(s_out, 16)

            pipeline(act, lambda k, h, static: store(k, h), 0, SEQS - 1, 2, SEQS)
            act.wait_ge(s_out, 16 * SEQS)

        @block.vector
        def _(dve):
            v = Chain(dve, s_v)

            def add(p, u):
                v.restart()
                after(dve, s_in[u], 24 * p + (48 - 24 * u))
                for k in range(2):
                    last = V.tensor_tensor(a[u][:, k, :, :], a[u][:, k, :, :],
                                           bc_last(c["gates"][:, k, cols(2 * p, S2)], D), ALU.mult)
                v.link(last)
                v.link(V.tensor_tensor(a[u][:, 0, :, :], a[u][:, 0, :, :], a[u][:, 1, :, :], ALU.add))
                v.link(V.tensor_tensor(a[u][:, 0, :, :], a[u][:, 0, :, :],
                                       gbc[u][:, :].unsqueeze(1).broadcast_to([P, S2, D]), ALU.mult))
                x = X[:, cols(2 * p, S2), :]
                V.tensor_tensor(x, x, a[u][:, 0, :, :], ALU.add).then_inc(s_done, 1)

            pipeline(dve, lambda k, h, static: add(k, h), 0, SEQS - 1, 2, SEQS)


def load_expert_weights(sp, t, c, layer):
    pre = f"L{layer}_ffn_"
    first = t[pre + ("W1" if layer == 0 else "w1")].rearrange("p e f -> p (e f)")
    second = t[pre + ("W2" if layer == 0 else "w2")].rearrange("p e b d -> p (e b d)")
    w = E * FF // WEIGHT_PARTS
    for dst, src in ((c["W1"], first), (c["W2"], second)):
        for q in range(WEIGHT_PARTS):
            sp.dma_start(dst[:, q * w:q * w + w], src[:, q * w:q * w + w]).then_inc(c["s_w"][layer], 16)
    sp.dma_start(c["b1"][:, :], t[pre + "b1"]).then_inc(c["s_w"][layer], 16)
    sp.dma_start(c["b2"][:, :], t[pre + "b2"].partition_broadcast(P)).then_inc(c["s_w"][layer], 16)


def experts(nc, c, sb, ps, sem, layer):
    V, A, T = nc.vector, nc.scalar, nc.tensor
    n_tiles = expert_tiles(layer)
    dump = (layer + 1) * TOKENS
    W1, W2, b1, b2, s_w = c["W1"], c["W2"], c["b1"], c["b2"], c["s_w"][layer]
    RINGS = 4
    w1 = [sb(f"w1_{u}", [P, FF]) for u in range(2)]
    xg = [sb(f"xg{u}", [P, ROW]) for u in range(RINGS)]
    xgT = [sb(f"xgT{u}", [P, P]) for u in range(2)]
    hid = [sb(f"hid{u}", [P, FB, P]) for u in range(2)]
    y = [sb(f"y{u}", [P, D]) for u in range(RINGS)]
    dest = [sb(f"dest{u}", [P, 1], I32) for u in range(RINGS)]
    padding = [sb(f"padding{u}", [P, 1]) for u in range(2)]
    nti, ntf = sb("nt_i", [P, E], I32), sb("nt_f", [P, E])
    ends = sb("ends", [P, E])
    onesE = sb("ones_e", [P, E])
    jt = sb("tile_no", [P, n_tiles])
    ge = sb("past", [P, n_tiles, E - 1])
    tmp = sb("plan_tmp", [P, n_tiles, E])
    ej, sj, nj, rj = (sb(f"plan_{n}", [P, n_tiles]) for n in ("expert", "start", "rows", "row"))
    expert_i, row_i = sb("plan_expert_i", [P, n_tiles], I32), sb("plan_row_i", [P, n_tiles], I32)
    pad_f, pad_i = sb("pad_f", [P, E]), sb("pad_i", [P, E], I32)
    pT = [ps(f"gT{u}", [P, 512])[:, 0:P] for u in range(2)]
    pH = [ps(f"gH{u}", [P, FB, P]) for u in range(2)]
    pY = [ps(f"gY{u}", [P, 512])[:, 0:D] for u in range(2)]

    n = "experts_"
    s_iota, s_pads, s_plan, s_pad = sem(n + "iota"), sem(n + "pads"), sem(n + "plan"), sem(n + "pad")
    s_xg = [sem(n + f"xg{u}") for u in range(RINGS)]
    s_xT, s_xgT, s_w1, s_h = sem(n + "xT"), sem(n + "xgT"), sem(n + "w1"), sem(n + "h")
    s_hid, s_yps, s_y, s_dest = sem(n + "hid"), sem(n + "yps"), sem(n + "y"), sem(n + "dest")
    s_out = [sem(f"experts{layer}_out{u}", kept=True) for u in range(RINGS)]
    s_v, s_padding = sem(n + "dve"), sem(n + "padding")

    def plan_value(engine, src, j, most):
        return engine.value_load(src[0:1, cols(j, 1)], min_val=0, max_val=most)

    def pad(engine, e):
        at = plan_value(engine, pad_i, e, E * REGION - P)
        engine.dma_start(c["routed"][layer][bass.ds(at, P), :], c["pad_rows"][:, :]).then_inc(s_pad, 16)

    with nc.Block() as block:
        @block.sync
        def _(sp):
            sp.wait_ge(s_pads, 1)
            for e in range(0, E, 2):
                pad(sp, e)
            sp.wait_ge(s_plan, 1)
            sp.wait_ge(s_pad, 16 * E)

            def load(tn):
                j, u = tn.unit(0), tn.ring(0)
                after(sp, s_xT, j - 3)
                after(sp, s_dest, j - 3)
                at = plan_value(sp, row_i, j, E * REGION - P)
                sp.dma_start(xg[u][:, :], c["routed"][layer][bass.ds(at, P), :]).then_inc(s_xg[u], 16)

            turns(sp, RINGS, load, n_tiles - 1, RINGS, n_tiles)

        @block.gpsimd
        def _(pool):
            nc.gpsimd.iota(c["pad_rows"][:, D:D + 1], pattern=[[0, 1]], base=dump, channel_multiplier=1,
                           allow_small_or_imprecise_dtypes=True).then_inc(s_iota, 1)
            nc.gpsimd.iota(jt[:, :], pattern=[[1, n_tiles]], base=0, channel_multiplier=0,
                           allow_small_or_imprecise_dtypes=True).then_inc(s_iota, 1)

            def scatter(tn):
                j, u = tn.unit(0), tn.ring(0)
                after_then(pool, s_y, j + 1, s_plan)
                pool.indirect_dma_start(c["answers"][layer], bass.IndirectOffsetOnAxis(ap=dest[u][:, :], axis=0),
                                        y[u][:, :], None).then_inc(s_out[u], 16)

            turns(pool, RINGS, scatter, n_tiles - 1, RINGS, n_tiles)
            for u in range(RINGS):
                pool.wait_ge(s_out[u], 16 * len(range(u, n_tiles, RINGS)))

        @block.scalar
        def _(act):
            act.wait_ge(s_pads, 1)
            for e in range(1, E, 2):
                pad(act, e)
            act.wait_ge(s_plan, 1)
            act.wait_ge(s_w, WEIGHT_LOADS)

            def hidden(tn):
                j, u = tn.unit(0), tn.ring(0) % 2
                block0 = plan_value(act, expert_i, j, E - 1) * FB
                after(act, s_h, j + 1)
                after(act, s_yps, j - 1)
                for b in range(FB):
                    last = A.activation(hid[u][:, b, :], pH[u][:, b, :], ACT.Relu if layer == 0 else ACT.Gelu,
                                        bias=b1[:, bass.ds(block0 + b, 1)])
                last.then_inc(s_hid, 1)

            turns(act, RINGS, hidden, n_tiles - 1, RINGS, n_tiles)

        @block.tensor
        def _(pe):
            pe.wait_ge(s_plan, 1)
            pe.wait_ge(s_w, WEIGHT_LOADS)

            def turn(tn):
                j, u = tn.unit(0), tn.ring(0)
                after(pe, s_xg[u], 16 * tn.lap(0) + 16)
                after(pe, s_xgT, j - 1)
                T.transpose(pT[u % 2][:, :], xg[u][:, 0:D], c["ident"][:, :]).then_inc(s_xT, 1)

            def up(tn):
                j, u = tn.unit(1), tn.ring(1) % 2
                after(pe, s_xgT, j + 1)
                after(pe, s_w1, j + 1)
                after(pe, s_hid, j - 1)
                for b in range(FB):
                    last = T.matmul(pH[u][:, b, :], w1[u][:, b * P:b * P + P], xgT[u][:, :], start=True, stop=True)
                last.then_inc(s_h, 1)

            def down(tn):
                j, u = tn.unit(2), tn.ring(2) % 2
                at = plan_value(pe, expert_i, j, E - 1) * FF
                after(pe, s_hid, j + 1)
                after(pe, s_y, j - 1)
                for b in range(FB):
                    last = T.matmul(pY[u][:, :], hid[u][:, b, :], W2[:, bass.ds(at + b * D, D)],
                                    start=(b == 0), stop=(b == FB - 1))
                last.then_inc(s_yps, 1)

            def step(tn):
                for lag, stage in ((0, turn), (1, up), (2, down)):
                    if tn.has(lag, n_tiles):
                        stage(tn)

            turns(pe, RINGS, step, n_tiles + 1, RINGS, n_tiles)

        @block.vector
        def _(dve):
            v = Chain(dve, s_v)
            counts = c["counts"]
            v.link(V.tensor_tensor(pad_f[:, :], counts[:, :], c["region0"][:, :], ALU.add))
            dve.wait_ge(s_iota, 1)
            V.tensor_copy(pad_i[:, :], pad_f[:, :]).then_inc(s_pads, 1)
            v.link(V.memset(onesE[:, :], 1.0))
            v.link(V.tensor_scalar(nti[:, :], counts[:, :], float(P - 1), None, ALU.add))
            v.link(V.tensor_scalar(nti[:, :], nti[:, :], 7, None, ALU.arith_shift_right))
            v.link(V.tensor_copy(ntf[:, :], nti[:, :]))
            v.link(V.tensor_tensor_scan(ends[:, :], onesE[:, :], ntf[:, :], 0.0, ALU.mult, ALU.add))
            dve.wait_ge(s_iota, 2)
            v.link(V.tensor_tensor(ge[:, :, :], bc_last(jt[:, :], E - 1),
                                   ends[:, 0:E - 1].unsqueeze(1).broadcast_to([P, n_tiles, E - 1]), ALU.is_ge))
            v.link(V.tensor_reduce(ej[:, :], ge[:, :, :], AX.X, ALU.add))
            V.tensor_copy(expert_i[:, :], ej[:, :])
            v.link(V.tensor_tensor(ge[:, :, :], ge[:, :, :],
                                   ntf[:, 0:E - 1].unsqueeze(1).broadcast_to([P, n_tiles, E - 1]), ALU.mult))
            V.tensor_reduce(sj[:, :], ge[:, :, :], AX.X, ALU.add)
            v.link(V.tensor_tensor(tmp[:, :, :], c["iota8"][:, :].unsqueeze(1).broadcast_to([P, n_tiles, E]),
                                   bc_last(ej[:, :], E), ALU.is_equal))
            v.link(V.tensor_tensor(tmp[:, :, :], tmp[:, :, :],
                                   counts[:, :].unsqueeze(1).broadcast_to([P, n_tiles, E]), ALU.mult))
            V.tensor_reduce(nj[:, :], tmp[:, :, :], AX.X, ALU.add)
            v.link(V.tensor_tensor(rj[:, :], jt[:, :], sj[:, :], ALU.subtract))
            v.link(V.scalar_tensor_tensor(rj[:, :], rj[:, :], float(P), nj[:, :], ALU.mult, ALU.min))
            v.link(V.scalar_tensor_tensor(rj[:, :], ej[:, :], float(REGION), rj[:, :], ALU.mult, ALU.add))
            V.tensor_copy(row_i[:, :], rj[:, :]).then_inc(s_plan, 1)
            dve.wait_ge(s_plan, 1)
            dve.wait_ge(s_w, WEIGHT_LOADS)

            def prepare(tn):
                j, u = tn.unit(0), tn.ring(0)
                at = plan_value(dve, expert_i, j, E - 1) * FF
                after(dve, s_h, j - 1)
                V.tensor_copy(w1[u % 2][:, :], W1[:, bass.ds(at, FF)]).then_inc(s_w1, 1)
                dve.wait_ge(s_xT, j + 1)
                V.tensor_copy(xgT[u % 2][:, :], pT[u % 2][:, :]).then_inc(s_xgT, 1)
                V.tensor_scalar(padding[u % 2][:, :], xg[u][:, D:D + 1], float(dump), jt[:, cols(j, 1)], ALU.is_ge,
                                ALU.mult).then_inc(s_padding, 1)
                dve.wait_ge(s_padding, j + 1)
                after(dve, s_out[u], 16 * tn.lap(0))
                V.scalar_tensor_tensor(dest[u][:, :], padding[u % 2][:, :], float(P), xg[u][:, D:D + 1], ALU.mult,
                                       ALU.add).then_inc(s_dest, 1)

            def result(tn):
                j, u = tn.unit(2), tn.ring(2)
                at = plan_value(dve, expert_i, j, E - 1) * D
                dve.wait_ge(s_yps, j + 1)
                V.tensor_tensor(y[u][:, :], pY[u % 2][:, :], b2[:, bass.ds(at, D)], ALU.add).then_inc(s_y, 1)

            def step(tn):
                for lag, stage in ((0, prepare), (2, result)):
                    if tn.has(lag, n_tiles):
                        stage(tn)

            turns(dve, RINGS, step, n_tiles + 1, RINGS, n_tiles)


def kernel(**inputs):
    import numpy as np
    import concourse.bacc as bacc
    from concourse.bass_utils import run_bass_kernel_spmd

    nc = bacc.Bacc("TRN2", target_bir_lowering=False, num_devices=1)
    arrays, t = {}, {}
    b_in = np.asarray(inputs.pop("L0_attn_b_in"))
    inputs["b_in_ch"], inputs["b_in_dt"] = b_in[:6 * P], b_in[6 * P:]
    for name, a in inputs.items():
        a = np.asarray(a)
        if name in ("L0_c", "L1_c", "L0_attn_W_in", "L0_attn_W_out", "L1_attn_W_uq", "L1_attn_W_o", "L1_ffn_router_w"):
            a = a.T
        elif name in ("L0_ffn_W1",):
            a = a.transpose(1, 0, 2)
        elif name == "L1_ffn_w1":
            a = a.transpose(2, 0, 1)
        elif name == "L0_ffn_W2":
            a = a.reshape(E, FB, P, D).transpose(2, 0, 1, 3)
        elif name == "L1_ffn_w2":
            a = a.transpose(0, 2, 1).reshape(E, FB, P, D).transpose(2, 0, 1, 3)
        elif name in ("L0_ffn_b1", "L1_ffn_b1"):
            a = a.reshape(E * FB, P).T
        elif name in ("L0_ffn_b2", "L1_ffn_b2"):
            a = a.reshape(1, E * D)
        elif name == "L0_attn_conv_w":
            a = a.reshape(4, P, 4).transpose(1, 0, 2)
        elif name in ("L0_attn_conv_b", "L0_attn_norm_w", "b_in_ch"):
            a = a.reshape(-1, P).T
        elif a.ndim == 1:
            a = a[None, :]
        a = np.ascontiguousarray(a)
        arrays[f"in_{name}"] = a
        t[name] = nc.dram_tensor(f"in_{name}", a.shape, mybir.dt.from_np(a.dtype), kind="ExternalInput").ap()
    out = nc.dram_tensor("out_0", (SEQS, SEQ_LEN, D), F32, kind="ExternalOutput").ap()
    build(nc, t, out)
    return run_bass_kernel_spmd(nc, [arrays], core_ids=[0]).results[0]["out_0"]
```

```python
from contextlib import ExitStack

import concourse.bass as bass
from concourse import mybir

F32 = mybir.dt.float32
BF16 = mybir.dt.bfloat16
I32 = mybir.dt.int32
U32 = mybir.dt.uint32
ALU = mybir.AluOpType
ACT = mybir.ActivationFunctionType
AX = mybir.AxisListType

P = 128
SEQS = 16
SEQ_LEN = 256
D = 128
TILES = SEQS * SEQ_LEN // P
TOKENS = TILES * P
PAIRS = SEQS // 2
PT = TILES // PAIRS
PW = PT * P
E = 8
FF = 512
FB = FF // P
DSSM = 256
HEADS0 = 4
HD0 = 64
HEADS1 = 16
HD1 = 8
LAT = 32
EPS_LN = 1e-5
EPS_RMS = 1e-12
ROW = 132
REGION = TOKENS + P
XPAD = SEQ_LEN + 3
SHIFT, SCALE, GATE = 0, 1, 2
MASKED = -1.0e30
WEIGHT_PARTS = 4
WEIGHT_LOADS = 16 * (2 * WEIGHT_PARTS + 2)


def after(engine, sem, value):
    if isinstance(value, int) and value <= 0:
        return
    engine.wait_ge(sem, value)


def after_then(engine, sem, value, passed):
    after(engine, sem, value)
    engine.wait_ge(passed, 1)
    engine.nop(nofuse=True)


class Chain:

    def __init__(self, engine, sem):
        self.engine, self.sem, self.n = engine, sem, 0

    def restart(self):
        if self.n:
            self.engine.wait_ge(self.sem, self.n)
            self.engine.nop(nofuse=True)
            self.engine.sem_clear(self.sem)
            self.n = 0

    def link(self, instruction):
        self.n += 1
        instruction.then_inc(self.sem, 1)
        self.engine.wait_ge(self.sem, self.n)

    def note(self, instruction):
        self.n += 1
        instruction.then_inc(self.sem, 1)

    def settle(self):
        self.engine.wait_ge(self.sem, self.n)

    def announce(self, instruction, sem, value):
        instruction.then_inc(sem, 1)
        self.engine.wait_ge(sem, value)


def bc_last(ap, n):
    return ap.unsqueeze(2).broadcast_to([ap.shape[0], ap.shape[1], n])


def pipeline(engine, step, first, last, full_from, full_to):
    for k in range(first, full_from):
        step(k, k % 2, k)
    n = (full_to - full_from) // 2
    if n > 0:
        with engine.Fori(0, n) as i:
            for h in range(2):
                step(2 * i + (full_from + h), (full_from + h) % 2, None)
    for k in range(full_from + 2 * n, last + 1):
        step(k, k % 2, k)


def expert_tiles(layer):
    return ((layer + 1) * TOKENS + E * (P - 1)) // P


def build(nc, t, out, stop=5):
    top = ExitStack()
    with top:
        def sb_in(ctx, phase=""):
            return lambda name, shape, dt=F32: ctx.enter_context(nc.sbuf_tensor(phase + name, shape, dt))

        def ps_in(ctx, phase=""):
            return lambda name, shape, dt=F32: ctx.enter_context(nc.psum_tensor(phase + name, shape, dt))

        def sem(name):
            return top.enter_context(nc.semaphore(name))

        def phase_semaphores(ctx, of_phase):
            def phase_sem(name, kept=False):
                if kept:
                    return sem(name)
                of_phase.append(ctx.enter_context(nc.semaphore(name)))
                return of_phase[-1]
            return phase_sem

        def clear(of_phase):
            with nc.Block() as block:
                @block.sync
                def _(sp):
                    for used in of_phase:
                        sp.sem_clear(used)

        sb = sb_in(top)
        c = {}
        c["X"] = sb("X", [P, TILES, D])
        c["ident"] = sb("ident", [P, P])
        c["identb"] = sb("identb", [P, P], BF16)
        c["upto"] = sb("upto", [P, P])
        c["beyond"] = sb("beyond", [P, P])
        c["before"] = sb("before", [P, P])
        c["ones"] = sb("ones", [P, P])
        c["minus_half"] = sb("minus_half", [P, PT])
        c["iota8"] = sb("iota8", [P, E])
        c["region0"] = sb("region0", [P, E])
        c["token_id"] = sb("token_id", [P, TILES])
        c["gates"] = sb("gates", [P, 2, TILES])
        c["counts"] = sb("counts", [P, E])
        c["modT"] = [sb(f"modT{l}", [P, 3, SEQS]) for l in range(2)]
        c["pad_rows"] = sb("pad_rows", [P, ROW])
        c["W1"] = sb("W1", [P, E * FF])
        c["W2"] = sb("W2", [P, E * FB * D])
        c["b1"] = sb("b1", [P, E * FB])
        c["b2"] = sb("b2", [P, E * D])
        c["s_w"] = [sem(f"expert_weights{l}") for l in range(2)]
        c["mod_dram"] = [nc.dram_tensor(f"mod_rows{l}", (SEQS, 6 * D), F32).ap() for l in range(2)]
        c["routed"] = [nc.dram_tensor(f"routed{l}", (E * REGION, ROW), F32).ap() for l in range(2)]
        c["answers"] = [nc.dram_tensor(f"answers{l}", ((l + 1) * TOKENS + expert_tiles(l) * P, D), F32).ap()
                        for l in range(2)]
        c["parts_dram"] = nc.dram_tensor("qk_parts_dram", (3, P, 3, 2 * SEQ_LEN), BF16).ap()
        w = {}
        setup(nc, t, c, w, sb, sem)
        phases = (lambda sb, ps, sem: mamba(nc, t, c, w, sb, ps, sem),
                  lambda sb, ps, sem: experts(nc, c, sb, ps, sem, 0),
                  lambda sb, ps, sem: attention(nc, t, c, w, sb, ps, sem),
                  lambda sb, ps, sem: experts(nc, c, sb, ps, sem, 1),
                  lambda sb, ps, sem: finish(nc, c, out, sb, sem))
        for i, phase in enumerate(phases[:stop]):
            with ExitStack() as ctx:
                of_phase = []
                phase(sb_in(ctx, f"{i}_"), ps_in(ctx, f"{i}_"), phase_semaphores(ctx, of_phase))
                if i < len(phases) - 1:
                    clear(of_phase)
        if stop < 4:
            s_dbg = sem("s_dbg")
            with nc.Block() as block:
                @block.sync
                def _(sp):
                    sp.dma_start(out.rearrange("s (j p) d -> p (s j) d", p=P), c["X"][:, :, :]).then_inc(s_dbg, 16)
                    sp.wait_ge(s_dbg, 16)


def setup(nc, t, c, w, sb, sem):
    s_x = sem("s_x")
    s_small = sem("s_small")
    s_mod = sem("s_mod")
    s_modw = sem("s_modw")
    s_memset = sem("s_memset")
    s_masks = sem("s_masks")
    s_tanh = sem("s_tanh")
    s_silu = sem("s_silu")
    s_modps = sem("s_modps")
    s_v = sem("s_setup_chain")
    s_wps = sem("s_wps")
    s_wcp = sem("s_wcp")
    w["WinT"] = sb("WinT", [P, 772])
    w["WoT"] = sb("WoT", [P, 2, D])
    w["bin_ch"] = sb("bin_ch", [P, 6])
    w["conv_w"] = sb("conv_w", [P, 4, 4])
    w["conv_b"] = sb("conv_b", [P, 4])
    w["taps"] = sb("taps", [P, 4, 4 * P])
    w["conv_bias"] = sb("conv_bias", [P, 4])
    w["edge"] = sb("edge", [P, 4, 2, 3])
    w["D_ch"] = sb("D_ch", [P, 2])
    w["norm_ch"] = sb("norm_ch", [P, 2])
    w["heads_bc"] = sb("heads_bc", [P, 3, HEADS0])
    w["dt_bias"] = sb("dt_bias", [P, HEADS0])
    w["A"] = sb("A", [P, HEADS0])
    w["bout_bc"] = sb("bout_bc", [P, D])
    w["ln_bc"] = sb("ln_bc", [P, 2, D])
    w["br_bc"] = sb("br_bc", [P, E])
    w["Wr"] = [sb(f"Wr{l}", [P, E]) for l in range(2)]
    w["Wqkv"] = sb("Wqkv", [P, 3, D])
    with ExitStack() as ctx:
        sbx, psx = (lambda n, s, dt=F32: ctx.enter_context(nc.sbuf_tensor(n, s, dt))), \
                   (lambda n, s, dt=F32: ctx.enter_context(nc.psum_tensor(n, s, dt)))
        cT = sbx("cT", [P, 2, SEQS])
        th = sbx("th", [P, 2, SEQS])
        wmod = sbx("wmod", [P, 2, 6 * D])
        rows = sbx("mod_rows", [SEQS, 2, 6 * D])
        tmp = sbx("mod_tmp", [SEQS, 2, 2, D])
        sg = sbx("mod_sign", [SEQS, 2, 2, D])
        conv_rows = sbx("conv_rows", [P, 4, 4 * P])
        tap_sum = sbx("tap_sum", [P, 4, 4])
        wdq = sbx("wdq", [LAT, D])
        wuqT = sbx("wuqT", [LAT, D])
        wdkv = sbx("wdkv", [LAT, D])
        wuk = sbx("wuk", [P, LAT])
        wuv = sbx("wuv", [P, LAT])
        woT = sbx("woT", [P, D])
        wqT = sbx("wqT", [P, D])
        keT = sbx("keT", [LAT, D])
        ve = sbx("ve", [LAT, D])
        mps = psx("mod_ps", [P, 2, 6, SEQS])
        rps = psx("row_ps", [P, 2, 2, 512])
        wps = psx("w_ps", [P, 3, D])
        wps2 = psx("w_ps2", [P, 3, D])
        block = ctx.enter_context(nc.Block())
        small = [
            (cT[:, 0, :], t["L0_c"]), (cT[:, 1, :], t["L1_c"]),
            (wmod[:, 0, :], t["L0_wmod"]), (wmod[:, 1, :], t["L1_wmod"]),
            (wdq[:, :], t["L1_attn_W_dq"]), (wuqT[:, :], t["L1_attn_W_uq"]), (wdkv[:, :], t["L1_attn_W_dkv"]),
            (wuk[:, :], t["L1_attn_W_uk"]), (wuv[:, :], t["L1_attn_W_uv"]), (woT[:, :], t["L1_attn_W_o"]),
            (w["WinT"][:, :], t["L0_attn_W_in"]),
            (w["WoT"][:, :, :], t["L0_attn_W_out"].rearrange("(b p) d -> p b d", p=P)),
            (w["bin_ch"][:, :], t["b_in_ch"]),
            (w["conv_w"][:, :, :], t["L0_attn_conv_w"]),
            (w["conv_b"][:, :], t["L0_attn_conv_b"]),
            (conv_rows[:, :, :], t["conv_rows"].partition_broadcast(P)),
            (w["norm_ch"][:, :], t["L0_attn_norm_w"]),
            (w["heads_bc"][:, 0, :], t["b_in_dt"].partition_broadcast(P)),
            (w["heads_bc"][:, 1, :], t["L0_attn_dt_bias"].partition_broadcast(P)),
            (w["heads_bc"][:, 2, :], t["L0_attn_A_log"].partition_broadcast(P)),
            (w["bout_bc"][:, :], t["L0_attn_b_out"].partition_broadcast(P)),
            (w["ln_bc"][:, 0, :], t["L0_ffn_ln_g"].partition_broadcast(P)),
            (w["ln_bc"][:, 1, :], t["L0_ffn_ln_b"].partition_broadcast(P)),
            (w["br_bc"][:, :], t["L0_ffn_br"].partition_broadcast(P)),
            (w["Wr"][0][:, :], t["L0_ffn_Wr"]), (w["Wr"][1][:, :], t["L1_ffn_router_w"]),
        ]
        for h in range(HEADS0):
            small.append((w["D_ch"][HD0 * (h % 2):HD0 * (h % 2) + HD0, h // 2:h // 2 + 1],
                          t["L0_attn_D"][:, h:h + 1].partition_broadcast(HD0)))

        @block.sync
        def _(sp):
            for dst, src in small:
                sp.dma_start(dst, src).then_inc(s_small, 16)
            sp.wait_ge(s_mod, 1)
            for l in range(2):
                sp.dma_start(c["mod_dram"][l], rows[:, l, :]).then_inc(s_modw, 16)
            sp.wait_ge(s_modw, 32)

        @block.scalar
        def _(act):
            xv = t["L0_attn_u"].rearrange("s (j p) d -> p (s j) d", p=P)
            for q in range(4):
                act.dma_start(c["X"][:, 8 * q:8 * q + 8, :], xv[:, 8 * q:8 * q + 8, :]).then_inc(s_x, 16)
            act.wait_ge(s_small, 16 * len(small))
            nc.scalar.activation(th[:, :, :], cT[:, :, :], ACT.Tanh, scale=0.5).then_inc(s_tanh, 1)
            nc.scalar.activation(w["A"][:, :], w["heads_bc"][:, 2, :], ACT.Exp).then_inc(s_tanh, 1)
            act.wait_ge(s_x, 64)

        @block.gpsimd
        def _(pool):
            g = nc.gpsimd
            g.memset(c["ones"][:, :], 1.0).then_inc(s_memset, 1)
            for m in ("ident", "upto", "beyond", "before"):
                g.memset(c[m][:, :], 0.0 if m == "ident" else 1.0).then_inc(s_memset, 1)
            g.memset(c["identb"][:, :], 0.0).then_inc(s_memset, 1)
            g.memset(c["pad_rows"][:, :], 0.0).then_inc(s_memset, 1)
            g.memset(c["minus_half"][:, :], -0.5).then_inc(s_masks, 1)
            pool.wait_ge(s_memset, 7)
            for m, op, fill, sign in (("ident", ALU.not_equal, 1.0, 1), ("identb", ALU.not_equal, 1.0, 1),
                                      ("upto", ALU.is_ge, 0.0, -1), ("beyond", ALU.is_gt, 0.0, 1),
                                      ("before", ALU.is_gt, 0.0, -1)):
                g.affine_select(out=c[m][:, :], in_=c[m][:, :], compare_op=op, fill=fill, base=0,
                                pattern=[[-sign, P]], channel_multiplier=sign).then_inc(s_masks, 1)
            g.iota(c["iota8"][:, :], pattern=[[1, E]], base=0, channel_multiplier=0,
                   allow_small_or_imprecise_dtypes=True).then_inc(s_masks, 1)
            g.iota(c["region0"][:, :], pattern=[[REGION, E]], base=0, channel_multiplier=0,
                   allow_small_or_imprecise_dtypes=True).then_inc(s_masks, 1)
            g.iota(c["token_id"][:, :], pattern=[[P, TILES]], base=0, channel_multiplier=1,
                   allow_small_or_imprecise_dtypes=True).then_inc(s_masks, 1)

        @block.tensor
        def _(pe):
            pe.wait_ge(s_silu, 1)
            for l in range(2):
                for m in range(3):
                    nc.tensor.matmul(mps[:, l, m, :], wmod[:, l, m * D:(m + 1) * D], cT[:, l, :], start=True, stop=True)
                for h, (a, b) in enumerate(((0, 512), (512, 768))):
                    last = nc.tensor.matmul(rps[0:SEQS, l, h, 0:b - a], cT[:, l, :], wmod[:, l, a:b],
                                            start=True, stop=True)
            last.then_inc(s_modps, 1)
            nc.tensor.matmul(wps[:, 0, :], wdq[:, :], wuqT[:, :], start=True, stop=True)
            nc.tensor.matmul(wps[:, 1, :], wuqT[:, :], wdq[:, :], start=True, stop=True)
            nc.tensor.matmul(wps[0:LAT, 2, :], wuv[:, :], woT[:, :], start=True, stop=True).then_inc(s_wps, 1)
            pe.wait_ge(s_wcp, 3)
            nc.tensor.matmul(wps2[0:LAT, 0, :], wuk[:, :], wqT[:, :], start=True, stop=True).then_inc(s_wps, 1)
            pe.wait_ge(s_wcp, 4)
            nc.tensor.matmul(wps2[:, 1, :], wdkv[:, :], keT[:, :], start=True, stop=True)
            nc.tensor.matmul(wps2[:, 2, :], wdkv[:, :], ve[:, :], start=True, stop=True).then_inc(s_wps, 1)

        @block.vector
        def _(dve):
            v = Chain(dve, s_v)
            V = nc.vector
            dve.wait_ge(s_tanh, 2)
            v.link(V.tensor_scalar(cT[:, :, :], cT[:, :, :], 0.5, None, ALU.mult))
            V.scalar_tensor_tensor(cT[:, :, :], th[:, :, :], 1.0, cT[:, :, :], ALU.add, ALU.mult).then_inc(s_silu, 1)
            v.link(V.tensor_tensor(w["dt_bias"][:, :], w["heads_bc"][:, 0, :], w["heads_bc"][:, 1, :], ALU.add))
            v.link(V.tensor_scalar(w["A"][:, :], w["A"][:, :], -1.0, None, ALU.mult))
            v.link(V.tensor_copy(tap_sum[:, :, 0], w["conv_w"][:, :, 0]))
            for k in range(1, 4):
                v.link(V.tensor_tensor(tap_sum[:, :, k], tap_sum[:, :, k - 1], w["conv_w"][:, :, k], ALU.add))
            v.link(V.tensor_tensor(tap_sum[:, :, :], tap_sum[:, :, :], bc_last(w["bin_ch"][:, 2:6], 4), ALU.mult))
            v.link(V.tensor_tensor(w["conv_bias"][:, :], tap_sum[:, :, 3], w["conv_b"][:, :], ALU.add))
            for j in range(3):
                v.link(V.tensor_scalar(w["edge"][:, :, :, j], bc_last(tap_sum[:, :, 2 - j], 2), -1.0, None, ALU.mult))
            for k in range(4):
                v.link(V.tensor_tensor(w["taps"][:, k, :], w["WinT"][:, 2 * P:6 * P], conv_rows[:, k, :], ALU.mult))
            for b in range(2):
                v.link(V.tensor_scalar(w["WoT"][:, b, :], w["WoT"][:, b, :], w["norm_ch"][:, b:b + 1], None, ALU.mult))
            dve.wait_ge(s_wps, 1)
            V.tensor_copy(w["Wqkv"][:, 0, :], wps[:, 0, :]).then_inc(s_wcp, 1)
            V.tensor_copy(wqT[:, :], wps[:, 1, :]).then_inc(s_wcp, 1)
            V.tensor_copy(ve[:, :], wps[0:LAT, 2, :]).then_inc(s_wcp, 1)
            dve.wait_ge(s_wps, 2)
            V.tensor_copy(keT[:, :], wps2[0:LAT, 0, :]).then_inc(s_wcp, 1)
            dve.wait_ge(s_wps, 3)
            v.link(V.tensor_copy(w["Wqkv"][:, 1:3, :], wps2[:, 1:3, :]))
            dve.wait_ge(s_modps, 1)
            for l in range(2):
                v.link(V.tensor_copy(c["modT"][l][:, :, :], mps[:, l, 0:3, :]))
                v.link(V.tensor_scalar(c["modT"][l][:, SCALE, :], c["modT"][l][:, SCALE, :], 1.0, None, ALU.add))
                v.link(V.tensor_copy(rows[:, l, 0:512], rps[0:SEQS, l, 0, :]))
                v.link(V.tensor_copy(rows[:, l, 512:768], rps[0:SEQS, l, 1, 0:256]))
            r6 = rows[:, :, :].rearrange("s l (m d) -> s l m d", d=D)
            for g in range(2):
                m = 3 * g + GATE
                v.link(V.scalar_tensor_tensor(tmp[:, :, g, :], r6[:, :, m, :], -1.0, r6[:, :, m, :],
                                              ALU.mult, ALU.max))
                v.link(V.tensor_scalar(tmp[:, :, g, :], tmp[:, :, g, :], 0.25, None, ALU.max))
                v.link(V.tensor_scalar(sg[:, :, g, :], r6[:, :, m, :], 0.0, 2.0, ALU.is_ge, ALU.mult))
                v.link(V.tensor_scalar(sg[:, :, g, :], sg[:, :, g, :], -1.0, None, ALU.add))
                v.link(V.tensor_tensor(r6[:, :, m, :], tmp[:, :, g, :], sg[:, :, g, :], ALU.mult))
            v.link(V.tensor_scalar(r6[:, :, 3 + SCALE, :], r6[:, :, 3 + SCALE, :], 1.0, None, ALU.add))
            V.tensor_scalar(r6[:, :, SCALE, :], r6[:, :, SCALE, :], 1.0, None, ALU.add).then_inc(s_mod, 1)


def moments(V, v, x, stats, mv, tiles):
    for n in range(tiles):
        last = V.bn_stats(stats[:, n, :], x(n))
    v.link(last)
    for n in range(tiles):
        last = V.bn_aggr(mv[:, n, :], stats[:, n, :])
    return last


def normalize(V, x, xhat, mv, rstd, tiles):
    for n in range(tiles):
        last = V.tensor_scalar(xhat(n), x(n), mv[:, n, 0:1], rstd[:, n:n + 1], ALU.subtract, ALU.mult)
    return last


def inverse_root(G, ch, c, out, tmp, x, eps):
    ch.link(G.tensor_scalar(tmp, x, eps, None, ALU.add))
    return G.tensor_tensor(out, tmp, c["minus_half"][:, 0:tmp.shape[-1]], ALU.pow)


def tile_at(x, n):
    return x[:, n, :] if isinstance(n, int) else x[:, bass.ds(n, 1), :].rearrange("p o d -> p (o d)")


def cols(n, size):
    return slice(n, n + size) if isinstance(n, int) else bass.ds(n, size)


def route(V, v, c, logits, r, tiles, layer):
    top, idx, idxf, pick = r["top"], r["idx"], r["idxf"], r["pick"]
    for n in range(tiles):
        last = V.max(top[:, n, :], logits[:, n, :])
    v.link(last)
    for n in range(tiles):
        last = V.max_index(idx[:, n, :], top[:, n, :], logits[:, n, :])
    v.link(last)
    v.link(V.tensor_copy(idxf[:, :, :], idx[:, :, 0:2]))
    for k in range(layer + 1):
        last = V.tensor_tensor(pick[:, k, :, :], c["iota8"][:, :].unsqueeze(1).broadcast_to([P, tiles, E]),
                               bc_last(idxf[:, :, k], E), ALU.is_equal)
    return last


def place_rows(G, ch, c, r, rank, total, slot_i, tiles, signal, value):
    pick, acc, base = r["pick"], r["acc"], r["base"]
    for n in range(tiles):
        ch.link(G.tensor_tensor(base[:, n, :], c["counts"][:, :], c["region0"][:, :], ALU.add))
        ch.link(G.tensor_tensor(c["counts"][:, :], c["counts"][:, :], total[:, n, :], ALU.add))
    ch.link(G.tensor_tensor(base[:, :, :], base[:, :, :], rank, ALU.add))
    for k in range(pick.shape[1]):
        last = G.tensor_tensor(acc[:, k, :, :], base[:, :, :], pick[:, k, :, :], ALU.mult)
    ch.link(last)
    half = E // 2
    while half > 0:
        ch.link(G.tensor_tensor(acc[:, :, :, 0:half], acc[:, :, :, 0:half], acc[:, :, :, half:2 * half], ALU.add))
        half //= 2
    ch.announce(G.tensor_copy(slot_i, acc[:, :, :, 0]), signal, value)


class Turn:

    def __init__(self, k, first, lap0, static, rings):
        self.k, self.first, self.lap0, self.static, self.rings = k, first, lap0, static, rings

    def unit(self, lag):
        return self.k - lag

    def ring(self, lag):
        return (self.first - lag) % self.rings

    def lap(self, lag):
        return self.lap0 + (self.first - lag) // self.rings

    def has(self, lag, units):
        return self.static is None or 0 <= self.static - lag < units


def turns(engine, rings, step, last, full_from, full_to):
    for k in range(full_from):
        step(Turn(k, k % rings, k // rings, k, rings))
    n = (full_to - full_from) // rings
    with engine.Fori(0, n) as i:
        for h in range(rings):
            step(Turn(rings * i + (full_from + h), h, i + full_from // rings, None, rings))
    for k in range(full_from + rings * n, last + 1):
        step(Turn(k, k % rings, k // rings, k, rings))


def free_bank(engine, sems, turn, units, *readers):
    for name, lag, count, before in readers[:1] if turn.static is None else readers:
        value = (turn.k - lag) * count + before
        after(engine, sems[name], min(value, count * units) if turn.static is not None else value)


def mamba(nc, t, c, w, sb, ps, sem):
    X = c["X"]
    V, A, T = nc.vector, nc.scalar, nc.tensor
    hT = sb("hT", [P, 2, XPAD])
    xs = [sb(f"xs{u}", [P, 4, PW]) for u in range(2)]
    zs = [sb(f"zs{u}", [P, 2, PW]) for u in range(2)]
    xhat = sb("xhat", [P, PT, D])
    stats = sb("stats", [P, PT, 6])
    mv0, rstd0, rtmp = sb("mv0", [P, TILES, 2]), sb("rstd0", [P, TILES]), sb("rtmp", [P, 4, PT])
    mv1, rstd1 = sb("mv1", [P, PT, 2]), sb("rstd1", [P, PT])
    mv2, rstd2 = sb("mv2", [P, PT, 2]), sb("rstd2", [P, PT])
    sqs = sb("mean_square", [P, PT])
    dtr = sb("dt_raw", [P, PT, HEADS0])
    dte = sb("dt_exp", [P, PT, HEADS0])
    dtl = sb("dt_log", [P, PT, HEADS0])
    dtv = [sb(f"dt{u}", [P, PT, HEADS0]) for u in range(2)]
    dA = [sb(f"dA{u}", [P, PT, HEADS0]) for u in range(2)]
    uz = sb("dA_upto", [P, PT, HEADS0, P])
    L = [sb(f"decay{u}", [P, 2, 3, HEADS0, P]) for u in range(2)]
    sfx = sb("decay_to_end", [P, 2, HEADS0])
    cbm = sb("cb_masked", [P, 2, 3, P])
    mask3 = sb("mask3", [P, 3, P])
    xdt = [sb(f"x_dt{u}", [P, PT, HEADS0, HD0]) for u in range(2)]
    xde = [sb(f"x_dt_end{u}", [P, 2, HEADS0, HD0]) for u in range(2)]
    yg = sb("y_gated", [P, 2, PW])
    ysq = sb("y_square", [P, 2, PW])
    rms = sb("rms", [P, PT])
    res = sb("res", [P, PT, D])
    modbc = [sb(f"modbc{u}", [P, 2, 3, D]) for u in range(2)]
    h2 = sb("h2", [P, PT, D])
    h2T = sb("h2T", [P, PT, P])
    rows = [sb(f"rows{u}", [P, PT, ROW]) for u in range(2)]
    logits = sb("logits", [P, PT, E])
    diff = sb("logit_diff", [P, TILES, E])
    gsum = sb("gate_sum", [P, TILES])
    r = dict(top=sb("top", [P, PT, E]), idx=sb("idx", [P, PT, E], U32), idxf=sb("idxf", [P, PT, 2]),
             pick=sb("pick", [P, 1, PT, E]), acc=sb("pick_acc", [P, 1, PT, E]),
             base=sb("slot_base", [P, PT, E]))
    slot_i = [sb(f"slot_i{u}", [P, 1, PT], I32) for u in range(2)]

    pT = ps("pT", [P, 512])
    pX = [ps(f"pX{i}", [P, 512]) for i in range(2)]
    pS = [ps(f"pS{i}", [P, HEADS0, P]) for i in range(2)]
    pC = ps("pC", [P, 512])
    pY = [ps(f"pY{i}", [P, 2, 2, P]) for i in range(2)]
    pCB = pC[:, 0:384].rearrange("p (k t) -> p k t", t=P)
    p_dt = pC[:, 384:400].rearrange("p (t h) -> p t h", h=HEADS0)
    p_ss = pC[:, 400:404]
    p_lg = pC[:, 404:436].rearrange("p (t e) -> p t e", e=E)
    p_rk = pC[:, 436:468].rearrange("p (t e) -> p t e", e=E)
    p_tot = pC[:, 468:500].rearrange("p (t e) -> p t e", e=E)

    names = ("zeroed xhat hT_ps hT x_ps silu dt_ps dt_in dt_e dt_l dA uz seg_ps "
             "decay cb_ps cbm xv_ps xv sfx M_pool M y_ps yg ysq out_ps x1 mod router_in h2T_ps h2T lg_ps pick rk_ps "
             "slot diff gate_e lg_read mv0 rstd0 mv1 rstd1 mv2 rstd2 ss_ps sqs rms").split()
    s = {n: sem("m_" + n) for n in names}
    s_mod = [sem(f"m_modbc{u}") for u in range(2)]
    s_scat = [sem(f"m_scatter{u}", kept=True) for u in range(2)]
    s_v, s_a, s_g = sem("m_dve"), sem("m_act"), sem("m_pool")

    def bank_free(engine, turn, *readers):
        free_bank(engine, s, turn, PAIRS, *readers)

    def run_stages(tn, stages):
        for lag, stage, *more in stages:
            if tn.has(lag, PAIRS):
                stage(tn, tn.unit(lag), tn.ring(lag), *more)

    with nc.Block() as block:
        @block.sync
        def _(sp):
            load_expert_weights(sp, t, c, 0)
            def modulation(tn, p, u):
                after(sp, s["router_in"], p - 1)
                src = c["mod_dram"][0].rearrange("s (m d) -> s m d", d=D)[cols(2 * p, 2), 2:5, :]
                sp.dma_start(modbc[u][:, :, :, :], src.partition_broadcast(P)).then_inc(s_mod[u], 16)

            turns(sp, 2, lambda tn: run_stages(tn, ((1, modulation),)), PAIRS, 4, PAIRS)

        @block.gpsimd
        def _(pool):
            g = nc.gpsimd
            ch = Chain(pool, s_g)
            ch.link(g.memset(hT[:, :, 0:3], 0.0))
            for u in range(2):
                ch.link(g.memset(rows[u][:, :, :], 0.0))
            g.memset(mask3[:, 1, :], 1.0).then_inc(s["zeroed"], 1)
            for k in (0, 2):
                g.tensor_copy(mask3[:, k, :], c["upto"][:, :]).then_inc(s["zeroed"], 1)

            for n in range(PAIRS):
                pool.wait_ge(s["mv0"], n + 1)
                inverse_root(g, ch, c, rstd0[:, PT * n:PT * n + PT], rtmp[:, 0, :], mv0[:, PT * n:PT * n + PT, 1],
                             EPS_LN).then_inc(s["rstd0"], 1)
                pool.wait_ge(s["rstd0"], n + 1)

            def decays(tn, p, u):
                after(pool, s["dA"], p + 1)
                after(pool, s["seg_ps"], 6 * p)
                for n in range(PT):
                    g.tensor_tensor(uz[:, n, :, :], bc_last(dA[u][:, n, :], P),
                                    c["upto"][:, :].unsqueeze(1).broadcast_to([P, HEADS0, P]),
                                    ALU.mult).then_inc(s["uz"], 1)

            def experts_norm(tn, p, u):
                after_then(pool, s["mv2"], p + 1, s["rstd0"])
                inverse_root(g, ch, c, rstd2[:, :], rtmp[:, 2, :], mv2[:, :, 1], EPS_LN).then_inc(s["rstd2"], 1)

            def weigh(tn, p, u):
                for q in range(2):
                    after(pool, s["sfx"], 2 * p + q + 1)
                    after(pool, s["cbm"], 2 * p + q + 1)
                    g.tensor_tensor(L[u][:, q, 0, :, :], L[u][:, q, 0, :, :],
                                    cbm[:, q, 0, :].unsqueeze(1).broadcast_to([P, HEADS0, P]),
                                    ALU.mult).then_inc(s["M_pool"], 1)

            def squares(tn, p, u):
                after_then(pool, s["sqs"], p + 1, s["rstd0"])
                inverse_root(g, ch, c, rms[:, :], rtmp[:, 3, :], sqs[:, :], EPS_RMS).then_inc(s["rms"], 1)

            def scatter(tn, p, u):
                after_then(pool, s["slot"], p + 1, s["rstd0"])
                for n in range(PT):
                    pool.indirect_dma_start(c["routed"][0], bass.IndirectOffsetOnAxis(ap=slot_i[u][:, 0, n:n + 1], axis=0),
                                            rows[u][:, n, :], None).then_inc(s_scat[u], 16)

            def router_norm(tn, p, u):
                after_then(pool, s["mv1"], p + 1, s["rstd0"])
                inverse_root(g, ch, c, rstd1[:, :], rtmp[:, 1, :], mv1[:, :, 1], EPS_LN).then_inc(s["rstd1"], 1)

            def step(tn):
                ch.restart()
                run_stages(tn, ((3, experts_norm), (2, squares), (1, weigh), (0, decays), (2, router_norm),
                                (3, scatter)))
                ch.restart()

            turns(pool, 2, step, PAIRS + 2, 4, PAIRS)
            for u in range(2):
                pool.wait_ge(s_scat[u], 16 * PT * PAIRS // 2)

        @block.scalar
        def _(act):
            def modulate(tn, p, u):
                after(act, s["hT_ps"], p + 1)
                after(act, s["x_ps"], 6 * p)
                for q in range(2):
                    seq = cols(2 * p + q, 1)
                    A.activation(hT[:, q, 3:XPAD], pT[:, q * 256:q * 256 + 256], ACT.Identity,
                                 bias=c["modT"][0][:, SHIFT, seq], scale=c["modT"][0][:, SCALE, seq])\
                        .then_inc(s["hT"], 1)

            def softplus(tn, p, u):
                after(act, s["dt_in"], p + 1)
                A.activation(dte[:, :, :], dte[:, :, :], ACT.Exp).then_inc(s["dt_e"], 1)
                after(act, s["dt_e"], p + 1)
                A.activation(dtl[:, :, :], dte[:, :, :], ACT.Ln, bias=1.0).then_inc(s["dt_l"], 1)

            def silu(tn, p, u, b):
                if b == 0:
                    after(act, s["yg"], p - 1)
                after(act, s["x_ps"], 6 * p + b + 1)
                if b < 4:
                    A.activation(xs[u][:, b, :], pX[b % 2][:, :], ACT.Silu, bias=w["conv_bias"][:, b:b + 1])\
                        .then_inc(s["silu"], 1)
                else:
                    A.activation(zs[u][:, b - 4, :], pX[b % 2][:, :], ACT.Silu, bias=w["bin_ch"][:, b - 4:b - 3])\
                        .then_inc(s["silu"], 1)

            def decays(tn, p, u, first, end):
                after(act, s["y_ps"], 2 * (p - 1))
                for n in range(first, end):
                    after(act, s["seg_ps"], 6 * p + n + 1)
                    A.activation(L[u][:, n // 3, n % 3, :, :], pS[n % 2][:, :, :], ACT.Exp).then_inc(s["decay"], 1)

            def squares(tn, p, u):
                after(act, s["yg"], p + 1)
                after(act, s["ss_ps"], p)
                A.activation(ysq[:, :, :], yg[:, :, :], ACT.Square).then_inc(s["ysq"], 1)

            def router(tn, p, u):
                after(act, s["h2T_ps"], p + 1)
                after(act, s["lg_ps"], p)
                A.activation(h2T[:, :, :], pT[:, :].rearrange("p (n t) -> p n t", t=P), ACT.Copy)\
                    .then_inc(s["h2T"], 1)

            def step(tn):
                run_stages(tn, ((1, decays, 0, 4), (0, modulate), (1, decays, 4, 6), (2, squares), (0, softplus), (0, silu, 0), (3, router),
                                *((0, silu, b) for b in range(1, 6))))

            turns(act, 2, step, PAIRS + 2, 4, PAIRS)
            act.wait_ge(s["diff"], PAIRS)
            A.activation(diff[:, :, :], diff[:, :, :], ACT.Exp).then_inc(s["gate_e"], 1)

        @block.tensor
        def _(pe):
            def turn_input(tn, p, u):
                after(pe, s["xhat"], p + 1)
                bank_free(pe, tn, ("x1", 2, 1, 0), ("xv", 1, 2, 0), ("h2T", 3, 1, 0), ("hT", 0, 2, 0))
                for n in range(PT):
                    last = T.transpose(pT[:, n * P:n * P + P], xhat[:, n, :], c["ident"][:, :])
                last.then_inc(s["hT_ps"], 1)

            def steps(tn, p, u):
                pe.wait_ge(s["hT"], 2 * (p + 1))
                bank_free(pe, tn, ("slot", 3, 1, 0), ("cbm", 1, 2, 0), ("sqs", 2, 1, 0), ("dt_in", 0, 1, 0))
                for n in range(PT):
                    t0 = 3 + n % 2 * P
                    last = T.matmul(p_dt[:, n, :], hT[:, n // 2, t0:t0 + P], w["WinT"][:, 6 * P:6 * P + HEADS0],
                                    start=True, stop=True)
                last.then_inc(s["dt_ps"], 1)

            def project(tn, p, u, b):
                x2 = pX[b % 2][:, :].rearrange("p (q t) -> p q t", q=2)
                after(pe, s["silu"], 6 * p + b - 1)
                if b < 4:
                    for k in range(4):
                        last = T.matmul(x2, w["taps"][:, k, b * P:b * P + P], hT[:, :, k:k + SEQ_LEN],
                                        start=(k == 0), stop=(k == 3))
                        if k == 0:
                            T.matmul(x2[:, :, 0:3], c["ident"][:, :], w["edge"][:, b, :, :], start=False, stop=False)
                else:
                    last = T.matmul(x2, w["WinT"][:, (b - 4) * P:(b - 3) * P], hT[:, :, 3:XPAD],
                                    start=True, stop=True)
                last.then_inc(s["x_ps"], 1)

            def decays(tn, p, u, first, end):
                for n in range(first, end):
                    q, k = n // 3, n % 3
                    tile = 2 * q + (k > 0)
                    after(pe, s["uz"], PT * p + tile + 1)
                    after(pe, s["decay"], 6 * p + n - 1)
                    T.matmul(pS[n % 2][:, :, :], c["ones"][:, :] if k == 1 else c["beyond"][:, :],
                             uz[:, tile, :, :], start=True, stop=True).then_inc(s["seg_ps"], 1)

            def values(tn, p, u, q):
                pe.wait_ge(s["silu"], 6 * p + 4)
                if q == 0:
                    bank_free(pe, tn, ("h2T", 3, 1, 1), ("hT", 0, 2, 2), ("x1", 2, 1, 0))
                else:
                    pe.wait_ge(s["xv"], 2 * p + 1)
                for n in range(2):
                    for b in range(2):
                        last = T.transpose(pT[:, (2 * n + b) * P:(2 * n + b + 1) * P],
                                           xs[u][:, b, (2 * q + n) * P:(2 * q + n + 1) * P], c["ident"][:, :])
                last.then_inc(s["xv_ps"], 1)
                if q == 0:
                    bank_free(pe, tn, ("sqs", 2, 1, 1), ("lg_read", 3, 1, 1), ("dt_in", 0, 1, 1))
                else:
                    pe.wait_ge(s["cbm"], 2 * p + 1)
                t0 = q * SEQ_LEN
                T.matmul(pC[:, 0:256], xs[u][:, 2, t0:t0 + P], xs[u][:, 3, t0:t0 + 256], start=True, stop=True)
                T.matmul(pC[:, 256:384], xs[u][:, 2, t0 + P:t0 + 256], xs[u][:, 3, t0 + P:t0 + 256],
                         start=True, stop=True).then_inc(s["cb_ps"], 1)

            def mixed(tn, p, u):
                after(pe, s["M_pool"], 2 * p + 2)
                after(pe, s["M"], 2 * p + 2)
                after(pe, s["yg"], p)
                for b in range(2):
                    for q in range(2):
                        for e in range(2):
                            h = 2 * b + e
                            o = slice(HD0 * e, HD0 * e + HD0)
                            T.matmul(pY[b][o, q, 0, :], xdt[u][:, 2 * q, h, :], L[u][:, q, 0, h, :],
                                     start=True, stop=True)
                            T.matmul(pY[b][o, q, 1, :], xde[u][:, q, h, :], L[u][:, q, 1, h, :],
                                     start=True, stop=False)
                            last = T.matmul(pY[b][o, q, 1, :], xdt[u][:, 2 * q + 1, h, :], L[u][:, q, 2, h, :],
                                            start=False, stop=True)
                    last.then_inc(s["y_ps"], 1)

            def output(tn, p, u):
                pe.wait_ge(s["yg"], p + 1)
                bank_free(pe, tn, ("xv", 1, 2, 2), ("h2T", 3, 1, 1), ("hT", 0, 2, 2))
                for n in range(PT):
                    for b in range(2):
                        last = T.matmul(pT[:, n * P:n * P + P], yg[:, b, n * P:n * P + P], w["WoT"][:, b, :],
                                        start=(b == 0), stop=(b == 1))
                last.then_inc(s["out_ps"], 1)

            def squares(tn, p, u):
                pe.wait_ge(s["ysq"], p + 1)
                bank_free(pe, tn, ("lg_read", 3, 1, 1), ("dt_in", 0, 1, 1), ("cbm", 1, 2, 0))
                for n in range(PT):
                    for b in range(2):
                        last = T.matmul(p_ss[:, n:n + 1], ysq[:, b, n * P:n * P + P], c["ones"][:, 0:1],
                                        start=(b == 0), stop=(b == 1))
                last.then_inc(s["ss_ps"], 1)

            def turn_router(tn, p, u):
                pe.wait_ge(s["router_in"], p + 1)
                bank_free(pe, tn, ("hT", 0, 2, 2), ("x1", 2, 1, 0), ("xv", 1, 2, 0))
                for n in range(PT):
                    last = T.transpose(pT[:, n * P:n * P + P], h2[:, n, :], c["ident"][:, :])
                last.then_inc(s["h2T_ps"], 1)

            def logits_(tn, p, u):
                pe.wait_ge(s["h2T"], p + 1)
                bank_free(pe, tn, ("dt_in", 0, 1, 1), ("cbm", 1, 2, 0), ("sqs", 2, 1, 0), ("slot", 3, 1, 0))
                for n in range(PT):
                    last = T.matmul(p_lg[:, n, :], h2T[:, n, :], w["Wr"][0][:, :], start=True, stop=True)
                last.then_inc(s["lg_ps"], 1)

            def ranks(tn, p, u):
                pe.wait_ge(s["pick"], p + 1)
                bank_free(pe, tn, ("cbm", 1, 2, 2), ("sqs", 2, 1, 1), ("lg_read", 3, 1, 1))
                T.matmul(p_rk, c["before"][:, :], r["pick"][:, 0, :, :], start=True, stop=True)
                T.matmul(p_tot, c["ones"][:, :], r["pick"][:, 0, :, :], start=True, stop=True).then_inc(s["rk_ps"], 1)

            def step(tn):
                run_stages(tn, ((2, mixed), (1, decays, 0, 4), (0, turn_input), (1, decays, 4, 6), (0, steps),
                                (0, project, 0), (3, turn_router), (0, project, 1), (3, logits_), (2, squares),
                                (1, values, 0), (0, project, 2), (1, values, 1), (0, project, 3), (3, ranks),
                                (2, output), (0, project, 4), (0, project, 5)))

            turns(pe, 2, step, PAIRS + 2, 4, PAIRS)

        @block.vector
        def _(dve):
            v = Chain(dve, s_v)
            v.link(V.memset(c["counts"][:, :], 0.0))
            for n in range(PAIRS):
                moments(V, v, lambda i: X[:, PT * n + i, :], stats, mv0[:, PT * n:PT * n + PT, :], PT)\
                    .then_inc(s["mv0"], 1)
                dve.wait_ge(s["mv0"], n + 1)
            dve.wait_ge(s["rstd0"], PAIRS)
            dve.wait_ge(s["zeroed"], 3)
            def norm_input(tn, p, u):
                after(dve, s["hT_ps"], p)
                m, r0 = mv0[:, cols(PT * p, PT), :], rstd0[:, cols(PT * p, PT)]
                v.announce(normalize(V, lambda n: tile_at(X, PT * p + n), lambda n: xhat[:, n, :], m, r0, PT),
                           s["xhat"], p + 1)

            def dt_in(tn, p, u):
                dve.wait_ge(s["dt_ps"], p + 1)
                v.link(V.tensor_tensor(dtr[:, :, :], p_dt,
                                       w["dt_bias"][:, :].unsqueeze(1).broadcast_to([P, PT, HEADS0]), ALU.add))
                v.announce(V.scalar_tensor_tensor(dte[:, :, :], dtr[:, :, :], -1.0, dtr[:, :, :], ALU.mult, ALU.min),
                           s["dt_in"], p + 1)

            def dt_out(tn, p, u):
                dve.wait_ge(s["dt_l"], p + 1)
                v.link(V.scalar_tensor_tensor(dtv[u][:, :, :], dtr[:, :, :], 0.0, dtl[:, :, :], ALU.max, ALU.add))
                v.announce(V.tensor_tensor(dA[u][:, :, :], dtv[u][:, :, :],
                                           w["A"][:, :].unsqueeze(1).broadcast_to([P, PT, HEADS0]), ALU.mult),
                           s["dA"], p + 1)

            def values(tn, p, u, q):
                dve.wait_ge(s["cb_ps"], 2 * p + q + 1)
                after(dve, s["M_pool"], 2 * p + q - 1)
                V.tensor_tensor(cbm[:, q, :, :], pCB, mask3[:, :, :], ALU.mult).then_inc(s["cbm"], 1)
                dve.wait_ge(s["xv_ps"], 2 * p + q + 1)
                V.tensor_tensor(xdt[u][:, 2 * q:2 * q + 2, :, :].rearrange("p n h d -> p (n h) d"),
                                pT[:, :].rearrange("p (n d) -> p n d", d=HD0),
                                bc_last(dtv[u][:, 2 * q:2 * q + 2, :].rearrange("p n h -> p (n h)"), HD0),
                                ALU.mult).then_inc(s["xv"], 1)
                dve.wait_ge(s["decay"], 6 * p + 3 * q + 3)
                V.tensor_copy(sfx[:, q, :], L[u][:, q, 0, :, P - 1]).then_inc(s["sfx"], 1)
                dve.wait_ge(s["cbm"], 2 * p + q + 1)
                last = V.tensor_tensor(L[u][:, q, 1, :, :], L[u][:, q, 1, :, :],
                                       cbm[:, q, 1, :].unsqueeze(1).broadcast_to([P, HEADS0, P]), ALU.mult)
                dve.wait_ge(s["sfx"], 2 * p + q + 1)
                dve.wait_ge(s["xv"], 2 * p + q + 1)
                V.tensor_tensor(xde[u][:, q, :, :], xdt[u][:, 2 * q, :, :], bc_last(sfx[:, q, :], HD0), ALU.mult)
                v.announce(V.tensor_tensor(L[u][:, q, 2, :, :], L[u][:, q, 2, :, :],
                                           cbm[:, q, 2, :].unsqueeze(1).broadcast_to([P, HEADS0, P]), ALU.mult),
                           s["M"], 2 * p + q + 1)

            def mixed(tn, p, u):
                dve.wait_ge(s["silu"], 6 * p + 6)
                for b in range(2):
                    dve.wait_ge(s["y_ps"], 2 * p + b + 1)
                    last = V.scalar_tensor_tensor(yg[:, b, :], xs[u][:, b, :], w["D_ch"][:, b:b + 1],
                                                  pY[b][:, :, :, :].rearrange("p q k t -> p (q k t)"),
                                                  ALU.mult, ALU.add)
                v.link(last)
                v.announce(V.tensor_tensor(yg[:, :, :], yg[:, :, :], zs[u][:, :, :], ALU.mult), s["yg"], p + 1)

            def squares(tn, p, u):
                dve.wait_ge(s["ss_ps"], p + 1)
                v.announce(V.tensor_scalar(sqs[:, :], p_ss, 1.0 / DSSM, None, ALU.mult), s["sqs"], p + 1)

            def output(tn, p, u):
                dve.wait_ge(s["out_ps"], p + 1)
                dve.wait_ge(s["rms"], p + 1)
                v.link(V.tensor_tensor(res[:, :, :], pT[:, :].rearrange("p (n d) -> p n d", d=D),
                                       bc_last(rms[:, :], D), ALU.mult))
                v.link(V.tensor_tensor(res[:, :, :], res[:, :, :],
                                       w["bout_bc"][:, :].unsqueeze(1).broadcast_to([P, PT, D]), ALU.add))
                after(dve, s_mod[u], 16 * tn.lap(2) + 16)
                for q in range(2):
                    last = V.tensor_tensor(res[:, 2 * q:2 * q + 2, :], res[:, 2 * q:2 * q + 2, :],
                                           modbc[u][:, q, 0, :].unsqueeze(1).broadcast_to([P, 2, D]), ALU.mult)
                v.link(last)
                x = X[:, cols(PT * p, PT), :]
                V.tensor_tensor(x, x, res[:, :, :], ALU.add).then_inc(s["x1"], 1)
                after_then(dve, s["x1"], p + 1, s["rstd0"])
                v.announce(moments(V, v, lambda n: tile_at(X, PT * p + n), stats, mv1, PT), s["mv1"], p + 1)

            def router_input(tn, p, u):
                dve.wait_ge(s["rstd1"], p + 1)
                v.link(normalize(V, lambda n: tile_at(X, PT * p + n), lambda n: h2[:, n, :], mv1, rstd1, PT))
                for m, op in ((2, ALU.mult), (1, ALU.add)):
                    for q in range(2):
                        last = V.tensor_tensor(h2[:, 2 * q:2 * q + 2, :], h2[:, 2 * q:2 * q + 2, :],
                                               modbc[u][:, q, m, :].unsqueeze(1).broadcast_to([P, 2, D]), op)
                    if m == 2:
                        v.link(last)
                last.then_inc(s["router_in"], 1)
                after_then(dve, s["router_in"], p + 1, s["rstd0"])
                v.announce(moments(V, v, lambda n: h2[:, n, :], stats, mv2, PT), s["mv2"], p + 1)

            def choose(tn, p, u):
                dve.wait_ge(s["lg_ps"], p + 1)
                v.announce(V.tensor_tensor(logits[:, :, :], p_lg,
                                           w["br_bc"][:, :].unsqueeze(1).broadcast_to([P, PT, E]), ALU.add),
                           s["lg_read"], p + 1)
                dve.wait_ge(s["rstd0"], 1)
                dve.nop(nofuse=True)
                v.announce(route(V, v, c, logits, r, PT, 0), s["pick"], p + 1)
                v.announce(V.tensor_tensor(diff[:, cols(PT * p, PT), :], logits[:, :, :],
                                           bc_last(r["top"][:, :, 0], E), ALU.subtract), s["diff"], p + 1)

            def experts_input(tn, p, u):
                dve.wait_ge(s["rstd2"], p + 1)
                after(dve, s_scat[1 - u], 16 * PT * (tn.lap(3) + u))
                v.link(normalize(V, lambda n: h2[:, n, :], lambda n: rows[u][:, n, 0:D], mv2, rstd2, PT))
                for m, op in ((0, ALU.mult), (1, ALU.add)):
                    v.link(V.tensor_tensor(rows[u][:, :, 0:D], rows[u][:, :, 0:D],
                                           w["ln_bc"][:, m, :].unsqueeze(1).broadcast_to([P, PT, D]), op))
                v.link(V.tensor_copy(rows[u][:, :, D], c["token_id"][:, cols(PT * p, PT)]))

            def place(tn, p, u):
                dve.wait_ge(s["rk_ps"], p + 1)
                place_rows(V, v, c, r, p_rk, p_tot, slot_i[u][:, :, :], PT, s["slot"], p + 1)

            def step(tn):
                v.restart()
                run_stages(tn, ((2, mixed), (0, norm_input), (3, router_input), (0, dt_in), (0, dt_out),
                                (3, experts_input), (3, choose), (2, squares), (1, values, 0), (1, values, 1),
                                (3, place), (2, output)))
                v.restart()

            turns(dve, 2, step, PAIRS + 2, 4, PAIRS)
            dve.wait_ge(s["gate_e"], 1)
            v.link(V.tensor_reduce(gsum[:, :], diff[:, :, :], AX.X, ALU.add))
            v.link(V.reciprocal(c["gates"][:, 0, :], gsum[:, :]))


def attention(nc, t, c, w, sb, ps, sem):
    X = c["X"]
    V, A, T = nc.vector, nc.scalar, nc.tensor
    S2 = SEQ_LEN // P
    H, KR = HEADS1, 6 * HD1
    a0 = [sb(f"a0_{u}", [P, S2, D]) for u in range(3)]
    gbc = [sb(f"gate0_bc{u}", [P, D]) for u in range(3)]
    modbc = [sb(f"modbc{u}", [P, 3, D]) for u in range(3)]
    mv0, rstd0 = [sb(f"mv0_{u}", [P, S2, 2]) for u in range(3)], [sb(f"rstd0_{u}", [P, S2]) for u in range(3)]
    mv1, rstd1 = [sb(f"mv1_{u}", [P, S2, 2]) for u in range(3)], [sb(f"rstd1_{u}", [P, S2]) for u in range(3)]
    stats, rtmp = sb("stats", [P, S2, 6]), sb("rtmp", [P, 2, S2])
    res = sb("res", [P, S2, D])
    xhat = sb("xhat", [P, S2, D])
    hT = sb("hT", [P, SEQ_LEN])
    parts = [sb(f"qk_parts{u}", [P, 3, 2 * SEQ_LEN], BF16) for u in range(3)]
    rest = sb("qk_rest", [P, 2 * SEQ_LEN])
    vv = [sb(f"v_ones{u}", [P, S2, H, LAT]) for u in range(3)]
    Q = [sb(f"q_rows{u}", [P, H, SEQ_LEN], BF16) for u in range(3)]
    K = [sb(f"k_rows{u}", [P, H, SEQ_LEN], BF16) for u in range(3)]
    maskq, maskk = sb("mask_q", [P, 4, P], BF16), sb("mask_k", [P, 4, P], BF16)
    mx = sb("row_max", [P, 3, H])
    nm = sb("neg_max", [P, S2, H])
    mT = sb("max_parts", [H, 2, SEQ_LEN], BF16)
    pr = [sb(f"probs{i}", [P, 4, P]) for i in range(6)]
    oT = sb("out_T", [P, 4, SEQ_LEN])
    rden = sb("rden", [P, S2, H])
    yv = sb("y_tok", [P, S2, H, HD1])
    h2T = sb("h2T", [P, S2, P])
    rows = [sb(f"rows{u}", [P, 2, S2, ROW]) for u in range(3)]
    top2 = sb("top2", [P, TILES, 2])
    logits = sb("logits", [P, S2, E])
    r = dict(top=sb("top", [P, S2, E]), idx=sb("idx", [P, S2, E], U32), idxf=sb("idxf", [P, S2, 2]),
             pick=sb("pick", [P, 2, S2, E]), acc=sb("pick_acc", [P, 2, S2, E]), base=sb("slot_base", [P, S2, E]))
    rk = sb("ranks", [P, 2, S2, E])
    both = sb("pick_both", [P, S2, E])
    slot_i = [sb(f"slot_i{u}", [P, 2, S2], I32) for u in range(3)]
    gexp = sb("gate_exp", [P, TILES])

    pT, pP = ps("pT", [P, 512]), ps("pP", [P, 512])
    pS = [ps(f"pS{i}", [P, 4, P]) for i in range(4)]
    pO = ps("pO", [P, 4, SEQ_LEN])
    p_lg = pT[:, 0:S2 * E].rearrange("p (n e) -> p n e", e=E)
    p_rk = pT[:, 0:2 * S2 * E].rearrange("p (k n e) -> p k n e", n=S2, e=E)

    names = ("zeroed mv0 rstd0 xhat hT_ps hT qk_ps part1 rest1 part2 parts v_ps v scores max neg mT_ps m1 m2 "
             "probs_ps probs pv oT yT_ps yT x3 mv1 rstd1 h2 h2T_ps h2T lg_ps lg_read pick rk_ps rk_read slot gexp").split()
    s = {n: sem("a_" + n) for n in names}
    s_a0, s_mod, s_dram, s_qk, s_m = ([sem(f"a_{n}{u}") for u in range(3)] for n in
                                      ("answers", "modbc", "parts_dram", "packed", "max_rows"))
    s_scat = [sem(f"a_scatter{u}", kept=True) for u in range(3)]
    s_v, s_g = sem("a_dve"), sem("a_pool")
    ZEROED = 12

    def bank_free(engine, turn, *readers):
        free_bank(engine, s, turn, SEQS, *readers)

    UNITS = [(g, m) for g in range(4) for m in range(3)]
    TILE_PAIR = ((0, 0), (0, 1), (1, 1))

    with nc.Block() as block:
        @block.sync
        def _(sp):
            load_expert_weights(sp, t, c, 1)
            qp = c["parts_dram"]

            def load(p, u, lap):
                after(sp, s["mv0"], p - 2)
                sp.dma_start(a0[u][:, :, :], c["answers"][0][cols(2 * P * p, 2 * P), :]
                             .rearrange("(n p) d -> p n d", p=P)).then_inc(s_a0[u], 16)
                m0 = c["mod_dram"][0].rearrange("s (m d) -> s m d", d=D)[cols(p, 1), 5:6, :]
                sp.dma_start(gbc[u][:, :], m0.rearrange("s m d -> (s m) d").rearrange("a d -> (a d)").partition_broadcast(P))\
                    .then_inc(s_a0[u], 16)

            def modulation(p, u, lap):
                after(sp, s["h2"], p - 2)
                m1 = c["mod_dram"][1].rearrange("s (m d) -> s m d", d=D)[cols(p, 1), 2:5, :]
                sp.dma_start(modbc[u][:, :, :], m1.rearrange("s m d -> (s m) d").partition_broadcast(P))\
                    .then_inc(s_mod[u], 16)

            def pack(p, u, lap):
                after(sp, s["parts"], p + 1)
                sp.dma_start(qp[u], parts[u][:, :, :]).then_inc(s_dram[u], 16)
                after(sp, s_dram[u], 16 * lap + 16)
                after(sp, s["probs_ps"], 12 * (p - 2))
                v = qp[u].rearrange("(h d) i t -> i d h t", d=HD1)
                for r6, (a, b) in enumerate(((0, 0), (1, 0), (2, 0), (0, 1), (1, 1), (0, 2))):
                    sp.dma_start(Q[u][r6 * HD1:r6 * HD1 + HD1, :, :], v[a][:, :, 0:SEQ_LEN]).then_inc(s_qk[u], 16)
                    sp.dma_start(K[u][r6 * HD1:r6 * HD1 + HD1, :, :], v[b][:, :, SEQ_LEN:2 * SEQ_LEN])\
                        .then_inc(s_qk[u], 16)
                sp.dma_start(Q[u][KR:KR + 2, :, :], Q[u][P - 2:P, :, :]).then_inc(s_qk[u], 16)

            def max_rows(p, u, lap):
                after(sp, s["m2"], p + 1)
                after(sp, s["scores"], 12 * p + 12)
                for i in range(2):
                    sp.dma_start(Q[u][KR + i:KR + i + 1, :, :], mT[:, i, :]).then_inc(s_m[u], 16)

            def step(tn):
                for lag, stage in ((2, pack), (0, load), (4, modulation), (3, max_rows)):
                    if tn.has(lag, SEQS):
                        stage(tn.unit(lag), tn.ring(lag), tn.lap(lag))

            sp.wait_ge(s["zeroed"], ZEROED)
            turns(sp, 3, step, SEQS + 3, 9, SEQS)

        @block.gpsimd
        def _(pool):
            g = nc.gpsimd
            ch = Chain(pool, s_g)
            for u in range(3):
                g.memset(Q[u][:, :, :], 0.0).then_inc(s["zeroed"], 1)
                ch.link(g.memset(K[u][:, :, :], 1.0))
                g.affine_select(out=K[u][:, :, :], in_=K[u][:, :, :], compare_op=ALU.is_ge, fill=0.0,
                                base=KR + 1, pattern=[[0, H * SEQ_LEN]], channel_multiplier=-1)\
                    .then_inc(s["zeroed"], 1)
                ch.link(g.memset(vv[u][:, :, :, :], 0.0))
                ch.link(g.memset(rows[u][:, :, :, :], 0.0))
                g.memset(vv[u][:, :, :, HD1:HD1 + 1], 1.0).then_inc(s["zeroed"], 1)
            for n, (m, sign) in enumerate(((maskq, 1), (maskk, -1))):
                ch.link(g.memset(m[:, :, :], 0.0))
                g.affine_select(out=m[:, :, :], in_=m[:, :, :], compare_op=ALU.is_ge, fill=MASKED, base=0,
                                pattern=[[0, 4], [-sign, P]], channel_multiplier=sign).then_inc(s["zeroed"], 1)
            g.memset(rtmp[:, :, :], 0.0).then_inc(s["zeroed"], 1)
            pool.wait_ge(s["zeroed"], ZEROED)

            def load(p, u):
                after_then(pool, s["mv0"], p + 1, s["zeroed"])
                inverse_root(g, ch, c, rstd0[u][:, :], rtmp[:, 0, :], mv0[u][:, :, 1], EPS_LN).then_inc(s["rstd0"], 1)

            def output(p, u):
                after_then(pool, s["mv1"], p + 1, s["zeroed"])
                inverse_root(g, ch, c, rstd1[u][:, :], rtmp[:, 1, :], mv1[u][:, :, 1], EPS_LN)\
                    .then_inc(s["rstd1"], 1)

            def place(p, u):
                after_then(pool, s["rk_read"], p + 1, s["zeroed"])
                place_rows(g, ch, c, r, rk[:, 0, :, :], rk[:, 1, :, :], slot_i[u][:, :, :], S2, s["slot"], p + 1)

            def scatter(p, u):
                after_then(pool, s["slot"], p + 1, s["zeroed"])
                for k in range(2):
                    for n in range(S2):
                        pool.indirect_dma_start(c["routed"][1],
                                                bass.IndirectOffsetOnAxis(ap=slot_i[u][:, k, n:n + 1], axis=0),
                                                rows[u][:, k, n, :], None).then_inc(s_scat[u], 16)

            def step(tn):
                ch.restart()
                for lag, stage in ((7, place), (5, output), (0, load), (7, scatter)):
                    if tn.has(lag, SEQS):
                        stage(tn.unit(lag), tn.ring(lag))
                ch.restart()

            turns(pool, 3, step, SEQS + 6, 9, SEQS)
            for u in range(3):
                pool.wait_ge(s_scat[u], 16 * 4 * len(range(u, SEQS, 3)))

        @block.scalar
        def _(act):
            def project(tn):
                p = tn.unit(1)
                after(act, s["hT_ps"], p + 1)
                after(act, s["v_ps"], p)
                A.activation(hT[:, :], pT[:, 0:SEQ_LEN], ACT.Identity, bias=c["modT"][1][:, SHIFT, cols(p, 1)],
                             scale=c["modT"][1][:, SCALE, cols(p, 1)]).then_inc(s["hT"], 1)

            def ranks(tn):
                p = tn.unit(7)
                after(act, s["rk_ps"], p + 1)
                after(act, s["slot"], p)
                A.activation(rk[:, :, :, :], p_rk, ACT.Copy).then_inc(s["rk_read"], 1)

            def router(tn):
                p = tn.unit(6)
                after(act, s["h2T_ps"], p + 1)
                after(act, s["lg_ps"], p)
                A.activation(h2T[:, :, :], pP[:, 0:SEQ_LEN].rearrange("p (n t) -> p n t", t=P), ACT.Copy)\
                    .then_inc(s["h2T"], 1)

            def first_part(tn):
                p, u = tn.unit(1), tn.ring(1)
                after(act, s["qk_ps"], p + 1)
                after(act, s_dram[u], 16 * tn.lap(1))
                A.activation(parts[u][:, 0, :], pP[:, :], ACT.Copy).then_inc(s["part1"], 1)

            def second_part(tn):
                p, u = tn.unit(1), tn.ring(1)
                after(act, s["rest1"], p + 1)
                A.activation(parts[u][:, 1, :], rest[:, :], ACT.Copy).then_inc(s["part2"], 1)

            def exponentials(tn, g):
                p = tn.unit(4)
                after(act, s["pv"], 4 * p + g - 1)
                for i in range(3 * g, 3 * g + 3):
                    after(act, s["probs_ps"], 12 * p + i + 1)
                    A.activation(pr[i % 6][:, :, :], pS[2 + i % 2][:, :, :], ACT.Exp, scale=HD1 ** -0.5)\
                        .then_inc(s["probs"], 1)

            def mixed(tn):
                p = tn.unit(4)
                after(act, s["pv"], 4 * p + 4)
                after(act, s["yT_ps"], 2 * p)
                A.activation(oT[:, :, :], pO[:, :, :], ACT.Copy).then_inc(s["oT"], 1)

            def maxima(tn):
                p, u = tn.unit(3), tn.ring(3)
                after(act, s["mT_ps"], p + 1)
                if tn.has(4, SEQS):
                    after(act, s_m[tn.ring(4)], 32 * tn.lap(4) + 32)
                A.activation(mT[:, 0, :], pT[0:H, 0:SEQ_LEN], ACT.Copy).then_inc(s["m1"], 1)

            def step(tn):
                for lag, stage, *rest_ in (
                        (1, project), (7, ranks), (4, exponentials, 0), (4, exponentials, 1), (6, router), (4, exponentials, 2),
                        (1, first_part), (4, exponentials, 3), (1, second_part), (3, maxima), (4, mixed)):
                    if tn.has(lag, SEQS):
                        stage(tn, *rest_)

            turns(act, 3, step, SEQS + 6, 9, SEQS)
            act.wait_ge(s["gexp"], 1)
            A.activation(gexp[:, :], gexp[:, :], ACT.Exp).then_inc(s["gexp"], 1)

        @block.tensor
        def _(pe):
            def turn_input(tn):
                p = tn.unit(1)
                after(pe, s["xhat"], p + 1)
                bank_free(pe, tn, ("m2", 3, 1, 0), ("lg_read", 6, 1, 0), ("rk_read", 7, 1, 0), ("hT", 1, 1, 0))
                for n in range(S2):
                    last = T.transpose(pT[:, n * P:n * P + P], xhat[:, n, :], c["ident"][:, :])
                last.then_inc(s["hT_ps"], 1)

            def turn_router(tn):
                p = tn.unit(6)
                after(pe, s["h2"], p + 1)
                bank_free(pe, tn, ("yT", 5, 2, 2), ("v", 1, 1, 0))
                for n in range(S2):
                    last = T.transpose(pP[:, n * P:n * P + P], rows[tn.ring(6)][:, 0, n, 0:D], c["ident"][:, :])
                last.then_inc(s["h2T_ps"], 1)

            def maxima(tn, i):
                p, u = tn.unit(3), tn.ring(3)
                if i == 0:
                    after(pe, s_qk[u], 16 * 13 * tn.lap(3) + 16 * 13)
                g, m = UNITS[i]
                kt, qt = TILE_PAIR[m]
                after(pe, s["max"], 12 * p + i - 1)
                if kt == qt:
                    T.matmul(pS[i % 2][:, :, :], c["identb"][:, :], maskq[:, :, :], start=True, stop=False)
                for h in range(4):
                    last = T.matmul(pS[i % 2][:, h, :], Q[u][:, 4 * g + h, qt * P:qt * P + P],
                                    K[u][:, 4 * g + h, kt * P:kt * P + P], start=(kt != qt),
                                    stop=(kt != qt or h == 3))
                last.then_inc(s["scores"], 1)

            def logits_(tn):
                p = tn.unit(6)
                after(pe, s["h2T"], p + 1)
                bank_free(pe, tn, ("rk_read", 7, 1, 1), ("hT", 1, 1, 1), ("m2", 3, 1, 0))
                for n in range(S2):
                    last = T.matmul(p_lg[:, n, :], h2T[:, n, :], w["Wr"][1][:, :], start=True, stop=True)
                last.then_inc(s["lg_ps"], 1)

            def queries_keys(tn):
                p = tn.unit(1)
                after(pe, s["hT"], p + 1)
                bank_free(pe, tn, ("h2T", 6, 1, 1), ("yT", 5, 2, 2), ("v", 1, 1, 0))
                for i in range(2):
                    last = T.matmul(pP[:, i * SEQ_LEN:i * SEQ_LEN + SEQ_LEN], w["Wqkv"][:, i, :], hT[:, :],
                                    start=True, stop=True)
                last.then_inc(s["qk_ps"], 1)

            def ranks(tn):
                p = tn.unit(7)
                after(pe, s["pick"], p + 1)
                bank_free(pe, tn, ("hT", 1, 1, 1), ("m2", 3, 1, 0), ("lg_read", 6, 1, 0))
                T.matmul(p_rk[:, 0, :, :], c["before"][:, :], both[:, :, :], start=True, stop=True)
                T.matmul(p_rk[:, 1, :, :], c["ones"][:, :], both[:, :, :], start=True, stop=True)\
                    .then_inc(s["rk_ps"], 1)

            def mix(tn, g, m):
                p, u = tn.unit(4), tn.ring(4)
                kt, qt = TILE_PAIR[m]
                if g == 0 and m == 0:
                    after(pe, s_m[u], 32 * tn.lap(4) + 32)
                if g < 4:
                    i = 3 * g + m
                    after(pe, s["probs"], 12 * p + i - 1)
                    if kt == qt:
                        T.matmul(pS[2 + i % 2][:, :, :], c["identb"][:, :], maskk[:, :, :], start=True, stop=False)
                    for h in range(4):
                        last = T.matmul(pS[2 + i % 2][:, h, :], K[u][:, 4 * g + h, kt * P:kt * P + P],
                                        Q[u][:, 4 * g + h, qt * P:qt * P + P], start=(kt != qt),
                                        stop=(kt != qt or h == 3))
                    last.then_inc(s["probs_ps"], 1)
                if g > 0:
                    if g == 1 and m == 0:
                        after(pe, s["v"], p + 1)
                        after(pe, s["oT"], p)
                    i = 3 * (g - 1) + m
                    after(pe, s["probs"], 12 * p + i + 1)
                    for h in range(4):
                        last = T.matmul(pO[32 * h:32 * h + 32, g - 1, qt * P:qt * P + P],
                                        vv[u][:, kt, 4 * (g - 1) + h, :], pr[i % 6][:, h, :],
                                        start=(m != 2), stop=(m != 1))
                    if m == 2:
                        last.then_inc(s["pv"], 1)

            def turn_output(tn, n):
                p = tn.unit(5)
                after(pe, s["oT"], p + 1)
                bank_free(pe, tn, *([("yT", 5, 2, 1)] if n else [("v", 1, 1, 0), ("yT", 5, 2, 0), ("h2T", 6, 1, 0)]))
                for g in range(4):
                    last = T.transpose(pP[:, g * P:g * P + P], oT[:, g, n * P:n * P + P], c["ident"][:, :])
                last.then_inc(s["yT_ps"], 1)

            def turn_max(tn):
                p = tn.unit(3)
                after(pe, s["neg"], p + 1)
                bank_free(pe, tn, ("lg_read", 6, 1, 1), ("rk_read", 7, 1, 1), ("hT", 1, 1, 1))
                for n in range(S2):
                    last = T.transpose(pT[0:H, n * P:n * P + P], nm[:, n, :], c["ident"][:, :])
                last.then_inc(s["mT_ps"], 1)

            def values(tn):
                p = tn.unit(1)
                after(pe, s["rest1"], p + 1)
                for n in range(S2):
                    last = T.matmul(pP[:, n * P:n * P + P], hT[:, n * P:n * P + P], w["Wqkv"][:, 2, :],
                                    start=True, stop=True)
                last.then_inc(s["v_ps"], 1)

            def step(tn):
                for lag, stage, *rest_ in (
                        (1, turn_input), (3, maxima, 0), (3, maxima, 1), (5, turn_output, 0), (3, maxima, 2),
                        (5, turn_output, 1), (7, ranks), (4, mix, 0, 0), (3, maxima, 3), (4, mix, 0, 1),
                        (3, maxima, 4), (4, mix, 0, 2), (4, mix, 1, 0), (3, maxima, 5), (4, mix, 1, 1),
                        (3, maxima, 6), (4, mix, 1, 2), (6, turn_router), (4, mix, 2, 0), (3, maxima, 7),
                        (4, mix, 2, 1), (3, maxima, 8), (4, mix, 2, 2), (6, logits_), (1, queries_keys),
                        (3, maxima, 9), (4, mix, 3, 0), (3, maxima, 10), (4, mix, 3, 1), (3, maxima, 11),
                        (4, mix, 3, 2), (1, values), (4, mix, 4, 0), (3, turn_max), (4, mix, 4, 1), (4, mix, 4, 2)):
                    if tn.has(lag, SEQS):
                        stage(tn, *rest_)

            pe.wait_ge(s["zeroed"], ZEROED)
            turns(pe, 3, step, SEQS + 6, 9, SEQS)

        @block.vector
        def _(dve):
            v = Chain(dve, s_v)
            dve.wait_ge(s["zeroed"], ZEROED)
            v.link(V.memset(c["counts"][:, :], 0.0))

            def maxima(tn, i):
                g, m = UNITS[i]
                dve.wait_ge(s["scores"], 12 * tn.unit(3) + i + 1)
                V.tensor_reduce(mx[:, m, 4 * g:4 * g + 4], pS[i % 2][:, :, :], AX.X, ALU.max).then_inc(s["max"], 1)

            def negate(tn):
                p = tn.unit(3)
                dve.wait_ge(s["max"], 12 * p + 12)
                after(dve, s["mT_ps"], p)
                v.link(V.tensor_tensor(mx[:, 1, :], mx[:, 1, :], mx[:, 2, :], ALU.max))
                V.tensor_scalar(nm[:, :, :], mx[:, 0:2, :], -1.0, None, ALU.mult).then_inc(s["neg"], 1)

            def second_max(tn):
                p = tn.unit(3)
                dve.wait_ge(s["m1"], p + 1)
                V.tensor_tensor(mT[:, 1, :], pT[0:H, 0:SEQ_LEN], mT[:, 0, :], ALU.subtract).then_inc(s["m2"], 1)

            def load(tn, piece):
                p, u = tn.unit(0), tn.ring(0)
                x = X[:, cols(2 * p, S2), :]
                if piece == 0:
                    after(dve, s_a0[u], 32 * tn.lap(0) + 32)
                    v.note(V.tensor_tensor(a0[u][:, :, :], a0[u][:, :, :],
                                           bc_last(c["gates"][:, 0, cols(2 * p, S2)], D), ALU.mult))
                elif piece == 1:
                    v.settle()
                    v.note(V.tensor_tensor(a0[u][:, :, :], a0[u][:, :, :],
                                           gbc[u][:, :].unsqueeze(1).broadcast_to([P, S2, D]), ALU.mult))
                else:
                    v.settle()
                    v.note(V.tensor_tensor(x, x, a0[u][:, :, :], ALU.add))

            def load_moments(tn, piece):
                p, u = tn.unit(0), tn.ring(0)
                v.settle()
                if piece == 0:
                    for n in range(S2):
                        last = V.bn_stats(stats[:, n, :], tile_at(X, 2 * p + n))
                    v.note(last)
                else:
                    for n in range(S2):
                        last = V.bn_aggr(mv0[u][:, n, :], stats[:, n, :])
                    last.then_inc(s["mv0"], 1)

            def norm_input(tn):
                p, u = tn.unit(0), tn.ring(0)
                after(dve, s["hT_ps"], p)
                dve.wait_ge(s["rstd0"], p + 1)
                normalize(V, lambda n: tile_at(X, 2 * p + n), lambda n: xhat[:, n, :], mv0[u], rstd0[u], S2)\
                    .then_inc(s["xhat"], 1)

            def split(tn):
                p, u = tn.unit(1), tn.ring(1)
                dve.wait_ge(s["part1"], p + 1)
                V.tensor_tensor(rest[:, :], pP[:, :], parts[u][:, 0, :], ALU.subtract).then_inc(s["rest1"], 1)

            def third_part(tn):
                p, u = tn.unit(1), tn.ring(1)
                dve.wait_ge(s["part2"], p + 1)
                V.tensor_tensor(parts[u][:, 2, :], rest[:, :], parts[u][:, 1, :], ALU.subtract)\
                    .then_inc(s["parts"], 1)

            def values(tn):
                p, u = tn.unit(1), tn.ring(1)
                dve.wait_ge(s["v_ps"], p + 1)
                after(dve, s["pv"], 4 * (p - 2))
                V.tensor_copy(vv[u][:, :, :, 0:HD1],
                              pP[:, 0:SEQ_LEN].rearrange("p (n h d) -> p n h d", n=S2, d=HD1)).then_inc(s["v"], 1)

            def denominators(tn, n):
                dve.wait_ge(s["yT_ps"], 2 * tn.unit(5) + n + 1)
                v.note(V.reciprocal(rden[:, n, :], pP[:, :].rearrange("p (h l) -> p h l", l=LAT)[:, :, HD1]))

            def tokens(tn, n):
                v.settle()
                y = pP[:, :].rearrange("p (h l) -> p h l", l=LAT)
                V.tensor_tensor(yv[:, n, :, :], y[:, :, 0:HD1], bc_last(rden[:, n, :], HD1), ALU.mult)\
                    .then_inc(s["yT"], 1)

            def output(tn, piece):
                p, u = tn.unit(5), tn.ring(5)
                x = X[:, cols(2 * p, S2), :]
                if piece == 0:
                    after(dve, s_mod[u], 16 * tn.lap(5) + 16)
                    dve.wait_ge(s["yT"], 2 * p + 2)
                    v.note(V.tensor_tensor(yv[:, :, :, :].rearrange("p n h d -> p n (h d)"),
                                           yv[:, :, :, :].rearrange("p n h d -> p n (h d)"),
                                           modbc[u][:, 0, :].unsqueeze(1).broadcast_to([P, S2, D]), ALU.mult))
                else:
                    v.settle()
                    v.note(V.tensor_tensor(x, x, yv[:, :, :, :].rearrange("p n h d -> p n (h d)"), ALU.add))

            def output_moments(tn, piece):
                p, u = tn.unit(5), tn.ring(5)
                v.settle()
                if piece == 0:
                    for n in range(S2):
                        last = V.bn_stats(stats[:, n, :], tile_at(X, 2 * p + n))
                    v.note(last)
                else:
                    for n in range(S2):
                        last = V.bn_aggr(mv1[u][:, n, :], stats[:, n, :])
                    last.then_inc(s["mv1"], 1)

            def router_input(tn, piece):
                p, u = tn.unit(6), tn.ring(6)
                if piece == 0:
                    dve.wait_ge(s["rstd1"], p + 1)
                    v.note(normalize(V, lambda n: tile_at(X, 2 * p + n), lambda n: res[:, n, :], mv1[u], rstd1[u],
                                     S2))
                elif piece == 1:
                    after(dve, s_mod[u], 16 * tn.lap(6) + 16)
                    v.settle()
                    v.note(V.tensor_tensor(res[:, :, :], res[:, :, :],
                                           modbc[u][:, 2, :].unsqueeze(1).broadcast_to([P, S2, D]), ALU.mult))
                else:
                    after(dve, s_scat[u], 64 * tn.lap(6))
                    v.settle()
                    for k in range(2):
                        last = V.tensor_tensor(rows[u][:, k, :, 0:D], res[:, :, :],
                                               modbc[u][:, 1, :].unsqueeze(1).broadcast_to([P, S2, D]), ALU.add)
                    last.then_inc(s["h2"], 1)
                    for k in range(2):
                        last = V.tensor_scalar(rows[u][:, k, :, D], c["token_id"][:, cols(2 * p, S2)],
                                               float(k * TOKENS), None, ALU.add)
                    v.note(last)

            def read_logits(tn):
                dve.wait_ge(s["lg_ps"], tn.unit(6) + 1)
                V.tensor_copy(logits[:, :, :], p_lg).then_inc(s["lg_read"], 1)

            def choose(tn):
                p = tn.unit(6)
                dve.wait_ge(s["lg_read"], p + 1)
                after(dve, s["slot"], p)
                dve.wait_ge(s["zeroed"], 1)
                dve.nop(nofuse=True)
                v.link(route(V, v, c, logits, r, S2, 1))
                V.tensor_tensor(both[:, :, :], r["pick"][:, 0, :, :], r["pick"][:, 1, :, :], ALU.add)\
                    .then_inc(s["pick"], 1)
                v.note(V.tensor_copy(top2[:, cols(2 * p, S2), :], r["top"][:, :, 0:2]))

            def step(tn):
                v.restart()
                for lag, stage, *rest_ in (
                        (3, maxima, 0), (5, denominators, 0), (3, maxima, 1), (5, tokens, 0), (3, maxima, 2),
                        (5, denominators, 1), (6, router_input, 0), (5, tokens, 1), (3, maxima, 3),
                        (6, router_input, 1), (3, maxima, 4), (6, router_input, 2), (3, maxima, 5), (5, output, 0),
                        (3, maxima, 6), (5, output, 1), (3, maxima, 7), (5, output_moments, 0), (0, load, 0),
                        (5, output_moments, 1), (3, maxima, 8), (0, load, 1), (6, read_logits), (0, load, 2),
                        (3, maxima, 9), (0, load_moments, 0), (1, split), (0, load_moments, 1), (3, maxima, 10),
                        (3, maxima, 11), (3, negate), (0, norm_input), (1, third_part), (3, second_max), (1, values),
                        (6, choose)):
                    if tn.has(lag, SEQS):
                        stage(tn, *rest_)
                v.restart()

            turns(dve, 3, step, SEQS + 5, 9, SEQS)
            v.link(V.tensor_copy(gexp[:, :], top2[:, :, 1]))
            v.announce(V.tensor_tensor(gexp[:, :], gexp[:, :], top2[:, :, 0], ALU.subtract), s["gexp"], 1)
            dve.wait_ge(s["gexp"], 2)
            v.link(V.tensor_scalar(c["gates"][:, 0, :], gexp[:, :], 1.0, None, ALU.add))
            v.link(V.reciprocal(c["gates"][:, 0, :], c["gates"][:, 0, :]))
            v.link(V.tensor_tensor(c["gates"][:, 1, :], gexp[:, :], c["gates"][:, 0, :], ALU.mult))


def finish(nc, c, out, sb, sem):
    V = nc.vector
    S2 = SEQ_LEN // P
    a = [sb(f"fin{u}", [P, 2, S2, D]) for u in range(2)]
    gbc = [sb(f"gate1_bc{u}", [P, D]) for u in range(2)]
    s_in = [sem(f"f_in{u}") for u in range(2)]
    s_done, s_v = sem("f_done"), sem("f_dve")
    s_out = sem("f_out")
    X = c["X"]

    with nc.Block() as block:
        @block.sync
        def _(sp):
            def load(p, u):
                after(sp, s_done, p - 1)
                for k in range(2):
                    sp.dma_start(a[u][:, k, :, :], c["answers"][1][cols(2 * P * p + k * TOKENS, 2 * P), :]
                                 .rearrange("(n p) d -> p n d", p=P)).then_inc(s_in[u], 16)
                m = c["mod_dram"][1].rearrange("s (m d) -> s m d", d=D)[cols(p, 1), 5:6, :]
                sp.dma_start(gbc[u][:, :], m.rearrange("s m d -> (s m d)").partition_broadcast(P))\
                    .then_inc(s_in[u], 16)

            pipeline(sp, lambda k, h, static: load(k, h), 0, SEQS - 1, 2, SEQS)

        @block.scalar
        def _(act):
            def store(p, u):
                after(act, s_done, p + 1)
                act.dma_start(out[cols(p, 1), :, :].rearrange("s (n p) d -> p (s n) d", p=P),
                              X[:, cols(2 * p, S2), :]).then_inc(s_out, 16)

            pipeline(act, lambda k, h, static: store(k, h), 0, SEQS - 1, 2, SEQS)
            act.wait_ge(s_out, 16 * SEQS)

        @block.vector
        def _(dve):
            v = Chain(dve, s_v)

            def add(p, u):
                v.restart()
                after(dve, s_in[u], 24 * p + (48 - 24 * u))
                for k in range(2):
                    last = V.tensor_tensor(a[u][:, k, :, :], a[u][:, k, :, :],
                                           bc_last(c["gates"][:, k, cols(2 * p, S2)], D), ALU.mult)
                v.link(last)
                v.link(V.tensor_tensor(a[u][:, 0, :, :], a[u][:, 0, :, :], a[u][:, 1, :, :], ALU.add))
                v.link(V.tensor_tensor(a[u][:, 0, :, :], a[u][:, 0, :, :],
                                       gbc[u][:, :].unsqueeze(1).broadcast_to([P, S2, D]), ALU.mult))
                x = X[:, cols(2 * p, S2), :]
                V.tensor_tensor(x, x, a[u][:, 0, :, :], ALU.add).then_inc(s_done, 1)

            pipeline(dve, lambda k, h, static: add(k, h), 0, SEQS - 1, 2, SEQS)


def load_expert_weights(sp, t, c, layer):
    pre = f"L{layer}_ffn_"
    first = t[pre + ("W1" if layer == 0 else "w1")].rearrange("p e f -> p (e f)")
    second = t[pre + ("W2" if layer == 0 else "w2")].rearrange("p e b d -> p (e b d)")
    w = E * FF // WEIGHT_PARTS
    for dst, src in ((c["W1"], first), (c["W2"], second)):
        for q in range(WEIGHT_PARTS):
            sp.dma_start(dst[:, q * w:q * w + w], src[:, q * w:q * w + w]).then_inc(c["s_w"][layer], 16)
    sp.dma_start(c["b1"][:, :], t[pre + "b1"]).then_inc(c["s_w"][layer], 16)
    sp.dma_start(c["b2"][:, :], t[pre + "b2"].partition_broadcast(P)).then_inc(c["s_w"][layer], 16)


def experts(nc, c, sb, ps, sem, layer):
    V, A, T = nc.vector, nc.scalar, nc.tensor
    n_tiles = expert_tiles(layer)
    dump = (layer + 1) * TOKENS
    W1, W2, b1, b2, s_w = c["W1"], c["W2"], c["b1"], c["b2"], c["s_w"][layer]
    RINGS = 4
    w1 = [sb(f"w1_{u}", [P, FF]) for u in range(2)]
    xg = [sb(f"xg{u}", [P, ROW]) for u in range(RINGS)]
    xgT = [sb(f"xgT{u}", [P, P]) for u in range(2)]
    hid = [sb(f"hid{u}", [P, FB, P]) for u in range(2)]
    y = [sb(f"y{u}", [P, D]) for u in range(RINGS)]
    dest = [sb(f"dest{u}", [P, 1], I32) for u in range(RINGS)]
    padding = [sb(f"padding{u}", [P, 1]) for u in range(2)]
    nti, ntf = sb("nt_i", [P, E], I32), sb("nt_f", [P, E])
    ends = sb("ends", [P, E])
    onesE = sb("ones_e", [P, E])
    jt = sb("tile_no", [P, n_tiles])
    ge = sb("past", [P, n_tiles, E - 1])
    tmp = sb("plan_tmp", [P, n_tiles, E])
    ej, sj, nj, rj = (sb(f"plan_{n}", [P, n_tiles]) for n in ("expert", "start", "rows", "row"))
    expert_i, row_i = sb("plan_expert_i", [P, n_tiles], I32), sb("plan_row_i", [P, n_tiles], I32)
    pad_f, pad_i = sb("pad_f", [P, E]), sb("pad_i", [P, E], I32)
    pT = [ps(f"gT{u}", [P, 512])[:, 0:P] for u in range(2)]
    pH = [ps(f"gH{u}", [P, FB, P]) for u in range(2)]
    pY = [ps(f"gY{u}", [P, 512])[:, 0:D] for u in range(2)]

    n = "experts_"
    s_iota, s_pads, s_plan, s_pad = sem(n + "iota"), sem(n + "pads"), sem(n + "plan"), sem(n + "pad")
    s_xg = [sem(n + f"xg{u}") for u in range(RINGS)]
    s_xT, s_xgT, s_w1, s_h = sem(n + "xT"), sem(n + "xgT"), sem(n + "w1"), sem(n + "h")
    s_hid, s_yps, s_y, s_dest = sem(n + "hid"), sem(n + "yps"), sem(n + "y"), sem(n + "dest")
    s_out = [sem(f"experts{layer}_out{u}", kept=True) for u in range(RINGS)]
    s_v, s_padding = sem(n + "dve"), sem(n + "padding")

    def plan_value(engine, src, j, most):
        return engine.value_load(src[0:1, cols(j, 1)], min_val=0, max_val=most)

    def pad(engine, e):
        at = plan_value(engine, pad_i, e, E * REGION - P)
        engine.dma_start(c["routed"][layer][bass.ds(at, P), :], c["pad_rows"][:, :]).then_inc(s_pad, 16)

    with nc.Block() as block:
        @block.sync
        def _(sp):
            sp.wait_ge(s_pads, 1)
            for e in range(0, E, 2):
                pad(sp, e)
            sp.wait_ge(s_plan, 1)
            sp.wait_ge(s_pad, 16 * E)

            def load(tn):
                j, u = tn.unit(0), tn.ring(0)
                after(sp, s_xT, j - 3)
                after(sp, s_dest, j - 3)
                at = plan_value(sp, row_i, j, E * REGION - P)
                sp.dma_start(xg[u][:, :], c["routed"][layer][bass.ds(at, P), :]).then_inc(s_xg[u], 16)

            turns(sp, RINGS, load, n_tiles - 1, RINGS, n_tiles)

        @block.gpsimd
        def _(pool):
            nc.gpsimd.iota(c["pad_rows"][:, D:D + 1], pattern=[[0, 1]], base=dump, channel_multiplier=1,
                           allow_small_or_imprecise_dtypes=True).then_inc(s_iota, 1)
            nc.gpsimd.iota(jt[:, :], pattern=[[1, n_tiles]], base=0, channel_multiplier=0,
                           allow_small_or_imprecise_dtypes=True).then_inc(s_iota, 1)

            def scatter(tn):
                j, u = tn.unit(0), tn.ring(0)
                after_then(pool, s_y, j + 1, s_plan)
                pool.indirect_dma_start(c["answers"][layer], bass.IndirectOffsetOnAxis(ap=dest[u][:, :], axis=0),
                                        y[u][:, :], None).then_inc(s_out[u], 16)

            turns(pool, RINGS, scatter, n_tiles - 1, RINGS, n_tiles)
            for u in range(RINGS):
                pool.wait_ge(s_out[u], 16 * len(range(u, n_tiles, RINGS)))

        @block.scalar
        def _(act):
            act.wait_ge(s_pads, 1)
            for e in range(1, E, 2):
                pad(act, e)
            act.wait_ge(s_plan, 1)
            act.wait_ge(s_w, WEIGHT_LOADS)

            def hidden(tn):
                j, u = tn.unit(0), tn.ring(0) % 2
                block0 = plan_value(act, expert_i, j, E - 1) * FB
                after(act, s_h, j + 1)
                after(act, s_yps, j - 1)
                for b in range(FB):
                    last = A.activation(hid[u][:, b, :], pH[u][:, b, :], ACT.Relu if layer == 0 else ACT.Gelu,
                                        bias=b1[:, bass.ds(block0 + b, 1)])
                last.then_inc(s_hid, 1)

            turns(act, RINGS, hidden, n_tiles - 1, RINGS, n_tiles)

        @block.tensor
        def _(pe):
            pe.wait_ge(s_plan, 1)
            pe.wait_ge(s_w, WEIGHT_LOADS)

            def turn(tn):
                j, u = tn.unit(0), tn.ring(0)
                after(pe, s_xg[u], 16 * tn.lap(0) + 16)
                after(pe, s_xgT, j - 1)
                T.transpose(pT[u % 2][:, :], xg[u][:, 0:D], c["ident"][:, :]).then_inc(s_xT, 1)

            def up(tn):
                j, u = tn.unit(1), tn.ring(1) % 2
                after(pe, s_xgT, j + 1)
                after(pe, s_w1, j + 1)
                after(pe, s_hid, j - 1)
                for b in range(FB):
                    last = T.matmul(pH[u][:, b, :], w1[u][:, b * P:b * P + P], xgT[u][:, :], start=True, stop=True)
                last.then_inc(s_h, 1)

            def down(tn):
                j, u = tn.unit(2), tn.ring(2) % 2
                at = plan_value(pe, expert_i, j, E - 1) * FF
                after(pe, s_hid, j + 1)
                after(pe, s_y, j - 1)
                for b in range(FB):
                    last = T.matmul(pY[u][:, :], hid[u][:, b, :], W2[:, bass.ds(at + b * D, D)],
                                    start=(b == 0), stop=(b == FB - 1))
                last.then_inc(s_yps, 1)

            def step(tn):
                for lag, stage in ((0, turn), (1, up), (2, down)):
                    if tn.has(lag, n_tiles):
                        stage(tn)

            turns(pe, RINGS, step, n_tiles + 1, RINGS, n_tiles)

        @block.vector
        def _(dve):
            v = Chain(dve, s_v)
            counts = c["counts"]
            v.link(V.tensor_tensor(pad_f[:, :], counts[:, :], c["region0"][:, :], ALU.add))
            dve.wait_ge(s_iota, 1)
            V.tensor_copy(pad_i[:, :], pad_f[:, :]).then_inc(s_pads, 1)
            v.link(V.memset(onesE[:, :], 1.0))
            v.link(V.tensor_scalar(nti[:, :], counts[:, :], float(P - 1), None, ALU.add))
            v.link(V.tensor_scalar(nti[:, :], nti[:, :], 7, None, ALU.arith_shift_right))
            v.link(V.tensor_copy(ntf[:, :], nti[:, :]))
            v.link(V.tensor_tensor_scan(ends[:, :], onesE[:, :], ntf[:, :], 0.0, ALU.mult, ALU.add))
            dve.wait_ge(s_iota, 2)
            v.link(V.tensor_tensor(ge[:, :, :], bc_last(jt[:, :], E - 1),
                                   ends[:, 0:E - 1].unsqueeze(1).broadcast_to([P, n_tiles, E - 1]), ALU.is_ge))
            v.link(V.tensor_reduce(ej[:, :], ge[:, :, :], AX.X, ALU.add))
            V.tensor_copy(expert_i[:, :], ej[:, :])
            v.link(V.tensor_tensor(ge[:, :, :], ge[:, :, :],
                                   ntf[:, 0:E - 1].unsqueeze(1).broadcast_to([P, n_tiles, E - 1]), ALU.mult))
            V.tensor_reduce(sj[:, :], ge[:, :, :], AX.X, ALU.add)
            v.link(V.tensor_tensor(tmp[:, :, :], c["iota8"][:, :].unsqueeze(1).broadcast_to([P, n_tiles, E]),
                                   bc_last(ej[:, :], E), ALU.is_equal))
            v.link(V.tensor_tensor(tmp[:, :, :], tmp[:, :, :],
                                   counts[:, :].unsqueeze(1).broadcast_to([P, n_tiles, E]), ALU.mult))
            V.tensor_reduce(nj[:, :], tmp[:, :, :], AX.X, ALU.add)
            v.link(V.tensor_tensor(rj[:, :], jt[:, :], sj[:, :], ALU.subtract))
            v.link(V.scalar_tensor_tensor(rj[:, :], rj[:, :], float(P), nj[:, :], ALU.mult, ALU.min))
            v.link(V.scalar_tensor_tensor(rj[:, :], ej[:, :], float(REGION), rj[:, :], ALU.mult, ALU.add))
            V.tensor_copy(row_i[:, :], rj[:, :]).then_inc(s_plan, 1)
            dve.wait_ge(s_plan, 1)
            dve.wait_ge(s_w, WEIGHT_LOADS)

            def prepare(tn):
                j, u = tn.unit(0), tn.ring(0)
                at = plan_value(dve, expert_i, j, E - 1) * FF
                after(dve, s_h, j - 1)
                V.tensor_copy(w1[u % 2][:, :], W1[:, bass.ds(at, FF)]).then_inc(s_w1, 1)
                dve.wait_ge(s_xT, j + 1)
                V.tensor_copy(xgT[u % 2][:, :], pT[u % 2][:, :]).then_inc(s_xgT, 1)
                V.tensor_scalar(padding[u % 2][:, :], xg[u][:, D:D + 1], float(dump), jt[:, cols(j, 1)], ALU.is_ge,
                                ALU.mult).then_inc(s_padding, 1)
                dve.wait_ge(s_padding, j + 1)
                after(dve, s_out[u], 16 * tn.lap(0))
                V.scalar_tensor_tensor(dest[u][:, :], padding[u % 2][:, :], float(P), xg[u][:, D:D + 1], ALU.mult,
                                       ALU.add).then_inc(s_dest, 1)

            def result(tn):
                j, u = tn.unit(2), tn.ring(2)
                at = plan_value(dve, expert_i, j, E - 1) * D
                dve.wait_ge(s_yps, j + 1)
                V.tensor_tensor(y[u][:, :], pY[u % 2][:, :], b2[:, bass.ds(at, D)], ALU.add).then_inc(s_y, 1)

            def step(tn):
                for lag, stage in ((0, prepare), (2, result)):
                    if tn.has(lag, n_tiles):
                        stage(tn)

            turns(dve, RINGS, step, n_tiles + 1, RINGS, n_tiles)


def kernel(**inputs):
    import numpy as np
    import concourse.bacc as bacc
    from concourse.bass_utils import run_bass_kernel_spmd

    nc = bacc.Bacc("TRN2", target_bir_lowering=False, num_devices=1)
    arrays, t = {}, {}
    b_in = np.asarray(inputs.pop("L0_attn_b_in"))
    inputs["b_in_ch"], inputs["b_in_dt"] = b_in[:6 * P], b_in[6 * P:]
    inputs["conv_rows"] = inputs["L0_attn_conv_w"]
    for name, a in inputs.items():
        a = np.asarray(a)
        if name in ("L0_c", "L1_c", "L0_attn_W_in", "L0_attn_W_out", "L1_attn_W_uq", "L1_attn_W_o", "L1_ffn_router_w"):
            a = a.T
        elif name in ("L0_ffn_W1",):
            a = a.transpose(1, 0, 2)
        elif name == "L1_ffn_w1":
            a = a.transpose(2, 0, 1)
        elif name == "L0_ffn_W2":
            a = a.reshape(E, FB, P, D).transpose(2, 0, 1, 3)
        elif name == "L1_ffn_w2":
            a = a.transpose(0, 2, 1).reshape(E, FB, P, D).transpose(2, 0, 1, 3)
        elif name in ("L0_ffn_b1", "L1_ffn_b1"):
            a = a.reshape(E * FB, P).T
        elif name in ("L0_ffn_b2", "L1_ffn_b2"):
            a = a.reshape(1, E * D)
        elif name == "L0_attn_conv_w":
            a = a.reshape(4, P, 4).transpose(1, 0, 2)
        elif name == "conv_rows":
            a = a.T.reshape(1, 4 * 4 * P)
        elif name in ("L0_attn_conv_b", "L0_attn_norm_w", "b_in_ch"):
            a = a.reshape(-1, P).T
        elif a.ndim == 1:
            a = a[None, :]
        a = np.ascontiguousarray(a)
        arrays[f"in_{name}"] = a
        t[name] = nc.dram_tensor(f"in_{name}", a.shape, mybir.dt.from_np(a.dtype), kind="ExternalInput").ap()
    out = nc.dram_tensor("out_0", (SEQS, SEQ_LEN, D), F32, kind="ExternalOutput").ap()
    build(nc, t, out)
    return run_bass_kernel_spmd(nc, [arrays], core_ids=[0]).results[0]["out_0"]
```

```python
from contextlib import ExitStack

import concourse.bass as bass
from concourse import mybir

F32 = mybir.dt.float32
BF16 = mybir.dt.bfloat16
I32 = mybir.dt.int32
U32 = mybir.dt.uint32
ALU = mybir.AluOpType
ACT = mybir.ActivationFunctionType
AX = mybir.AxisListType

P = 128
SEQS = 16
SEQ_LEN = 256
D = 128
TILES = SEQS * SEQ_LEN // P
TOKENS = TILES * P
PAIRS = SEQS // 2
PT = TILES // PAIRS
PW = PT * P
E = 8
FF = 512
FB = FF // P
DSSM = 256
HEADS0 = 4
HD0 = 64
HEADS1 = 16
HD1 = 8
LAT = 32
EPS_LN = 1e-5
EPS_RMS = 1e-12
ROW = 132
REGION = TOKENS + P
XPAD = SEQ_LEN + 3
SHIFT, SCALE, GATE = 0, 1, 2
MASKED = -1.0e30
WEIGHT_PARTS = 4
BY_CHANNEL = {"c": 2 * SEQS, "b_in_ch": 6, "L0_attn_conv_w": 16, "L0_attn_conv_b": 4, "L0_attn_norm_w": 2,
              "L0_attn_D": 2, "L0_ffn_Wr": E, "L1_ffn_router_w": E, "L1_attn_W_uk": LAT, "L1_attn_W_uv": LAT,
              "L1_attn_W_o": D}
AS_ROW = {"b_in_dt": HEADS0, "L0_attn_dt_bias": HEADS0, "L0_attn_A_log": HEADS0, "L0_attn_b_out": D,
          "L0_ffn_ln_g": D, "L0_ffn_ln_b": D, "L0_ffn_br": E}
WEIGHT_LOADS = 16 * (2 * WEIGHT_PARTS + 2)


def after(engine, sem, value):
    if isinstance(value, int) and value <= 0:
        return
    engine.wait_ge(sem, value)


def after_then(engine, sem, value, passed):
    after(engine, sem, value)
    engine.wait_ge(passed, 1)
    engine.nop(nofuse=True)


class Chain:

    def __init__(self, engine, sem):
        self.engine, self.sem, self.n = engine, sem, 0

    def restart(self):
        if self.n:
            self.engine.wait_ge(self.sem, self.n)
            self.engine.nop(nofuse=True)
            self.engine.sem_clear(self.sem)
            self.n = 0

    def link(self, instruction):
        self.n += 1
        instruction.then_inc(self.sem, 1)
        self.engine.wait_ge(self.sem, self.n)

    def note(self, instruction):
        self.n += 1
        instruction.then_inc(self.sem, 1)

    def settle(self):
        self.engine.wait_ge(self.sem, self.n)

    def announce(self, instruction, sem, value):
        instruction.then_inc(sem, 1)
        self.engine.wait_ge(sem, value)


def bc_last(ap, n):
    return ap.unsqueeze(2).broadcast_to([ap.shape[0], ap.shape[1], n])


def expert_tiles(layer):
    return ((layer + 1) * TOKENS + E * (P - 1)) // P


def build(nc, t, out):
    top = ExitStack()
    with top:
        def sb_in(ctx, phase=""):
            return lambda name, shape, dt=F32: ctx.enter_context(nc.sbuf_tensor(phase + name, shape, dt))

        def ps_in(ctx, phase=""):
            return lambda name, shape, dt=F32: ctx.enter_context(nc.psum_tensor(phase + name, shape, dt))

        def sem(name):
            return top.enter_context(nc.semaphore(name))

        def phase_semaphores(ctx, of_phase):
            def phase_sem(name, kept=False):
                if kept:
                    return sem(name)
                of_phase.append(ctx.enter_context(nc.semaphore(name)))
                return of_phase[-1]
            return phase_sem

        def clear(of_phase):
            with nc.Block() as block:
                @block.sync
                def _(sp):
                    for used in of_phase:
                        sp.sem_clear(used)

        sb = sb_in(top)
        c = {}
        c["X"] = sb("X", [P, TILES, D])
        c["ident"] = sb("ident", [P, P])
        c["identb"] = sb("identb", [P, P], BF16)
        c["upto"] = sb("upto", [P, P])
        c["beyond"] = sb("beyond", [P, P])
        c["before"] = sb("before", [P, P])
        c["ones"] = sb("ones", [P, P])
        c["minus_half"] = sb("minus_half", [P, TILES])
        c["mv0"], c["rstd0"] = sb("mv0", [P, TILES, 2]), sb("rstd0", [P, TILES])
        c["iota8"] = sb("iota8", [P, E])
        c["region0"] = sb("region0", [P, E])
        c["token_id"] = sb("token_id", [P, TILES])
        c["gates"] = sb("gates", [P, 2, TILES])
        c["counts"] = sb("counts", [P, E])
        c["modT"] = [sb(f"modT{l}", [P, 3, SEQS]) for l in range(2)]
        c["pad_rows"] = sb("pad_rows", [P, ROW])
        c["W1"] = sb("W1", [P, E * FF])
        c["W2"] = sb("W2", [P, E * FB * D])
        c["b1"] = sb("b1", [P, E * FB])
        c["b2"] = sb("b2", [P, E * D])
        c["s_w"] = [sem(f"expert_weights{l}") for l in range(2)]
        c["mod_dram"] = [nc.dram_tensor(f"mod_rows{l}", (SEQS, 6 * D), F32).ap() for l in range(2)]
        c["routed"] = [nc.dram_tensor(f"routed{l}", (E * REGION, ROW), F32).ap() for l in range(2)]
        c["answers"] = [nc.dram_tensor(f"answers{l}", ((l + 1) * TOKENS + expert_tiles(l) * P, D), F32).ap()
                        for l in range(2)]
        c["parts_dram"] = nc.dram_tensor("qk_parts_dram", (3, P, 3, 2 * SEQ_LEN), BF16).ap()
        w = {}
        setup(nc, t, c, w, sb, sem)
        phases = (lambda sb, ps, sem: mamba(nc, t, c, w, sb, ps, sem),
                  lambda sb, ps, sem: experts(nc, c, sb, ps, sem, 0),
                  lambda sb, ps, sem: attention(nc, t, c, w, sb, ps, sem),
                  lambda sb, ps, sem: experts(nc, c, sb, ps, sem, 1),
                  lambda sb, ps, sem: finish(nc, c, out, sb, sem))
        for i, phase in enumerate(phases):
            with ExitStack() as ctx:
                of_phase = []
                phase(sb_in(ctx, f"{i}_"), ps_in(ctx, f"{i}_"), phase_semaphores(ctx, of_phase))
                if i < len(phases) - 1:
                    clear(of_phase)


def setup(nc, t, c, w, sb, sem):
    s_x = [sem(f"s_x{q}") for q in range(4)]
    s_moments, s_root, s_rows = sem("s_moments"), sem("s_root"), sem("s_rows")
    s_small = sem("s_small")
    s_mod = sem("s_mod")
    s_modw = sem("s_modw")
    s_memset = sem("s_memset")
    s_masks = sem("s_masks")
    s_tanh = sem("s_tanh")
    s_silu = sem("s_silu")
    s_modps = sem("s_modps")
    s_v = sem("s_setup_chain")
    s_wps = sem("s_wps")
    s_wcp = sem("s_wcp")
    w["WinT"] = sb("WinT", [P, 772])
    w["WoT"] = sb("WoT", [P, 2, D])
    by_channel = sb("by_channel", [P, sum(BY_CHANNEL.values())])
    as_row = sb("as_row", [P, sum(AS_ROW.values())])

    def part(packed, widths, name):
        at = list(widths).index(name)
        first = sum(list(widths.values())[:at])
        return packed[:, first:first + widths[name]]

    w["bin_ch"] = part(by_channel, BY_CHANNEL, "b_in_ch")
    w["conv_w"] = part(by_channel, BY_CHANNEL, "L0_attn_conv_w").rearrange("p (b k) -> p b k", k=4)
    w["conv_b"] = part(by_channel, BY_CHANNEL, "L0_attn_conv_b")
    w["norm_ch"] = part(by_channel, BY_CHANNEL, "L0_attn_norm_w")
    w["D_ch"] = part(by_channel, BY_CHANNEL, "L0_attn_D")
    w["Wr"] = [part(by_channel, BY_CHANNEL, n) for n in ("L0_ffn_Wr", "L1_ffn_router_w")]
    w["heads_bc"] = as_row[:, 0:3 * HEADS0].rearrange("p (k h) -> p k h", k=3)
    w["bout_bc"] = part(as_row, AS_ROW, "L0_attn_b_out")
    w["ln_g"], w["ln_b"] = part(as_row, AS_ROW, "L0_ffn_ln_g"), part(as_row, AS_ROW, "L0_ffn_ln_b")
    w["br_bc"] = part(as_row, AS_ROW, "L0_ffn_br")
    w["taps"] = sb("taps", [P, 4, 4 * P])
    w["conv_bias"] = sb("conv_bias", [P, 4])
    w["edge"] = sb("edge", [P, 4, 2, 3])
    w["dt_bias"] = sb("dt_bias", [P, HEADS0])
    w["A"] = sb("A", [P, HEADS0])
    w["Wqkv"] = sb("Wqkv", [P, 3, D])
    with ExitStack() as ctx:
        sbx, psx = (lambda n, s, dt=F32: ctx.enter_context(nc.sbuf_tensor(n, s, dt))), \
                   (lambda n, s, dt=F32: ctx.enter_context(nc.psum_tensor(n, s, dt)))
        cT = part(by_channel, BY_CHANNEL, "c").rearrange("p (l s) -> p l s", l=2)
        th = sbx("th", [P, 2, SEQS])
        wmod = sbx("wmod", [P, 2, 6 * D])
        rows = sbx("mod_rows", [SEQS, 2, 6 * D])
        tmp = sbx("mod_tmp", [SEQS, 2, 2, D])
        sg = sbx("mod_sign", [SEQS, 2, 2, D])
        conv_rows = sbx("conv_rows", [P, 4, 4 * P])
        tap_sum = sbx("tap_sum", [P, 4, 4])
        stats = sbx("x_stats", [P, TILES, 6])
        var_eps = sbx("var_eps", [P, TILES])
        low_rank = sbx("low_rank", [LAT, 3, D])
        wdq, wuqT, wdkv = (low_rank[:, i, :] for i in range(3))
        wuk, wuv, woT = (part(by_channel, BY_CHANNEL, "L1_attn_" + n) for n in ("W_uk", "W_uv", "W_o"))
        wqT = sbx("wqT", [P, D])
        keT = sbx("keT", [LAT, D])
        ve = sbx("ve", [LAT, D])
        mps = psx("mod_ps", [P, 2, 6, SEQS])
        rps = psx("row_ps", [P, 2, 2, 512])
        wps = psx("w_ps", [P, 3, D])
        wps2 = psx("w_ps2", [P, 3, D])
        block = ctx.enter_context(nc.Block())
        small = [
            (by_channel[:, :], t["by_channel"]), (as_row[:, :], t["as_row"].partition_broadcast(P)),
            (wmod[:, 0, :], t["L0_wmod"]), (wmod[:, 1, :], t["L1_wmod"]),
            (w["WinT"][:, :], t["L0_attn_W_in"]), (conv_rows[:, :, :], t["conv_rows"].partition_broadcast(P)),
            (w["WoT"][:, :, :], t["L0_attn_W_out"].rearrange("(b p) d -> p b d", p=P)),
            (low_rank[:, :, :], t["low_rank"]),
        ]

        @block.sync
        def _(sp):
            for dst, src in small:
                sp.dma_start(dst, src).then_inc(s_small, 16)
            sp.wait_ge(s_mod, 1)
            for l in range(2):
                sp.dma_start(c["mod_dram"][l], rows[:, l, :]).then_inc(s_modw, 16)
            sp.wait_ge(s_modw, 32)

        @block.scalar
        def _(act):
            xv = t["L0_attn_u"].rearrange("s (j p) d -> p (s j) d", p=P)
            for q in range(4):
                act.dma_start(c["X"][:, 8 * q:8 * q + 8, :], xv[:, 8 * q:8 * q + 8, :]).then_inc(s_x[q], 16)
            act.wait_ge(s_small, 16 * len(small))
            nc.scalar.activation(th[:, :, :], cT[:, :, :], ACT.Tanh, scale=0.5).then_inc(s_tanh, 1)
            nc.scalar.activation(w["A"][:, :], w["heads_bc"][:, 2, :], ACT.Exp).then_inc(s_tanh, 1)
            act.wait_ge(s_modps, 1)
            for l in range(2):
                nc.scalar.activation(rows[:, l, 0:512], rps[0:SEQS, l, 0, :], ACT.Copy).then_inc(s_rows, 1)
                nc.scalar.activation(rows[:, l, 512:768], rps[0:SEQS, l, 1, 0:256], ACT.Copy).then_inc(s_rows, 1)

        @block.gpsimd
        def _(pool):
            g = nc.gpsimd
            g.memset(c["ones"][:, :], 1.0).then_inc(s_memset, 1)
            for m in ("ident", "upto", "beyond", "before"):
                g.memset(c[m][:, :], 0.0 if m == "ident" else 1.0).then_inc(s_memset, 1)
            g.memset(c["identb"][:, :], 0.0).then_inc(s_memset, 1)
            g.memset(c["pad_rows"][:, :], 0.0).then_inc(s_memset, 1)
            g.memset(c["minus_half"][:, :], -0.5).then_inc(s_masks, 1)
            pool.wait_ge(s_memset, 7)
            for m, op, fill, sign in (("ident", ALU.not_equal, 1.0, 1), ("identb", ALU.not_equal, 1.0, 1),
                                      ("upto", ALU.is_ge, 0.0, -1), ("beyond", ALU.is_gt, 0.0, 1),
                                      ("before", ALU.is_gt, 0.0, -1)):
                g.affine_select(out=c[m][:, :], in_=c[m][:, :], compare_op=op, fill=fill, base=0,
                                pattern=[[-sign, P]], channel_multiplier=sign).then_inc(s_masks, 1)
            g.iota(c["iota8"][:, :], pattern=[[1, E]], base=0, channel_multiplier=0,
                   allow_small_or_imprecise_dtypes=True).then_inc(s_masks, 1)
            g.iota(c["region0"][:, :], pattern=[[REGION, E]], base=0, channel_multiplier=0,
                   allow_small_or_imprecise_dtypes=True).then_inc(s_masks, 1)
            g.iota(c["token_id"][:, :], pattern=[[P, TILES]], base=0, channel_multiplier=1,
                   allow_small_or_imprecise_dtypes=True).then_inc(s_masks, 1)
            pool.wait_ge(s_moments, 1)
            pool.wait_ge(s_masks, 1)
            g.tensor_scalar(var_eps[:, :], c["mv0"][:, :, 1], EPS_LN, None, ALU.add).then_inc(s_root, 1)
            pool.wait_ge(s_root, 1)
            g.tensor_tensor(c["rstd0"][:, :], var_eps[:, :], c["minus_half"][:, :], ALU.pow).then_inc(s_root, 1)

        @block.tensor
        def _(pe):
            pe.wait_ge(s_silu, 1)
            for l in range(2):
                for m in range(3):
                    nc.tensor.matmul(mps[:, l, m, :], wmod[:, l, m * D:(m + 1) * D], cT[:, l, :], start=True, stop=True)
                for h, (a, b) in enumerate(((0, 512), (512, 768))):
                    last = nc.tensor.matmul(rps[0:SEQS, l, h, 0:b - a], cT[:, l, :], wmod[:, l, a:b],
                                            start=True, stop=True)
            last.then_inc(s_modps, 1)
            nc.tensor.matmul(wps[:, 0, :], wdq[:, :], wuqT[:, :], start=True, stop=True)
            nc.tensor.matmul(wps[:, 1, :], wuqT[:, :], wdq[:, :], start=True, stop=True)
            nc.tensor.matmul(wps[0:LAT, 2, :], wuv[:, :], woT[:, :], start=True, stop=True).then_inc(s_wps, 1)
            pe.wait_ge(s_wcp, 3)
            nc.tensor.matmul(wps2[0:LAT, 0, :], wuk[:, :], wqT[:, :], start=True, stop=True).then_inc(s_wps, 1)
            pe.wait_ge(s_wcp, 4)
            nc.tensor.matmul(wps2[:, 1, :], wdkv[:, :], keT[:, :], start=True, stop=True)
            nc.tensor.matmul(wps2[:, 2, :], wdkv[:, :], ve[:, :], start=True, stop=True).then_inc(s_wps, 1)

        @block.vector
        def _(dve):
            v = Chain(dve, s_v)
            V = nc.vector
            for q in range(4):
                dve.wait_ge(s_x[q], 16)
                for n in range(8 * q, 8 * q + 8):
                    last = V.bn_stats(stats[:, n, :], c["X"][:, n, :])
                v.link(last)
            for n in range(TILES):
                last = V.bn_aggr(c["mv0"][:, n, :], stats[:, n, :])
            last.then_inc(s_moments, 1)
            dve.wait_ge(s_tanh, 2)
            v.link(V.tensor_scalar(cT[:, :, :], cT[:, :, :], 0.5, None, ALU.mult))
            V.scalar_tensor_tensor(cT[:, :, :], th[:, :, :], 1.0, cT[:, :, :], ALU.add, ALU.mult).then_inc(s_silu, 1)
            v.link(V.tensor_tensor(w["dt_bias"][:, :], w["heads_bc"][:, 0, :], w["heads_bc"][:, 1, :], ALU.add))
            v.link(V.tensor_scalar(w["A"][:, :], w["A"][:, :], -1.0, None, ALU.mult))
            v.link(V.tensor_copy(tap_sum[:, :, 0], w["conv_w"][:, :, 0]))
            for k in range(1, 4):
                v.link(V.tensor_tensor(tap_sum[:, :, k], tap_sum[:, :, k - 1], w["conv_w"][:, :, k], ALU.add))
            v.link(V.tensor_tensor(tap_sum[:, :, :], tap_sum[:, :, :], bc_last(w["bin_ch"][:, 2:6], 4), ALU.mult))
            v.link(V.tensor_tensor(w["conv_bias"][:, :], tap_sum[:, :, 3], w["conv_b"][:, :], ALU.add))
            for j in range(3):
                v.link(V.tensor_scalar(w["edge"][:, :, :, j], bc_last(tap_sum[:, :, 2 - j], 2), -1.0, None, ALU.mult))
            for k in range(4):
                v.link(V.tensor_tensor(w["taps"][:, k, :], w["WinT"][:, 2 * P:6 * P], conv_rows[:, k, :], ALU.mult))
            for b in range(2):
                v.link(V.tensor_scalar(w["WoT"][:, b, :], w["WoT"][:, b, :], w["norm_ch"][:, b:b + 1], None, ALU.mult))
            dve.wait_ge(s_wps, 1)
            V.tensor_copy(w["Wqkv"][:, 0, :], wps[:, 0, :]).then_inc(s_wcp, 1)
            V.tensor_copy(wqT[:, :], wps[:, 1, :]).then_inc(s_wcp, 1)
            V.tensor_copy(ve[:, :], wps[0:LAT, 2, :]).then_inc(s_wcp, 1)
            dve.wait_ge(s_wps, 2)
            V.tensor_copy(keT[:, :], wps2[0:LAT, 0, :]).then_inc(s_wcp, 1)
            dve.wait_ge(s_wps, 3)
            v.link(V.tensor_copy(w["Wqkv"][:, 1:3, :], wps2[:, 1:3, :]))
            dve.wait_ge(s_modps, 1)
            for l in range(2):
                v.link(V.tensor_copy(c["modT"][l][:, :, :], mps[:, l, 0:3, :]))
                v.link(V.tensor_scalar(c["modT"][l][:, SCALE, :], c["modT"][l][:, SCALE, :], 1.0, None, ALU.add))
            dve.wait_ge(s_rows, 4)
            r6 = rows[:, :, :].rearrange("s l (g m d) -> s l g m d", g=2, d=D)
            gate, scale = r6[:, :, :, GATE, :], r6[:, :, :, SCALE, :]
            v.link(V.scalar_tensor_tensor(tmp[:, :, :, :], gate, -1.0, gate, ALU.mult, ALU.max))
            v.link(V.tensor_scalar(sg[:, :, :, :], gate, 0.0, 2.0, ALU.is_ge, ALU.mult))
            v.link(V.tensor_scalar(tmp[:, :, :, :], tmp[:, :, :, :], 0.25, None, ALU.max))
            v.link(V.scalar_tensor_tensor(gate, sg[:, :, :, :], -1.0, tmp[:, :, :, :], ALU.add, ALU.mult))
            V.tensor_scalar(scale, scale, 1.0, None, ALU.add).then_inc(s_mod, 1)


def moments(V, v, x, stats, mv, tiles):
    for n in range(tiles):
        last = V.bn_stats(stats[:, n, :], x(n))
    v.link(last)
    for n in range(tiles):
        last = V.bn_aggr(mv[:, n, :], stats[:, n, :])
    return last


def normalize(V, x, xhat, mv, rstd, tiles):
    for n in range(tiles):
        last = V.tensor_scalar(xhat(n), x(n), mv[:, n, 0:1], rstd[:, n:n + 1], ALU.subtract, ALU.mult)
    return last


def inverse_root(G, ch, c, out, tmp, x, eps):
    ch.link(G.tensor_scalar(tmp, x, eps, None, ALU.add))
    return G.tensor_tensor(out, tmp, c["minus_half"][:, 0:tmp.shape[-1]], ALU.pow)


def tile_at(x, n):
    return x[:, n, :] if isinstance(n, int) else x[:, bass.ds(n, 1), :].rearrange("p o d -> p (o d)")


def cols(n, size):
    return slice(n, n + size) if isinstance(n, int) else bass.ds(n, size)


def route(V, v, c, logits, r, tiles, layer):
    top, idx, idxf, pick = r["top"], r["idx"], r["idxf"], r["pick"]
    for n in range(tiles):
        last = V.max(top[:, n, :], logits[:, n, :])
    v.link(last)
    for n in range(tiles):
        last = V.max_index(idx[:, n, :], top[:, n, :], logits[:, n, :])
    v.link(last)
    v.link(V.tensor_copy(idxf[:, :, :], idx[:, :, 0:2]))
    for k in range(layer + 1):
        last = V.tensor_tensor(pick[:, k, :, :], c["iota8"][:, :].unsqueeze(1).broadcast_to([P, tiles, E]),
                               bc_last(idxf[:, :, k], E), ALU.is_equal)
    return last


def place_rows(G, ch, c, r, rank, total, slot_i, tiles, signal, value):
    pick, acc, base = r["pick"], r["acc"], r["base"]
    for n in range(tiles):
        ch.link(G.tensor_tensor(base[:, n, :], c["counts"][:, :], c["region0"][:, :], ALU.add))
        ch.link(G.tensor_tensor(c["counts"][:, :], c["counts"][:, :], total[:, n, :], ALU.add))
    ch.link(G.tensor_tensor(base[:, :, :], base[:, :, :], rank, ALU.add))
    for k in range(pick.shape[1]):
        last = G.tensor_tensor(acc[:, k, :, :], base[:, :, :], pick[:, k, :, :], ALU.mult)
    ch.link(last)
    half = E // 2
    while half > 0:
        ch.link(G.tensor_tensor(acc[:, :, :, 0:half], acc[:, :, :, 0:half], acc[:, :, :, half:2 * half], ALU.add))
        half //= 2
    ch.announce(G.tensor_copy(slot_i, acc[:, :, :, 0]), signal, value)


class Turn:

    def __init__(self, k, first, lap0, static, rings):
        self.k, self.first, self.lap0, self.static, self.rings = k, first, lap0, static, rings

    def unit(self, lag):
        return self.k - lag

    def ring(self, lag):
        return (self.first - lag) % self.rings

    def lap(self, lag):
        return self.lap0 + (self.first - lag) // self.rings

    def has(self, lag, units):
        return self.static is None or 0 <= self.static - lag < units


def turns(engine, rings, step, last, full_from, full_to):
    for k in range(full_from):
        step(Turn(k, k % rings, k // rings, k, rings))
    n = (full_to - full_from) // rings
    with engine.Fori(0, n) as i:
        for h in range(rings):
            step(Turn(rings * i + (full_from + h), h, i + full_from // rings, None, rings))
    for k in range(full_from + rings * n, last + 1):
        step(Turn(k, k % rings, k // rings, k, rings))


def free_bank(engine, sems, turn, units, *readers):
    for name, lag, count, before in readers[:1] if turn.static is None else readers:
        value = (turn.k - lag) * count + before
        after(engine, sems[name], min(value, count * units) if turn.static is not None else value)


def mamba(nc, t, c, w, sb, ps, sem):
    X = c["X"]
    V, A, T = nc.vector, nc.scalar, nc.tensor
    hT = sb("hT", [P, 2, XPAD])
    xs = [sb(f"xs{u}", [P, 4, PW]) for u in range(2)]
    zs = [sb(f"zs{u}", [P, 2, PW]) for u in range(2)]
    xhat = sb("xhat", [P, PT, D])
    stats = sb("stats", [P, PT, 6])
    mv0, rstd0, rtmp = c["mv0"], c["rstd0"], sb("rtmp", [P, 4, PT])
    mv1, rstd1 = sb("mv1", [P, PT, 2]), sb("rstd1", [P, PT])
    mv2, rstd2 = sb("mv2", [P, PT, 2]), sb("rstd2", [P, PT])
    sqs = sb("mean_square", [P, PT])
    dtr = sb("dt_raw", [P, PT, HEADS0])
    dte = sb("dt_exp", [P, PT, HEADS0])
    dtl = sb("dt_log", [P, PT, HEADS0])
    dtv = [sb(f"dt{u}", [P, PT, HEADS0]) for u in range(2)]
    dA = [sb(f"dA{u}", [P, PT, HEADS0]) for u in range(2)]
    uz = sb("dA_upto", [P, PT, HEADS0, P])
    L = [sb(f"decay{u}", [P, 2, 3, HEADS0, P]) for u in range(2)]
    sfx = sb("decay_to_end", [P, 2, HEADS0])
    cbm = sb("cb_masked", [P, 2, 3, P])
    mask3 = sb("mask3", [P, 3, P])
    xdt = [sb(f"x_dt{u}", [P, PT, HEADS0, HD0]) for u in range(2)]
    xde = [sb(f"x_dt_end{u}", [P, 2, HEADS0, HD0]) for u in range(2)]
    yg = sb("y_gated", [P, 2, PW])
    ysq = sb("y_square", [P, 2, PW])
    c_in = sb("c_in", [P, 2, XPAD])
    c_out = sb("c_out", [P, 2, SEQ_LEN])
    rms = sb("rms", [P, PT])
    res = sb("res", [P, PT, D])
    modbc = [sb(f"modbc{u}", [P, 2, 3, D]) for u in range(2)]
    h2 = sb("h2", [P, PT, D])
    h2T = sb("h2T", [P, PT, P])
    rows = [sb(f"rows{u}", [P, PT, ROW]) for u in range(2)]
    logits = sb("logits", [P, PT, E])
    diff = sb("logit_diff", [P, TILES, E])
    gsum = sb("gate_sum", [P, TILES])
    r = dict(top=sb("top", [P, PT, E]), idx=sb("idx", [P, PT, E], U32), idxf=sb("idxf", [P, PT, 2]),
             pick=sb("pick", [P, 1, PT, E]), acc=sb("pick_acc", [P, 1, PT, E]),
             base=sb("slot_base", [P, PT, E]))
    slot_i = [sb(f"slot_i{u}", [P, 1, PT], I32) for u in range(2)]

    pT = ps("pT", [P, 512])
    pX = [ps(f"pX{i}", [P, 512]) for i in range(2)]
    pS = [ps(f"pS{i}", [P, HEADS0, P]) for i in range(2)]
    pC = ps("pC", [P, 512])
    pY = [ps(f"pY{i}", [P, 2, 2, P]) for i in range(2)]
    pCB = pC[:, 0:384].rearrange("p (k t) -> p k t", t=P)
    p_dt = pC[:, 384:400].rearrange("p (t h) -> p t h", h=HEADS0)
    p_ss = pC[:, 400:404]
    p_lg = pC[:, 404:436].rearrange("p (t e) -> p t e", e=E)
    p_rk = pC[:, 436:468].rearrange("p (t e) -> p t e", e=E)
    p_tot = pC[:, 468:500].rearrange("p (t e) -> p t e", e=E)

    names = ("zeroed xhat hT_ps hT x_ps silu dt_ps dt_in dt_e dt_l dA uz seg_ps "
             "decay cb_ps cbm xv_ps xv sfx M_pool M y_ps yg ysq out_ps x1 mod router_in h2T_ps h2T lg_ps pick rk_ps "
             "slot diff gate_e conv c_silu lg_read mv1 rstd1 mv2 rstd2 ss_ps sqs rms").split()
    s = {n: sem("m_" + n) for n in names}
    s_mod = [sem(f"m_modbc{u}") for u in range(2)]
    s_scat = [sem(f"m_scatter{u}", kept=True) for u in range(2)]
    s_v, s_g = sem("m_dve"), sem("m_pool")

    def bank_free(engine, turn, *readers):
        free_bank(engine, s, turn, PAIRS, *readers)

    def run_stages(tn, stages):
        for lag, stage, *more in stages:
            if tn.has(lag, PAIRS):
                stage(tn, tn.unit(lag), tn.ring(lag), *more)

    with nc.Block() as block:
        @block.sync
        def _(sp):
            load_expert_weights(sp, t, c, 0)
            def modulation(tn, p, u):
                after(sp, s["router_in"], p - 1)
                src = c["mod_dram"][0].rearrange("s (m d) -> s m d", d=D)[cols(2 * p, 2), 2:5, :]
                sp.dma_start(modbc[u][:, :, :, :], src.partition_broadcast(P)).then_inc(s_mod[u], 16)

            turns(sp, 2, lambda tn: run_stages(tn, ((1, modulation),)), PAIRS, 4, PAIRS)

        @block.gpsimd
        def _(pool):
            g = nc.gpsimd
            ch = Chain(pool, s_g)
            ch.link(g.memset(hT[:, :, 0:3], 0.0))
            ch.link(g.memset(c_in[:, :, 0:3], 0.0))
            for u in range(2):
                ch.link(g.memset(rows[u][:, :, :], 0.0))
            g.memset(mask3[:, 1, :], 1.0).then_inc(s["zeroed"], 1)
            for k in (0, 2):
                g.tensor_copy(mask3[:, k, :], c["upto"][:, :]).then_inc(s["zeroed"], 1)
            pool.wait_ge(s["zeroed"], 3)

            def decays(tn, p, u):
                after(pool, s["dA"], p + 1)
                after(pool, s["seg_ps"], 6 * p)
                for n in range(PT):
                    g.tensor_tensor(uz[:, n, :, :], bc_last(dA[u][:, n, :], P),
                                    c["upto"][:, :].unsqueeze(1).broadcast_to([P, HEADS0, P]),
                                    ALU.mult).then_inc(s["uz"], 1)

            def experts_norm(tn, p, u):
                after_then(pool, s["mv2"], p + 1, s["zeroed"])
                inverse_root(g, ch, c, rstd2[:, :], rtmp[:, 2, :], mv2[:, :, 1], EPS_LN).then_inc(s["rstd2"], 1)

            def weigh(tn, p, u):
                for q in range(2):
                    after(pool, s["sfx"], 2 * p + q + 1)
                    after(pool, s["cbm"], 2 * p + q + 1)
                    g.tensor_tensor(L[u][:, q, 0, :, :], L[u][:, q, 0, :, :],
                                    cbm[:, q, 0, :].unsqueeze(1).broadcast_to([P, HEADS0, P]),
                                    ALU.mult).then_inc(s["M_pool"], 1)

            def squares(tn, p, u):
                after_then(pool, s["sqs"], p + 1, s["zeroed"])
                inverse_root(g, ch, c, rms[:, :], rtmp[:, 3, :], sqs[:, :], EPS_RMS).then_inc(s["rms"], 1)

            def scatter(tn, p, u):
                after_then(pool, s["slot"], p + 1, s["zeroed"])
                for n in range(PT):
                    pool.indirect_dma_start(c["routed"][0], bass.IndirectOffsetOnAxis(ap=slot_i[u][:, 0, n:n + 1], axis=0),
                                            rows[u][:, n, :], None).then_inc(s_scat[u], 16)

            def router_norm(tn, p, u):
                after_then(pool, s["mv1"], p + 1, s["zeroed"])
                inverse_root(g, ch, c, rstd1[:, :], rtmp[:, 1, :], mv1[:, :, 1], EPS_LN).then_inc(s["rstd1"], 1)

            def step(tn):
                ch.restart()
                run_stages(tn, ((3, experts_norm), (2, squares), (1, weigh), (0, decays), (2, router_norm),
                                (3, scatter)))
                ch.restart()

            turns(pool, 2, step, PAIRS + 2, 4, PAIRS)
            for u in range(2):
                pool.wait_ge(s_scat[u], 16 * PT * PAIRS // 2)

        @block.scalar
        def _(act):
            def modulate(tn, p, u):
                after(act, s["hT_ps"], p + 1)
                after(act, s["x_ps"], 6 * p)
                for q in range(2):
                    seq = cols(2 * p + q, 1)
                    A.activation(hT[:, q, 3:XPAD], pT[:, q * 256:q * 256 + 256], ACT.Identity,
                                 bias=c["modT"][0][:, SHIFT, seq], scale=c["modT"][0][:, SCALE, seq])\
                        .then_inc(s["hT"], 1)

            def softplus(tn, p, u):
                after(act, s["dt_in"], p + 1)
                A.activation(dte[:, :, :], dte[:, :, :], ACT.Exp).then_inc(s["dt_e"], 1)
                after(act, s["dt_e"], p + 1)
                A.activation(dtl[:, :, :], dte[:, :, :], ACT.Ln, bias=1.0).then_inc(s["dt_l"], 1)

            def silu(tn, p, u, b):
                if b == 0:
                    after(act, s["conv"], p)
                if b == 1:
                    after(act, s["yg"], p - 1)
                after(act, s["x_ps"], 6 * p + b + 1)
                if b == 0:
                    A.activation(c_in[:, :, 3:XPAD], pX[0][:, :].rearrange("p (q t) -> p q t", q=2), ACT.Identity,
                                 bias=w["bin_ch"][:, 5:6]).then_inc(s["silu"], 1)
                elif b < 4:
                    A.activation(xs[u][:, b - 1, :], pX[b % 2][:, :], ACT.Silu, bias=w["conv_bias"][:, b - 1:b])\
                        .then_inc(s["silu"], 1)
                else:
                    A.activation(zs[u][:, b - 4, :], pX[b % 2][:, :], ACT.Silu, bias=w["bin_ch"][:, b - 4:b - 3])\
                        .then_inc(s["silu"], 1)

            def silu_c(tn, p, u):
                after(act, s["conv"], p + 1)
                A.activation(xs[u][:, 3, :], c_out[:, :, :].rearrange("p q t -> p (q t)"), ACT.Silu,
                             bias=w["conv_b"][:, 3:4]).then_inc(s["c_silu"], 1)

            def decays(tn, p, u, first, end):
                after(act, s["y_ps"], 2 * (p - 1))
                for n in range(first, end):
                    after(act, s["seg_ps"], 6 * p + n + 1)
                    A.activation(L[u][:, n // 3, n % 3, :, :], pS[n % 2][:, :, :], ACT.Exp).then_inc(s["decay"], 1)

            def squares(tn, p, u):
                after(act, s["yg"], p + 1)
                after(act, s["ss_ps"], p)
                A.activation(ysq[:, :, :], yg[:, :, :], ACT.Square).then_inc(s["ysq"], 1)

            def router(tn, p, u):
                after(act, s["h2T_ps"], p + 1)
                after(act, s["lg_ps"], p)
                A.activation(h2T[:, :, :], pT[:, :].rearrange("p (n t) -> p n t", t=P), ACT.Copy)\
                    .then_inc(s["h2T"], 1)

            def step(tn):
                run_stages(tn, ((1, decays, 0, 4), (0, modulate), (1, decays, 4, 6), (2, squares), (0, softplus),
                                (0, silu, 0), (3, router), (1, silu_c),
                                *((0, silu, b) for b in range(1, 6))))

            turns(act, 2, step, PAIRS + 2, 4, PAIRS)
            act.wait_ge(s["diff"], PAIRS)
            A.activation(diff[:, :, :], diff[:, :, :], ACT.Exp).then_inc(s["gate_e"], 1)

        @block.tensor
        def _(pe):
            def turn_input(tn, p, u):
                after(pe, s["xhat"], p + 1)
                bank_free(pe, tn, ("x1", 2, 1, 0), ("xv", 1, 2, 0), ("h2T", 3, 1, 0), ("hT", 0, 2, 0))
                for n in range(PT):
                    last = T.transpose(pT[:, n * P:n * P + P], xhat[:, n, :], c["ident"][:, :])
                last.then_inc(s["hT_ps"], 1)

            def steps(tn, p, u):
                pe.wait_ge(s["hT"], 2 * (p + 1))
                bank_free(pe, tn, ("slot", 3, 1, 0), ("cbm", 1, 2, 0), ("sqs", 2, 1, 0), ("dt_in", 0, 1, 0))
                for n in range(PT):
                    t0 = 3 + n % 2 * P
                    last = T.matmul(p_dt[:, n, :], hT[:, n // 2, t0:t0 + P], w["WinT"][:, 6 * P:6 * P + HEADS0],
                                    start=True, stop=True)
                last.then_inc(s["dt_ps"], 1)

            def project(tn, p, u, b):
                x2 = pX[b % 2][:, :].rearrange("p (q t) -> p q t", q=2)
                after(pe, s["silu"], 6 * p + b - 1)
                if 1 <= b <= 3:
                    for k in range(4):
                        last = T.matmul(x2, w["taps"][:, k, (b - 1) * P:b * P], hT[:, :, k:k + SEQ_LEN],
                                        start=(k == 0), stop=(k == 3))
                        if k == 0:
                            T.matmul(x2[:, :, 0:3], c["ident"][:, :], w["edge"][:, b - 1, :, :], start=False, stop=False)
                else:
                    block = 5 if b == 0 else b - 4
                    last = T.matmul(x2, w["WinT"][:, block * P:(block + 1) * P], hT[:, :, 3:XPAD],
                                    start=True, stop=True)
                last.then_inc(s["x_ps"], 1)

            def decays(tn, p, u, first, end):
                for n in range(first, end):
                    q, k = n // 3, n % 3
                    tile = 2 * q + (k > 0)
                    after(pe, s["uz"], PT * p + tile + 1)
                    after(pe, s["decay"], 6 * p + n - 1)
                    T.matmul(pS[n % 2][:, :, :], c["ones"][:, :] if k == 1 else c["beyond"][:, :],
                             uz[:, tile, :, :], start=True, stop=True).then_inc(s["seg_ps"], 1)

            def values(tn, p, u, q):
                pe.wait_ge(s["silu"], 6 * p + 4)
                pe.wait_ge(s["c_silu"], p + 1)
                if q == 0:
                    bank_free(pe, tn, ("h2T", 3, 1, 1), ("hT", 0, 2, 2), ("x1", 2, 1, 0))
                else:
                    pe.wait_ge(s["xv"], 2 * p + 1)
                for n in range(2):
                    for b in range(2):
                        last = T.transpose(pT[:, (2 * n + b) * P:(2 * n + b + 1) * P],
                                           xs[u][:, b, (2 * q + n) * P:(2 * q + n + 1) * P], c["ident"][:, :])
                last.then_inc(s["xv_ps"], 1)
                if q == 0:
                    bank_free(pe, tn, ("sqs", 2, 1, 1), ("lg_read", 3, 1, 1), ("dt_in", 0, 1, 1))
                else:
                    pe.wait_ge(s["cbm"], 2 * p + 1)
                t0 = q * SEQ_LEN
                T.matmul(pC[:, 0:256], xs[u][:, 2, t0:t0 + P], xs[u][:, 3, t0:t0 + 256], start=True, stop=True)
                T.matmul(pC[:, 256:384], xs[u][:, 2, t0 + P:t0 + 256], xs[u][:, 3, t0 + P:t0 + 256],
                         start=True, stop=True).then_inc(s["cb_ps"], 1)

            def mixed(tn, p, u):
                after(pe, s["M_pool"], 2 * p + 2)
                after(pe, s["M"], 2 * p + 2)
                after(pe, s["yg"], p)
                for b in range(2):
                    for q in range(2):
                        for e in range(2):
                            h = 2 * b + e
                            o = slice(HD0 * e, HD0 * e + HD0)
                            T.matmul(pY[b][o, q, 0, :], xdt[u][:, 2 * q, h, :], L[u][:, q, 0, h, :],
                                     start=True, stop=True)
                            T.matmul(pY[b][o, q, 1, :], xde[u][:, q, h, :], L[u][:, q, 1, h, :],
                                     start=True, stop=False)
                            last = T.matmul(pY[b][o, q, 1, :], xdt[u][:, 2 * q + 1, h, :], L[u][:, q, 2, h, :],
                                            start=False, stop=True)
                    last.then_inc(s["y_ps"], 1)

            def output(tn, p, u):
                pe.wait_ge(s["yg"], p + 1)
                bank_free(pe, tn, ("xv", 1, 2, 2), ("h2T", 3, 1, 1), ("hT", 0, 2, 2))
                for n in range(PT):
                    for b in range(2):
                        last = T.matmul(pT[:, n * P:n * P + P], yg[:, b, n * P:n * P + P], w["WoT"][:, b, :],
                                        start=(b == 0), stop=(b == 1))
                last.then_inc(s["out_ps"], 1)

            def squares(tn, p, u):
                pe.wait_ge(s["ysq"], p + 1)
                bank_free(pe, tn, ("lg_read", 3, 1, 1), ("dt_in", 0, 1, 1), ("cbm", 1, 2, 0))
                for n in range(PT):
                    for b in range(2):
                        last = T.matmul(p_ss[:, n:n + 1], ysq[:, b, n * P:n * P + P], c["ones"][:, 0:1],
                                        start=(b == 0), stop=(b == 1))
                last.then_inc(s["ss_ps"], 1)

            def turn_router(tn, p, u):
                pe.wait_ge(s["router_in"], p + 1)
                bank_free(pe, tn, ("hT", 0, 2, 2), ("x1", 2, 1, 0), ("xv", 1, 2, 0))
                for n in range(PT):
                    last = T.transpose(pT[:, n * P:n * P + P], h2[:, n, :], c["ident"][:, :])
                last.then_inc(s["h2T_ps"], 1)

            def logits_(tn, p, u):
                pe.wait_ge(s["h2T"], p + 1)
                bank_free(pe, tn, ("dt_in", 0, 1, 1), ("cbm", 1, 2, 0), ("sqs", 2, 1, 0), ("slot", 3, 1, 0))
                for n in range(PT):
                    last = T.matmul(p_lg[:, n, :], h2T[:, n, :], w["Wr"][0][:, :], start=True, stop=True)
                last.then_inc(s["lg_ps"], 1)

            def ranks(tn, p, u):
                pe.wait_ge(s["pick"], p + 1)
                bank_free(pe, tn, ("cbm", 1, 2, 2), ("sqs", 2, 1, 1), ("lg_read", 3, 1, 1))
                T.matmul(p_rk, c["before"][:, :], r["pick"][:, 0, :, :], start=True, stop=True)
                T.matmul(p_tot, c["ones"][:, :], r["pick"][:, 0, :, :], start=True, stop=True).then_inc(s["rk_ps"], 1)

            def step(tn):
                run_stages(tn, ((1, decays, 0, 2), (2, mixed), (1, decays, 2, 4), (0, turn_input),
                                (1, decays, 4, 6), (0, steps),
                                (0, project, 0), (3, turn_router), (0, project, 1), (3, logits_), (2, squares),
                                (1, values, 0), (0, project, 2), (1, values, 1), (0, project, 3), (3, ranks),
                                (2, output), (0, project, 4), (0, project, 5)))

            turns(pe, 2, step, PAIRS + 2, 4, PAIRS)

        @block.vector
        def _(dve):
            v = Chain(dve, s_v)
            v.link(V.memset(c["counts"][:, :], 0.0))
            dve.wait_ge(s["zeroed"], 3)
            def norm_input(tn, p, u):
                after(dve, s["hT_ps"], p)
                m, r0 = mv0[:, cols(PT * p, PT), :], rstd0[:, cols(PT * p, PT)]
                v.announce(normalize(V, lambda n: tile_at(X, PT * p + n), lambda n: xhat[:, n, :], m, r0, PT),
                           s["xhat"], p + 1)

            def dt_in(tn, p, u):
                dve.wait_ge(s["dt_ps"], p + 1)
                v.link(V.tensor_tensor(dtr[:, :, :], p_dt,
                                       w["dt_bias"][:, :].unsqueeze(1).broadcast_to([P, PT, HEADS0]), ALU.add))
                v.announce(V.scalar_tensor_tensor(dte[:, :, :], dtr[:, :, :], -1.0, dtr[:, :, :], ALU.mult, ALU.min),
                           s["dt_in"], p + 1)

            def dt_out(tn, p, u):
                dve.wait_ge(s["dt_l"], p + 1)
                v.link(V.scalar_tensor_tensor(dtv[u][:, :, :], dtr[:, :, :], 0.0, dtl[:, :, :], ALU.max, ALU.add))
                v.announce(V.tensor_tensor(dA[u][:, :, :], dtv[u][:, :, :],
                                           w["A"][:, :].unsqueeze(1).broadcast_to([P, PT, HEADS0]), ALU.mult),
                           s["dA"], p + 1)

            def conv(tn, p, u):
                dve.wait_ge(s["silu"], 6 * p + 1)
                after(dve, s["c_silu"], p)
                v.link(V.tensor_scalar(c_out[:, :, :], c_in[:, :, 0:SEQ_LEN], w["conv_w"][:, 3, 0:1], None, ALU.mult))
                for k in range(1, 4):
                    last = V.scalar_tensor_tensor(c_out[:, :, :], c_in[:, :, k:k + SEQ_LEN],
                                                  w["conv_w"][:, 3, k:k + 1], c_out[:, :, :], ALU.mult, ALU.add)
                    if k < 3:
                        v.link(last)
                v.announce(last, s["conv"], p + 1)

            def values(tn, p, u, q):
                dve.wait_ge(s["cb_ps"], 2 * p + q + 1)
                after(dve, s["M_pool"], 2 * p + q - 1)
                V.tensor_tensor(cbm[:, q, :, :], pCB, mask3[:, :, :], ALU.mult).then_inc(s["cbm"], 1)
                dve.wait_ge(s["xv_ps"], 2 * p + q + 1)
                V.tensor_tensor(xdt[u][:, 2 * q:2 * q + 2, :, :].rearrange("p n h d -> p (n h) d"),
                                pT[:, :].rearrange("p (n d) -> p n d", d=HD0),
                                bc_last(dtv[u][:, 2 * q:2 * q + 2, :].rearrange("p n h -> p (n h)"), HD0),
                                ALU.mult).then_inc(s["xv"], 1)
                dve.wait_ge(s["decay"], 6 * p + 3 * q + 3)
                V.tensor_copy(sfx[:, q, :], L[u][:, q, 0, :, P - 1]).then_inc(s["sfx"], 1)
                dve.wait_ge(s["cbm"], 2 * p + q + 1)
                last = V.tensor_tensor(L[u][:, q, 1, :, :], L[u][:, q, 1, :, :],
                                       cbm[:, q, 1, :].unsqueeze(1).broadcast_to([P, HEADS0, P]), ALU.mult)
                dve.wait_ge(s["sfx"], 2 * p + q + 1)
                dve.wait_ge(s["xv"], 2 * p + q + 1)
                V.tensor_tensor(xde[u][:, q, :, :], xdt[u][:, 2 * q, :, :], bc_last(sfx[:, q, :], HD0), ALU.mult)
                v.announce(V.tensor_tensor(L[u][:, q, 2, :, :], L[u][:, q, 2, :, :],
                                           cbm[:, q, 2, :].unsqueeze(1).broadcast_to([P, HEADS0, P]), ALU.mult),
                           s["M"], 2 * p + q + 1)

            def mixed(tn, p, u):
                dve.wait_ge(s["silu"], 6 * p + 6)
                for b in range(2):
                    dve.wait_ge(s["y_ps"], 2 * p + b + 1)
                    last = V.scalar_tensor_tensor(yg[:, b, :], xs[u][:, b, :], w["D_ch"][:, b:b + 1],
                                                  pY[b][:, :, :, :].rearrange("p q k t -> p (q k t)"),
                                                  ALU.mult, ALU.add)
                v.link(last)
                v.announce(V.tensor_tensor(yg[:, :, :], yg[:, :, :], zs[u][:, :, :], ALU.mult), s["yg"], p + 1)

            def squares(tn, p, u):
                dve.wait_ge(s["ss_ps"], p + 1)
                v.announce(V.tensor_scalar(sqs[:, :], p_ss, 1.0 / DSSM, None, ALU.mult), s["sqs"], p + 1)

            def output(tn, p, u):
                dve.wait_ge(s["out_ps"], p + 1)
                dve.wait_ge(s["rms"], p + 1)
                v.link(V.tensor_tensor(res[:, :, :], pT[:, :].rearrange("p (n d) -> p n d", d=D),
                                       bc_last(rms[:, :], D), ALU.mult))
                v.link(V.tensor_tensor(res[:, :, :], res[:, :, :],
                                       w["bout_bc"][:, :].unsqueeze(1).broadcast_to([P, PT, D]), ALU.add))
                after(dve, s_mod[u], 16 * tn.lap(2) + 16)
                for q in range(2):
                    last = V.tensor_tensor(res[:, 2 * q:2 * q + 2, :], res[:, 2 * q:2 * q + 2, :],
                                           modbc[u][:, q, 0, :].unsqueeze(1).broadcast_to([P, 2, D]), ALU.mult)
                v.link(last)
                x = X[:, cols(PT * p, PT), :]
                V.tensor_tensor(x, x, res[:, :, :], ALU.add).then_inc(s["x1"], 1)
                after_then(dve, s["x1"], p + 1, s["zeroed"])
                v.announce(moments(V, v, lambda n: tile_at(X, PT * p + n), stats, mv1, PT), s["mv1"], p + 1)

            def router_input(tn, p, u):
                dve.wait_ge(s["rstd1"], p + 1)
                v.link(normalize(V, lambda n: tile_at(X, PT * p + n), lambda n: h2[:, n, :], mv1, rstd1, PT))
                for m, op in ((2, ALU.mult), (1, ALU.add)):
                    for q in range(2):
                        last = V.tensor_tensor(h2[:, 2 * q:2 * q + 2, :], h2[:, 2 * q:2 * q + 2, :],
                                               modbc[u][:, q, m, :].unsqueeze(1).broadcast_to([P, 2, D]), op)
                    if m == 2:
                        v.link(last)
                last.then_inc(s["router_in"], 1)
                after_then(dve, s["router_in"], p + 1, s["zeroed"])
                v.announce(moments(V, v, lambda n: h2[:, n, :], stats, mv2, PT), s["mv2"], p + 1)

            def choose(tn, p, u):
                dve.wait_ge(s["lg_ps"], p + 1)
                v.announce(V.tensor_tensor(logits[:, :, :], p_lg,
                                           w["br_bc"][:, :].unsqueeze(1).broadcast_to([P, PT, E]), ALU.add),
                           s["lg_read"], p + 1)
                dve.wait_ge(s["zeroed"], 1)
                dve.nop(nofuse=True)
                v.announce(route(V, v, c, logits, r, PT, 0), s["pick"], p + 1)
                v.announce(V.tensor_tensor(diff[:, cols(PT * p, PT), :], logits[:, :, :],
                                           bc_last(r["top"][:, :, 0], E), ALU.subtract), s["diff"], p + 1)

            def experts_input(tn, p, u):
                dve.wait_ge(s["rstd2"], p + 1)
                after(dve, s_scat[1 - u], 16 * PT * (tn.lap(3) + u))
                v.link(normalize(V, lambda n: h2[:, n, :], lambda n: rows[u][:, n, 0:D], mv2, rstd2, PT))
                for m, op in (("ln_g", ALU.mult), ("ln_b", ALU.add)):
                    v.link(V.tensor_tensor(rows[u][:, :, 0:D], rows[u][:, :, 0:D],
                                           w[m][:, :].unsqueeze(1).broadcast_to([P, PT, D]), op))
                v.link(V.tensor_copy(rows[u][:, :, D], c["token_id"][:, cols(PT * p, PT)]))

            def place(tn, p, u):
                dve.wait_ge(s["rk_ps"], p + 1)
                place_rows(V, v, c, r, p_rk, p_tot, slot_i[u][:, :, :], PT, s["slot"], p + 1)

            def step(tn):
                v.restart()
                run_stages(tn, ((0, norm_input), (2, mixed), (3, router_input), (0, dt_in), (3, experts_input),
                                (0, dt_out), (3, choose), (2, squares), (0, conv), (1, values, 0), (1, values, 1),
                                (3, place), (2, output)))
                v.restart()

            turns(dve, 2, step, PAIRS + 2, 4, PAIRS)
            dve.wait_ge(s["gate_e"], 1)
            v.link(V.tensor_reduce(gsum[:, :], diff[:, :, :], AX.X, ALU.add))
            v.link(V.reciprocal(c["gates"][:, 0, :], gsum[:, :]))


def attention(nc, t, c, w, sb, ps, sem):
    X = c["X"]
    V, A, T = nc.vector, nc.scalar, nc.tensor
    S2 = SEQ_LEN // P
    H, KR = HEADS1, 6 * HD1
    a0 = [sb(f"a0_{u}", [P, S2, D]) for u in range(3)]
    gbc = [sb(f"gate0_bc{u}", [P, D]) for u in range(3)]
    modbc = [sb(f"modbc{u}", [P, 3, D]) for u in range(3)]
    mv0, rstd0 = [sb(f"mv0_{u}", [P, S2, 2]) for u in range(3)], [sb(f"rstd0_{u}", [P, S2]) for u in range(3)]
    mv1, rstd1 = [sb(f"mv1_{u}", [P, S2, 2]) for u in range(3)], [sb(f"rstd1_{u}", [P, S2]) for u in range(3)]
    stats, rtmp = sb("stats", [P, S2, 6]), sb("rtmp", [P, 2, S2])
    res = sb("res", [P, S2, D])
    xhat = sb("xhat", [P, S2, D])
    hT = sb("hT", [P, SEQ_LEN])
    parts = [sb(f"qk_parts{u}", [P, 3, 2 * SEQ_LEN], BF16) for u in range(3)]
    rest = sb("qk_rest", [P, 2 * SEQ_LEN])
    vv = [sb(f"v_ones{u}", [P, S2, H, LAT]) for u in range(3)]
    Q = [sb(f"q_rows{u}", [P, H, SEQ_LEN], BF16) for u in range(3)]
    K = [sb(f"k_rows{u}", [P, H, SEQ_LEN], BF16) for u in range(3)]
    maskq, maskk = sb("mask_q", [P, 4, P], BF16), sb("mask_k", [P, 4, P], BF16)
    key_ones = sb("key_ones", [P, 1])
    mx = sb("row_max", [P, 3, H])
    nm = sb("neg_max", [P, S2, H])
    mT = sb("max_parts", [H, 2, SEQ_LEN], BF16)
    pr = [sb(f"probs{i}", [P, 4, P]) for i in range(6)]
    oT = sb("out_T", [P, 4, SEQ_LEN])
    rden = sb("rden", [P, S2, H])
    yv = sb("y_tok", [P, S2, H, HD1])
    h2T = sb("h2T", [P, S2, P])
    rows = [sb(f"rows{u}", [P, 2, S2, ROW]) for u in range(3)]
    top2 = sb("top2", [P, TILES, 2])
    logits = sb("logits", [P, S2, E])
    r = dict(top=sb("top", [P, S2, E]), idx=sb("idx", [P, S2, E], U32), idxf=sb("idxf", [P, S2, 2]),
             pick=sb("pick", [P, 2, S2, E]), acc=sb("pick_acc", [P, 2, S2, E]), base=sb("slot_base", [P, S2, E]))
    rk = sb("ranks", [P, 2, S2, E])
    both = sb("pick_both", [P, S2, E])
    slot_i = [sb(f"slot_i{u}", [P, 2, S2], I32) for u in range(3)]
    gexp = sb("gate_exp", [P, TILES])

    pT, pP = ps("pT", [P, 512]), ps("pP", [P, 512])
    pS = [ps(f"pS{i}", [P, 4, P]) for i in range(4)]
    pO = ps("pO", [P, 4, SEQ_LEN])
    p_lg = pT[:, 0:S2 * E].rearrange("p (n e) -> p n e", e=E)
    p_rk = pT[:, 0:2 * S2 * E].rearrange("p (k n e) -> p k n e", n=S2, e=E)

    names = ("zeroed key_ones mv0 rstd0 xhat hT_ps hT qk_ps part1 rest1 part2 parts v_ps v scores max neg mT_ps m1 m2 "
             "probs_ps probs pv oT yT_ps yT x3 mv1 rstd1 h2 h2T_ps h2T lg_ps lg_read pick rk_ps rk_read slot gexp").split()
    s = {n: sem("a_" + n) for n in names}
    s_a0, s_mod, s_dram, s_qk, s_m = ([sem(f"a_{n}{u}") for u in range(3)] for n in
                                      ("answers", "modbc", "parts_dram", "packed", "max_rows"))
    s_scat = [sem(f"a_scatter{u}", kept=True) for u in range(3)]
    s_v, s_g = sem("a_dve"), sem("a_pool")
    ZEROED = 11

    def bank_free(engine, turn, *readers):
        free_bank(engine, s, turn, SEQS, *readers)

    UNITS = [(g, m) for g in range(4) for m in range(3)]
    TILE_PAIR = ((0, 0), (0, 1), (1, 1))

    with nc.Block() as block:
        @block.sync
        def _(sp):
            qp = c["parts_dram"]

            def load(p, u, lap):
                after(sp, s["mv0"], p - 2)
                sp.dma_start(a0[u][:, :, :], c["answers"][0][cols(2 * P * p, 2 * P), :]
                             .rearrange("(n p) d -> p n d", p=P)).then_inc(s_a0[u], 16)
                m0 = c["mod_dram"][0].rearrange("s (m d) -> s m d", d=D)[cols(p, 1), 5:6, :]
                sp.dma_start(gbc[u][:, :], m0.rearrange("s m d -> (s m) d").rearrange("a d -> (a d)").partition_broadcast(P))\
                    .then_inc(s_a0[u], 16)

            def modulation(p, u, lap):
                after(sp, s["h2"], p - 2)
                m1 = c["mod_dram"][1].rearrange("s (m d) -> s m d", d=D)[cols(p, 1), 2:5, :]
                sp.dma_start(modbc[u][:, :, :], m1.rearrange("s m d -> (s m) d").partition_broadcast(P))\
                    .then_inc(s_mod[u], 16)

            def pack(p, u, lap):
                after(sp, s["parts"], p + 1)
                sp.dma_start(qp[u], parts[u][:, :, :]).then_inc(s_dram[u], 16)
                after(sp, s_dram[u], 16 * lap + 16)
                after(sp, s["probs_ps"], 12 * (p - 2))
                v = qp[u].rearrange("(h d) i t -> i d h t", d=HD1)
                for r6, (a, b) in enumerate(((0, 0), (1, 0), (2, 0), (0, 1), (1, 1), (0, 2))):
                    sp.dma_start(Q[u][r6 * HD1:r6 * HD1 + HD1, :, :], v[a][:, :, 0:SEQ_LEN]).then_inc(s_qk[u], 16)
                    sp.dma_start(K[u][r6 * HD1:r6 * HD1 + HD1, :, :], v[b][:, :, SEQ_LEN:2 * SEQ_LEN])\
                        .then_inc(s_qk[u], 16)
                sp.dma_start(Q[u][KR:KR + 2, :, :], Q[u][P - 2:P, :, :]).then_inc(s_qk[u], 16)

            def max_rows(p, u, lap):
                after(sp, s["m2"], p + 1)
                after(sp, s["scores"], 12 * p + 12)
                for i in range(2):
                    sp.dma_start(Q[u][KR + i:KR + i + 1, :, :], mT[:, i, :]).then_inc(s_m[u], 16)

            def step(tn):
                for lag, stage in ((0, load), (2, pack), (4, modulation), (3, max_rows)):
                    if tn.has(lag, SEQS):
                        stage(tn.unit(lag), tn.ring(lag), tn.lap(lag))
                if tn.static == 1:
                    sp.wait_ge(s["zeroed"], ZEROED)

            turns(sp, 3, step, SEQS + 3, 9, SEQS)
            load_expert_weights(sp, t, c, 1)

        @block.gpsimd
        def _(pool):
            g = nc.gpsimd
            ch = Chain(pool, s_g)
            ch.link(g.memset(key_ones[:, :], 1.0))
            g.affine_select(out=key_ones[:, :], in_=key_ones[:, :], compare_op=ALU.is_ge, fill=0.0,
                            base=KR + 1, pattern=[[0, 1]], channel_multiplier=-1).then_inc(s["key_ones"], 1)
            for u in range(3):
                ch.link(g.memset(vv[u][:, :, :, :], 0.0))
                ch.link(g.memset(rows[u][:, :, :, :], 0.0))
                g.memset(vv[u][:, :, :, HD1:HD1 + 1], 1.0).then_inc(s["zeroed"], 1)
            for n, (m, sign) in enumerate(((maskq, 1), (maskk, -1))):
                ch.link(g.memset(m[:, :, :], 0.0))
                g.affine_select(out=m[:, :, :], in_=m[:, :, :], compare_op=ALU.is_ge, fill=MASKED, base=0,
                                pattern=[[0, 4], [-sign, P]], channel_multiplier=sign).then_inc(s["zeroed"], 1)
            g.memset(rtmp[:, :, :], 0.0).then_inc(s["zeroed"], 1)
            pool.wait_ge(s["zeroed"], ZEROED)

            def load(p, u):
                after_then(pool, s["mv0"], p + 1, s["zeroed"])
                inverse_root(g, ch, c, rstd0[u][:, :], rtmp[:, 0, :], mv0[u][:, :, 1], EPS_LN).then_inc(s["rstd0"], 1)

            def output(p, u):
                after_then(pool, s["mv1"], p + 1, s["zeroed"])
                inverse_root(g, ch, c, rstd1[u][:, :], rtmp[:, 1, :], mv1[u][:, :, 1], EPS_LN)\
                    .then_inc(s["rstd1"], 1)

            def place(p, u):
                after_then(pool, s["rk_read"], p + 1, s["zeroed"])
                place_rows(g, ch, c, r, rk[:, 0, :, :], rk[:, 1, :, :], slot_i[u][:, :, :], S2, s["slot"], p + 1)

            def scatter(p, u):
                after_then(pool, s["slot"], p + 1, s["zeroed"])
                for k in range(2):
                    for n in range(S2):
                        pool.indirect_dma_start(c["routed"][1],
                                                bass.IndirectOffsetOnAxis(ap=slot_i[u][:, k, n:n + 1], axis=0),
                                                rows[u][:, k, n, :], None).then_inc(s_scat[u], 16)

            def step(tn):
                ch.restart()
                for lag, stage in ((7, place), (5, output), (0, load), (7, scatter)):
                    if tn.has(lag, SEQS):
                        stage(tn.unit(lag), tn.ring(lag))
                ch.restart()

            turns(pool, 3, step, SEQS + 6, 9, SEQS)
            for u in range(3):
                pool.wait_ge(s_scat[u], 16 * 4 * len(range(u, SEQS, 3)))

        @block.scalar
        def _(act):
            def project(tn):
                p = tn.unit(1)
                after(act, s["hT_ps"], p + 1)
                after(act, s["v_ps"], p)
                A.activation(hT[:, :], pT[:, 0:SEQ_LEN], ACT.Identity, bias=c["modT"][1][:, SHIFT, cols(p, 1)],
                             scale=c["modT"][1][:, SCALE, cols(p, 1)]).then_inc(s["hT"], 1)

            def ranks(tn):
                p = tn.unit(7)
                after(act, s["rk_ps"], p + 1)
                after(act, s["slot"], p)
                A.activation(rk[:, :, :, :], p_rk, ACT.Copy).then_inc(s["rk_read"], 1)

            def router(tn):
                p = tn.unit(6)
                after(act, s["h2T_ps"], p + 1)
                after(act, s["lg_ps"], p)
                A.activation(h2T[:, :, :], pP[:, 0:SEQ_LEN].rearrange("p (n t) -> p n t", t=P), ACT.Copy)\
                    .then_inc(s["h2T"], 1)

            def first_part(tn):
                p, u = tn.unit(1), tn.ring(1)
                after(act, s["qk_ps"], p + 1)
                after(act, s_dram[u], 16 * tn.lap(1))
                A.activation(parts[u][:, 0, :], pP[:, :], ACT.Copy).then_inc(s["part1"], 1)

            def second_part(tn):
                p, u = tn.unit(1), tn.ring(1)
                after(act, s["rest1"], p + 1)
                A.activation(parts[u][:, 1, :], rest[:, :], ACT.Copy).then_inc(s["part2"], 1)

            def exponentials(tn, g):
                p = tn.unit(4)
                after(act, s["pv"], 4 * p + g - 1)
                for i in range(3 * g, 3 * g + 3):
                    after(act, s["probs_ps"], 12 * p + i + 1)
                    A.activation(pr[i % 6][:, :, :], pS[2 + i % 2][:, :, :], ACT.Exp, scale=HD1 ** -0.5)\
                        .then_inc(s["probs"], 1)

            def mixed(tn):
                p = tn.unit(4)
                after(act, s["pv"], 4 * p + 4)
                after(act, s["yT_ps"], 2 * p)
                A.activation(oT[:, :, :], pO[:, :, :], ACT.Copy).then_inc(s["oT"], 1)

            def maxima(tn):
                p, u = tn.unit(3), tn.ring(3)
                after(act, s["mT_ps"], p + 1)
                if tn.has(4, SEQS):
                    after(act, s_m[tn.ring(4)], 32 * tn.lap(4) + 32)
                A.activation(mT[:, 0, :], pT[0:H, 0:SEQ_LEN], ACT.Copy).then_inc(s["m1"], 1)

            def step(tn):
                for lag, stage, *rest_ in (
                        (1, project), (7, ranks), (4, exponentials, 0), (4, exponentials, 1), (6, router), (4, exponentials, 2),
                        (1, first_part), (4, exponentials, 3), (1, second_part), (3, maxima), (4, mixed)):
                    if tn.has(lag, SEQS):
                        stage(tn, *rest_)

            turns(act, 3, step, SEQS + 6, 9, SEQS)
            act.wait_ge(s["gexp"], 1)
            A.activation(gexp[:, :], gexp[:, :], ACT.Exp).then_inc(s["gexp"], 1)

        @block.tensor
        def _(pe):
            def turn_input(tn):
                p = tn.unit(1)
                after(pe, s["xhat"], p + 1)
                bank_free(pe, tn, ("m2", 3, 1, 0), ("lg_read", 6, 1, 0), ("rk_read", 7, 1, 0), ("hT", 1, 1, 0))
                for n in range(S2):
                    last = T.transpose(pT[:, n * P:n * P + P], xhat[:, n, :], c["ident"][:, :])
                last.then_inc(s["hT_ps"], 1)

            def turn_router(tn):
                p = tn.unit(6)
                after(pe, s["h2"], p + 1)
                bank_free(pe, tn, ("yT", 5, 2, 2), ("v", 1, 1, 0))
                for n in range(S2):
                    last = T.transpose(pP[:, n * P:n * P + P], rows[tn.ring(6)][:, 0, n, 0:D], c["ident"][:, :])
                last.then_inc(s["h2T_ps"], 1)

            def maxima(tn, i):
                p, u = tn.unit(3), tn.ring(3)
                if i == 0:
                    after(pe, s_qk[u], 16 * 13 * tn.lap(3) + 16 * 13)
                g, m = UNITS[i]
                kt, qt = TILE_PAIR[m]
                after(pe, s["max"], 12 * p + i - 1)
                if kt == qt:
                    T.matmul(pS[i % 2][:, :, :], c["identb"][:, :], maskq[:, :, :], start=True, stop=False)
                for h in range(4):
                    last = T.matmul(pS[i % 2][:, h, :], Q[u][:, 4 * g + h, qt * P:qt * P + P],
                                    K[u][:, 4 * g + h, kt * P:kt * P + P], start=(kt != qt),
                                    stop=(kt != qt or h == 3))
                last.then_inc(s["scores"], 1)

            def logits_(tn):
                p = tn.unit(6)
                after(pe, s["h2T"], p + 1)
                bank_free(pe, tn, ("rk_read", 7, 1, 1), ("hT", 1, 1, 1), ("m2", 3, 1, 0))
                for n in range(S2):
                    last = T.matmul(p_lg[:, n, :], h2T[:, n, :], w["Wr"][1][:, :], start=True, stop=True)
                last.then_inc(s["lg_ps"], 1)

            def queries_keys(tn):
                p = tn.unit(1)
                after(pe, s["hT"], p + 1)
                bank_free(pe, tn, ("h2T", 6, 1, 1), ("yT", 5, 2, 2), ("v", 1, 1, 0))
                for i in range(2):
                    last = T.matmul(pP[:, i * SEQ_LEN:i * SEQ_LEN + SEQ_LEN], w["Wqkv"][:, i, :], hT[:, :],
                                    start=True, stop=True)
                last.then_inc(s["qk_ps"], 1)

            def ranks(tn):
                p = tn.unit(7)
                after(pe, s["pick"], p + 1)
                bank_free(pe, tn, ("hT", 1, 1, 1), ("m2", 3, 1, 0), ("lg_read", 6, 1, 0))
                T.matmul(p_rk[:, 0, :, :], c["before"][:, :], both[:, :, :], start=True, stop=True)
                T.matmul(p_rk[:, 1, :, :], c["ones"][:, :], both[:, :, :], start=True, stop=True)\
                    .then_inc(s["rk_ps"], 1)

            def mix(tn, g, m):
                p, u = tn.unit(4), tn.ring(4)
                kt, qt = TILE_PAIR[m]
                if g == 0 and m == 0:
                    after(pe, s_m[u], 32 * tn.lap(4) + 32)
                if g < 4:
                    i = 3 * g + m
                    after(pe, s["probs"], 12 * p + i - 1)
                    if kt == qt:
                        T.matmul(pS[2 + i % 2][:, :, :], c["identb"][:, :], maskk[:, :, :], start=True, stop=False)
                    for h in range(4):
                        last = T.matmul(pS[2 + i % 2][:, h, :], K[u][:, 4 * g + h, kt * P:kt * P + P],
                                        Q[u][:, 4 * g + h, qt * P:qt * P + P], start=(kt != qt),
                                        stop=(kt != qt or h == 3))
                    last.then_inc(s["probs_ps"], 1)
                if g > 0:
                    if g == 1 and m == 0:
                        after(pe, s["v"], p + 1)
                        after(pe, s["oT"], p)
                    i = 3 * (g - 1) + m
                    after(pe, s["probs"], 12 * p + i + 1)
                    for h in range(4):
                        last = T.matmul(pO[32 * h:32 * h + 32, g - 1, qt * P:qt * P + P],
                                        vv[u][:, kt, 4 * (g - 1) + h, :], pr[i % 6][:, h, :],
                                        start=(m != 2), stop=(m != 1))
                    if m == 2:
                        last.then_inc(s["pv"], 1)

            def turn_output(tn, n):
                p = tn.unit(5)
                after(pe, s["oT"], p + 1)
                bank_free(pe, tn, *([("yT", 5, 2, 1)] if n else [("v", 1, 1, 0), ("yT", 5, 2, 0), ("h2T", 6, 1, 0)]))
                for g in range(4):
                    last = T.transpose(pP[:, g * P:g * P + P], oT[:, g, n * P:n * P + P], c["ident"][:, :])
                last.then_inc(s["yT_ps"], 1)

            def turn_max(tn):
                p = tn.unit(3)
                after(pe, s["neg"], p + 1)
                bank_free(pe, tn, ("lg_read", 6, 1, 1), ("rk_read", 7, 1, 1), ("hT", 1, 1, 1))
                for n in range(S2):
                    last = T.transpose(pT[0:H, n * P:n * P + P], nm[:, n, :], c["ident"][:, :])
                last.then_inc(s["mT_ps"], 1)

            def values(tn):
                p = tn.unit(1)
                after(pe, s["rest1"], p + 1)
                for n in range(S2):
                    last = T.matmul(pP[:, n * P:n * P + P], hT[:, n * P:n * P + P], w["Wqkv"][:, 2, :],
                                    start=True, stop=True)
                last.then_inc(s["v_ps"], 1)

            def step(tn):
                for lag, stage, *rest_ in (
                        (1, turn_input), (3, maxima, 0), (3, maxima, 1), (5, turn_output, 0), (3, maxima, 2),
                        (5, turn_output, 1), (7, ranks), (4, mix, 0, 0), (3, maxima, 3), (4, mix, 0, 1),
                        (3, maxima, 4), (4, mix, 0, 2), (4, mix, 1, 0), (3, maxima, 5), (4, mix, 1, 1),
                        (3, maxima, 6), (4, mix, 1, 2), (6, turn_router), (4, mix, 2, 0), (3, maxima, 7),
                        (4, mix, 2, 1), (3, maxima, 8), (4, mix, 2, 2), (6, logits_), (1, queries_keys),
                        (3, maxima, 9), (4, mix, 3, 0), (3, maxima, 10), (4, mix, 3, 1), (3, maxima, 11),
                        (4, mix, 3, 2), (1, values), (4, mix, 4, 0), (3, turn_max), (4, mix, 4, 1), (4, mix, 4, 2)):
                    if tn.has(lag, SEQS):
                        stage(tn, *rest_)

            pe.wait_ge(s["zeroed"], ZEROED)
            turns(pe, 3, step, SEQS + 6, 9, SEQS)

        @block.vector
        def _(dve):
            v = Chain(dve, s_v)
            v.link(V.memset(Q[0][:, :, :], 0.0))
            dve.wait_ge(s["key_ones"], 1)
            for u in range(3):
                V.tensor_scalar(K[u][:, :, :], Q[0][:, :, :], key_ones[:, 0:1], None, ALU.add)\
                    .then_inc(s["zeroed"], 1)
            for u in range(1, 3):
                V.tensor_copy(Q[u][:, :, :], Q[0][:, :, :]).then_inc(s["zeroed"], 1)
            dve.wait_ge(s["zeroed"], ZEROED)
            v.link(V.memset(c["counts"][:, :], 0.0))

            def maxima(tn, i):
                g, m = UNITS[i]
                dve.wait_ge(s["scores"], 12 * tn.unit(3) + i + 1)
                V.tensor_reduce(mx[:, m, 4 * g:4 * g + 4], pS[i % 2][:, :, :], AX.X, ALU.max).then_inc(s["max"], 1)

            def negate(tn):
                p = tn.unit(3)
                dve.wait_ge(s["max"], 12 * p + 12)
                after(dve, s["mT_ps"], p)
                v.link(V.tensor_tensor(mx[:, 1, :], mx[:, 1, :], mx[:, 2, :], ALU.max))
                V.tensor_scalar(nm[:, :, :], mx[:, 0:2, :], -1.0, None, ALU.mult).then_inc(s["neg"], 1)

            def second_max(tn):
                p = tn.unit(3)
                dve.wait_ge(s["m1"], p + 1)
                V.tensor_tensor(mT[:, 1, :], pT[0:H, 0:SEQ_LEN], mT[:, 0, :], ALU.subtract).then_inc(s["m2"], 1)

            def load(tn, piece):
                p, u = tn.unit(0), tn.ring(0)
                x = X[:, cols(2 * p, S2), :]
                if piece == 0:
                    after(dve, s_a0[u], 32 * tn.lap(0) + 32)
                    v.note(V.tensor_tensor(a0[u][:, :, :], a0[u][:, :, :],
                                           bc_last(c["gates"][:, 0, cols(2 * p, S2)], D), ALU.mult))
                elif piece == 1:
                    v.settle()
                    v.note(V.tensor_tensor(a0[u][:, :, :], a0[u][:, :, :],
                                           gbc[u][:, :].unsqueeze(1).broadcast_to([P, S2, D]), ALU.mult))
                else:
                    v.settle()
                    v.note(V.tensor_tensor(x, x, a0[u][:, :, :], ALU.add))

            def load_moments(tn, piece):
                p, u = tn.unit(0), tn.ring(0)
                v.settle()
                if piece == 0:
                    for n in range(S2):
                        last = V.bn_stats(stats[:, n, :], tile_at(X, 2 * p + n))
                    v.note(last)
                else:
                    for n in range(S2):
                        last = V.bn_aggr(mv0[u][:, n, :], stats[:, n, :])
                    last.then_inc(s["mv0"], 1)

            def norm_input(tn):
                p, u = tn.unit(0), tn.ring(0)
                after(dve, s["hT_ps"], p)
                dve.wait_ge(s["rstd0"], p + 1)
                normalize(V, lambda n: tile_at(X, 2 * p + n), lambda n: xhat[:, n, :], mv0[u], rstd0[u], S2)\
                    .then_inc(s["xhat"], 1)

            def split(tn):
                p, u = tn.unit(1), tn.ring(1)
                dve.wait_ge(s["part1"], p + 1)
                V.tensor_tensor(rest[:, :], pP[:, :], parts[u][:, 0, :], ALU.subtract).then_inc(s["rest1"], 1)

            def third_part(tn):
                p, u = tn.unit(1), tn.ring(1)
                dve.wait_ge(s["part2"], p + 1)
                V.tensor_tensor(parts[u][:, 2, :], rest[:, :], parts[u][:, 1, :], ALU.subtract)\
                    .then_inc(s["parts"], 1)

            def values(tn):
                p, u = tn.unit(1), tn.ring(1)
                dve.wait_ge(s["v_ps"], p + 1)
                after(dve, s["pv"], 4 * (p - 2))
                V.tensor_copy(vv[u][:, :, :, 0:HD1],
                              pP[:, 0:SEQ_LEN].rearrange("p (n h d) -> p n h d", n=S2, d=HD1)).then_inc(s["v"], 1)

            def denominators(tn, n):
                dve.wait_ge(s["yT_ps"], 2 * tn.unit(5) + n + 1)
                v.note(V.reciprocal(rden[:, n, :], pP[:, :].rearrange("p (h l) -> p h l", l=LAT)[:, :, HD1]))

            def tokens(tn, n):
                v.settle()
                y = pP[:, :].rearrange("p (h l) -> p h l", l=LAT)
                V.tensor_tensor(yv[:, n, :, :], y[:, :, 0:HD1], bc_last(rden[:, n, :], HD1), ALU.mult)\
                    .then_inc(s["yT"], 1)

            def output(tn, piece):
                p, u = tn.unit(5), tn.ring(5)
                x = X[:, cols(2 * p, S2), :]
                if piece == 0:
                    after(dve, s_mod[u], 16 * tn.lap(5) + 16)
                    dve.wait_ge(s["yT"], 2 * p + 2)
                    v.note(V.tensor_tensor(yv[:, :, :, :].rearrange("p n h d -> p n (h d)"),
                                           yv[:, :, :, :].rearrange("p n h d -> p n (h d)"),
                                           modbc[u][:, 0, :].unsqueeze(1).broadcast_to([P, S2, D]), ALU.mult))
                else:
                    v.settle()
                    v.note(V.tensor_tensor(x, x, yv[:, :, :, :].rearrange("p n h d -> p n (h d)"), ALU.add))

            def output_moments(tn, piece):
                p, u = tn.unit(5), tn.ring(5)
                v.settle()
                if piece == 0:
                    for n in range(S2):
                        last = V.bn_stats(stats[:, n, :], tile_at(X, 2 * p + n))
                    v.note(last)
                else:
                    for n in range(S2):
                        last = V.bn_aggr(mv1[u][:, n, :], stats[:, n, :])
                    last.then_inc(s["mv1"], 1)

            def router_input(tn, piece):
                p, u = tn.unit(6), tn.ring(6)
                if piece == 0:
                    dve.wait_ge(s["rstd1"], p + 1)
                    v.note(normalize(V, lambda n: tile_at(X, 2 * p + n), lambda n: res[:, n, :], mv1[u], rstd1[u],
                                     S2))
                elif piece == 1:
                    after(dve, s_mod[u], 16 * tn.lap(6) + 16)
                    v.settle()
                    v.note(V.tensor_tensor(res[:, :, :], res[:, :, :],
                                           modbc[u][:, 2, :].unsqueeze(1).broadcast_to([P, S2, D]), ALU.mult))
                else:
                    after(dve, s_scat[u], 64 * tn.lap(6))
                    v.settle()
                    for k in range(2):
                        last = V.tensor_tensor(rows[u][:, k, :, 0:D], res[:, :, :],
                                               modbc[u][:, 1, :].unsqueeze(1).broadcast_to([P, S2, D]), ALU.add)
                    last.then_inc(s["h2"], 1)
                    for k in range(2):
                        last = V.tensor_scalar(rows[u][:, k, :, D], c["token_id"][:, cols(2 * p, S2)],
                                               float(k * TOKENS), None, ALU.add)
                    v.note(last)

            def read_logits(tn):
                dve.wait_ge(s["lg_ps"], tn.unit(6) + 1)
                V.tensor_copy(logits[:, :, :], p_lg).then_inc(s["lg_read"], 1)

            def choose(tn):
                p = tn.unit(6)
                dve.wait_ge(s["lg_read"], p + 1)
                after(dve, s["slot"], p)
                dve.wait_ge(s["zeroed"], 1)
                dve.nop(nofuse=True)
                v.link(route(V, v, c, logits, r, S2, 1))
                V.tensor_tensor(both[:, :, :], r["pick"][:, 0, :, :], r["pick"][:, 1, :, :], ALU.add)\
                    .then_inc(s["pick"], 1)
                v.note(V.tensor_copy(top2[:, cols(2 * p, S2), :], r["top"][:, :, 0:2]))

            def step(tn):
                v.restart()
                for lag, stage, *rest_ in (
                        (3, maxima, 0), (5, denominators, 0), (3, maxima, 1), (5, tokens, 0), (3, maxima, 2),
                        (5, denominators, 1), (6, router_input, 0), (5, tokens, 1), (3, maxima, 3),
                        (6, router_input, 1), (3, maxima, 4), (6, router_input, 2), (3, maxima, 5), (5, output, 0),
                        (3, maxima, 6), (5, output, 1), (3, maxima, 7), (5, output_moments, 0), (0, load, 0),
                        (5, output_moments, 1), (3, maxima, 8), (0, load, 1), (6, read_logits), (0, load, 2),
                        (3, maxima, 9), (0, load_moments, 0), (1, split), (0, load_moments, 1), (3, maxima, 10),
                        (3, maxima, 11), (3, negate), (0, norm_input), (1, third_part), (3, second_max), (1, values),
                        (6, choose)):
                    if tn.has(lag, SEQS):
                        stage(tn, *rest_)
                v.restart()

            turns(dve, 3, step, SEQS + 5, 9, SEQS)
            v.link(V.tensor_copy(gexp[:, :], top2[:, :, 1]))
            v.announce(V.tensor_tensor(gexp[:, :], gexp[:, :], top2[:, :, 0], ALU.subtract), s["gexp"], 1)
            dve.wait_ge(s["gexp"], 2)
            v.link(V.tensor_scalar(c["gates"][:, 0, :], gexp[:, :], 1.0, None, ALU.add))
            v.link(V.reciprocal(c["gates"][:, 0, :], c["gates"][:, 0, :]))
            v.link(V.tensor_tensor(c["gates"][:, 1, :], gexp[:, :], c["gates"][:, 0, :], ALU.mult))


def finish(nc, c, out, sb, sem):
    V = nc.vector
    RINGS = 4
    X = c["X"]
    a = [sb(f"answers{u}", [P, 2, PT, D]) for u in range(RINGS)]
    gbc = sb("gate1_bc", [P, SEQS, D])
    s_gate = sem("f_gate")
    s_in = [sem(f"f_in{u}") for u in range(RINGS)]
    s_second, s_sum, s_gated, s_done, s_out = (sem("f_" + n) for n in ("second", "sum", "gated", "done", "out"))

    with nc.Block() as block:
        @block.sync
        def _(sp):
            m = c["mod_dram"][1].rearrange("s (m d) -> s m d", d=D)[:, 5:6, :]
            sp.dma_start(gbc[:, :, :], m.rearrange("s m d -> (s m) d").partition_broadcast(P)).then_inc(s_gate, 16)

            def load(tn):
                p, u = tn.unit(0), tn.ring(0)
                after(sp, s_done, p - 3)
                for k in range(2):
                    sp.dma_start(a[u][:, k, :, :], c["answers"][1][cols(PT * P * p + k * TOKENS, PT * P), :]
                                 .rearrange("(n p) d -> p n d", p=P)).then_inc(s_in[u], 16)

            turns(sp, RINGS, load, PAIRS - 1, RINGS, PAIRS)

        @block.scalar
        def _(act):
            def second(tn):
                p, u = tn.unit(0), tn.ring(0)
                act.wait_ge(s_in[u], 32 * tn.lap(0) + 32)
                for n in range(PT):
                    last = nc.scalar.activation(a[u][:, 1, n, :], a[u][:, 1, n, :], ACT.Copy,
                                                scale=c["gates"][:, 1, cols(PT * p + n, 1)])
                last.then_inc(s_second, 1)

            def store(tn):
                p = tn.unit(2)
                act.wait_ge(s_done, p + 1)
                act.dma_start(out[cols(2 * p, 2), :, :].rearrange("s (n p) d -> p (s n) d", p=P),
                              X[:, cols(PT * p, PT), :]).then_inc(s_out, 16)

            def step(tn):
                for lag, stage in ((0, second), (2, store)):
                    if tn.has(lag, PAIRS):
                        stage(tn)

            turns(act, RINGS, step, PAIRS + 1, RINGS, PAIRS)
            act.wait_ge(s_out, 16 * PAIRS)

        @block.vector
        def _(dve):
            dve.wait_ge(s_gate, 16)

            def add(tn):
                p, u = tn.unit(0), tn.ring(0)
                dve.wait_ge(s_second, p + 1)
                for n in range(PT):
                    last = V.scalar_tensor_tensor(a[u][:, 0, n, :], a[u][:, 0, n, :],
                                                  c["gates"][:, 0, cols(PT * p + n, 1)], a[u][:, 1, n, :],
                                                  ALU.mult, ALU.add)
                last.then_inc(s_sum, 1)

            def gate(tn):
                p, u = tn.unit(1), tn.ring(1)
                dve.wait_ge(s_sum, p + 1)
                for q in range(2):
                    last = V.tensor_tensor(a[u][:, 1, 2 * q:2 * q + 2, :], a[u][:, 0, 2 * q:2 * q + 2, :],
                                           gbc[:, cols(2 * p + q, 1), :].broadcast_to([P, 2, D]), ALU.mult)
                last.then_inc(s_gated, 1)

            def residual(tn):
                p, u = tn.unit(2), tn.ring(2)
                dve.wait_ge(s_gated, p + 1)
                x = X[:, cols(PT * p, PT), :]
                V.tensor_tensor(x, x, a[u][:, 1, :, :], ALU.add).then_inc(s_done, 1)

            def step(tn):
                for lag, stage in ((0, add), (1, gate), (2, residual)):
                    if tn.has(lag, PAIRS):
                        stage(tn)

            turns(dve, RINGS, step, PAIRS + 1, RINGS, PAIRS)


def load_expert_weights(sp, t, c, layer):
    pre = f"L{layer}_ffn_"
    w = E * FF // WEIGHT_PARTS
    loads = []
    for dst, src in ((c["W1"], t[pre + ("W1" if layer == 0 else "w1")].rearrange("p e f -> p (e f)")),
                     (c["W2"], t[pre + ("W2" if layer == 0 else "w2")].rearrange("p e b d -> p (e b d)"))):
        loads += [(dst[:, q * w:q * w + w], src[:, q * w:q * w + w]) for q in range(WEIGHT_PARTS)]
    loads += [(c["b1"][:, :], t[pre + "b1"]), (c["b2"][:, :], t[pre + "b2"].partition_broadcast(P))]
    for dst, src in loads:
        sp.dma_start(dst, src).then_inc(c["s_w"][layer], 16)


def experts(nc, c, sb, ps, sem, layer):
    V, A, T = nc.vector, nc.scalar, nc.tensor
    n_tiles = expert_tiles(layer)
    dump = (layer + 1) * TOKENS
    W1, W2, b1, b2, s_w = c["W1"], c["W2"], c["b1"], c["b2"], c["s_w"][layer]
    RINGS = 4
    w1 = [sb(f"w1_{u}", [P, FF]) for u in range(2)]
    xg = [sb(f"xg{u}", [P, ROW]) for u in range(RINGS)]
    xgT = [sb(f"xgT{u}", [P, P]) for u in range(2)]
    hid = [sb(f"hid{u}", [P, FB, P]) for u in range(RINGS)]
    y = [sb(f"y{u}", [P, D]) for u in range(RINGS)]
    dest = [sb(f"dest{u}", [P, 1], I32) for u in range(RINGS)]
    padding = [sb(f"padding{u}", [P, 1]) for u in range(2)]
    nti, ntf = sb("nt_i", [P, E], I32), sb("nt_f", [P, E])
    ends = sb("ends", [P, E])
    onesE = sb("ones_e", [P, E])
    jt = sb("tile_no", [P, n_tiles])
    ge = sb("past", [P, n_tiles, E - 1])
    tmp = sb("plan_tmp", [P, n_tiles, E])
    ej, sj, nj, rj = (sb(f"plan_{n}", [P, n_tiles]) for n in ("expert", "start", "rows", "row"))
    expert_i, row_i = sb("plan_expert_i", [P, n_tiles], I32), sb("plan_row_i", [P, n_tiles], I32)
    four, four_i = sb("plan_four", [P, n_tiles - 3]), sb("plan_four_i", [P, n_tiles - 3], I32)
    pad_f, pad_i = sb("pad_f", [P, E]), sb("pad_i", [P, E], I32)
    pT = [ps(f"gT{u}", [P, 512])[:, 0:P] for u in range(2)]
    pH = [ps(f"gH{u}", [P, FB, P]) for u in range(2)]
    pY = [ps(f"gY{u}", [P, 512])[:, 0:D] for u in range(2)]

    n = "experts_"
    s_iota, s_pads, s_plan, s_pad = sem(n + "iota"), sem(n + "pads"), sem(n + "plan"), sem(n + "pad")
    s_xg = [sem(n + f"xg{u}") for u in range(RINGS)]
    s_xT, s_xgT, s_w1, s_h = sem(n + "xT"), sem(n + "xgT"), sem(n + "w1"), sem(n + "h")
    s_hid, s_yps, s_y, s_dest = sem(n + "hid"), sem(n + "yps"), sem(n + "y"), sem(n + "dest")
    s_out = [sem(f"experts{layer}_out{u}", kept=True) for u in range(RINGS)]
    s_v, s_padding = sem(n + "dve"), sem(n + "padding")

    def plan_value(engine, src, j, most):
        return engine.value_load(src[0:1, cols(j, 1)], min_val=0, max_val=most)

    def expert_numbers(engine, lag):
        loaded = []

        def number(tn):
            if tn.static is not None:
                return plan_value(engine, expert_i, tn.unit(lag), E - 1)
            if tn.first == 0:
                loaded[:] = [plan_value(engine, four_i, tn.unit(lag), E ** RINGS - 1)]
            return (loaded[0] >> (3 * tn.first)) & (E - 1)
        return number

    def pad(engine, e):
        at = plan_value(engine, pad_i, e, E * REGION - P)
        engine.dma_start(c["routed"][layer][bass.ds(at, P), :], c["pad_rows"][:, :]).then_inc(s_pad, 16)

    with nc.Block() as block:
        @block.sync
        def _(sp):
            sp.wait_ge(s_pads, 1)
            for e in range(0, E, 2):
                pad(sp, e)
            sp.wait_ge(s_plan, 1)
            sp.wait_ge(s_pad, 16 * E)

            def load(tn):
                j, u = tn.unit(0), tn.ring(0)
                after(sp, s_xT, j - 3)
                after(sp, s_dest, j - 3)
                at = plan_value(sp, row_i, j, E * REGION - P)
                sp.dma_start(xg[u][:, :], c["routed"][layer][bass.ds(at, P), :]).then_inc(s_xg[u], 16)

            turns(sp, RINGS, load, n_tiles - 1, RINGS, n_tiles)

        @block.gpsimd
        def _(pool):
            nc.gpsimd.iota(c["pad_rows"][:, D:D + 1], pattern=[[0, 1]], base=dump, channel_multiplier=1,
                           allow_small_or_imprecise_dtypes=True).then_inc(s_iota, 1)
            nc.gpsimd.iota(jt[:, :], pattern=[[1, n_tiles]], base=0, channel_multiplier=0,
                           allow_small_or_imprecise_dtypes=True).then_inc(s_iota, 1)

            def scatter(tn):
                j, u = tn.unit(0), tn.ring(0)
                after_then(pool, s_y, j + 1, s_plan)
                pool.indirect_dma_start(c["answers"][layer], bass.IndirectOffsetOnAxis(ap=dest[u][:, :], axis=0),
                                        y[u][:, :], None).then_inc(s_out[u], 16)

            turns(pool, RINGS, scatter, n_tiles - 1, RINGS, n_tiles)
            for u in range(RINGS):
                pool.wait_ge(s_out[u], 16 * len(range(u, n_tiles, RINGS)))

        @block.scalar
        def _(act):
            act.wait_ge(s_pads, 1)
            for e in range(1, E, 2):
                pad(act, e)
            act.wait_ge(s_plan, 1)
            act.wait_ge(s_w, WEIGHT_LOADS)

            number = expert_numbers(act, 0)

            def hidden(tn):
                j, u = tn.unit(0), tn.ring(0)
                block0 = number(tn) * FB
                after(act, s_h, j + 1)
                after(act, s_yps, j - 3)
                for b in range(FB):
                    last = A.activation(hid[u][:, b, :], pH[u % 2][:, b, :], ACT.Relu if layer == 0 else ACT.Gelu,
                                        bias=b1[:, bass.ds(block0 + b, 1)])
                last.then_inc(s_hid, 1)

            turns(act, RINGS, hidden, n_tiles - 1, RINGS, n_tiles)

        @block.tensor
        def _(pe):
            pe.wait_ge(s_plan, 1)
            pe.wait_ge(s_w, WEIGHT_LOADS)

            def turn(tn):
                j, u = tn.unit(0), tn.ring(0)
                after(pe, s_xg[u], 16 * tn.lap(0) + 16)
                after(pe, s_xgT, j - 1)
                T.transpose(pT[u % 2][:, :], xg[u][:, 0:D], c["ident"][:, :]).then_inc(s_xT, 1)

            def up(tn):
                j, u = tn.unit(1), tn.ring(1) % 2
                after(pe, s_xgT, j + 1)
                after(pe, s_w1, j + 1)
                after(pe, s_hid, j - 1)
                for b in range(FB):
                    last = T.matmul(pH[u][:, b, :], w1[u][:, b * P:b * P + P], xgT[u][:, :], start=True, stop=True)
                last.then_inc(s_h, 1)

            def down(tn):
                j, u = tn.unit(2), tn.ring(2)
                at = number(tn) * FF
                after(pe, s_hid, j + 1)
                after(pe, s_y, j - 1)
                for b in range(FB):
                    last = T.matmul(pY[u % 2][:, :], hid[u][:, b, :], W2[:, bass.ds(at + b * D, D)],
                                    start=(b == 0), stop=(b == FB - 1))
                last.then_inc(s_yps, 1)

            number = expert_numbers(pe, 2)

            def step(tn):
                for lag, stage in ((0, turn), (1, up), (2, down)):
                    if tn.has(lag, n_tiles):
                        stage(tn)

            turns(pe, RINGS, step, n_tiles + 1, RINGS, n_tiles)

        @block.vector
        def _(dve):
            v = Chain(dve, s_v)
            counts = c["counts"]
            v.link(V.tensor_tensor(pad_f[:, :], counts[:, :], c["region0"][:, :], ALU.add))
            dve.wait_ge(s_iota, 1)
            V.tensor_copy(pad_i[:, :], pad_f[:, :]).then_inc(s_pads, 1)
            v.link(V.memset(onesE[:, :], 1.0))
            v.link(V.tensor_scalar(nti[:, :], counts[:, :], float(P - 1), None, ALU.add))
            v.link(V.tensor_scalar(nti[:, :], nti[:, :], 7, None, ALU.arith_shift_right))
            v.link(V.tensor_copy(ntf[:, :], nti[:, :]))
            v.link(V.tensor_tensor_scan(ends[:, :], onesE[:, :], ntf[:, :], 0.0, ALU.mult, ALU.add))
            dve.wait_ge(s_iota, 2)
            v.link(V.tensor_tensor(ge[:, :, :], bc_last(jt[:, :], E - 1),
                                   ends[:, 0:E - 1].unsqueeze(1).broadcast_to([P, n_tiles, E - 1]), ALU.is_ge))
            v.link(V.tensor_reduce(ej[:, :], ge[:, :, :], AX.X, ALU.add))
            V.tensor_copy(expert_i[:, :], ej[:, :])
            v.link(V.tensor_tensor(ge[:, :, :], ge[:, :, :],
                                   ntf[:, 0:E - 1].unsqueeze(1).broadcast_to([P, n_tiles, E - 1]), ALU.mult))
            V.tensor_reduce(sj[:, :], ge[:, :, :], AX.X, ALU.add)
            v.link(V.tensor_tensor(tmp[:, :, :], c["iota8"][:, :].unsqueeze(1).broadcast_to([P, n_tiles, E]),
                                   bc_last(ej[:, :], E), ALU.is_equal))
            v.link(V.tensor_tensor(tmp[:, :, :], tmp[:, :, :],
                                   counts[:, :].unsqueeze(1).broadcast_to([P, n_tiles, E]), ALU.mult))
            V.tensor_reduce(nj[:, :], tmp[:, :, :], AX.X, ALU.add)
            v.link(V.tensor_tensor(rj[:, :], jt[:, :], sj[:, :], ALU.subtract))
            v.link(V.scalar_tensor_tensor(rj[:, :], rj[:, :], float(P), nj[:, :], ALU.mult, ALU.min))
            v.link(V.scalar_tensor_tensor(rj[:, :], ej[:, :], float(REGION), rj[:, :], ALU.mult, ALU.add))
            v.link(V.scalar_tensor_tensor(four[:, :], ej[:, 3:n_tiles], float(E), ej[:, 2:n_tiles - 1], ALU.mult,
                                          ALU.add))
            v.link(V.scalar_tensor_tensor(four[:, :], four[:, :], float(E), ej[:, 1:n_tiles - 2], ALU.mult, ALU.add))
            v.link(V.scalar_tensor_tensor(four[:, :], four[:, :], float(E), ej[:, 0:n_tiles - 3], ALU.mult, ALU.add))
            V.tensor_copy(four_i[:, :], four[:, :])
            V.tensor_copy(row_i[:, :], rj[:, :]).then_inc(s_plan, 1)
            dve.wait_ge(s_plan, 1)
            dve.wait_ge(s_w, WEIGHT_LOADS)

            number, number_of_result = expert_numbers(dve, 0), expert_numbers(dve, 2)

            def prepare(tn):
                j, u = tn.unit(0), tn.ring(0)
                at = number(tn) * FF
                after(dve, s_h, j - 1)
                V.tensor_copy(w1[u % 2][:, :], W1[:, bass.ds(at, FF)]).then_inc(s_w1, 1)
                dve.wait_ge(s_xT, j + 1)
                V.tensor_copy(xgT[u % 2][:, :], pT[u % 2][:, :]).then_inc(s_xgT, 1)
                V.tensor_scalar(padding[u % 2][:, :], xg[u][:, D:D + 1], float(dump), jt[:, cols(j, 1)], ALU.is_ge,
                                ALU.mult).then_inc(s_padding, 1)
                dve.wait_ge(s_padding, j + 1)
                after(dve, s_out[u], 16 * tn.lap(0))
                V.scalar_tensor_tensor(dest[u][:, :], padding[u % 2][:, :], float(P), xg[u][:, D:D + 1], ALU.mult,
                                       ALU.add).then_inc(s_dest, 1)

            def result(tn):
                j, u = tn.unit(2), tn.ring(2)
                at = number_of_result(tn) * D
                dve.wait_ge(s_yps, j + 1)
                V.tensor_tensor(y[u][:, :], pY[u % 2][:, :], b2[:, bass.ds(at, D)], ALU.add).then_inc(s_y, 1)

            def step(tn):
                for lag, stage in ((0, prepare), (2, result)):
                    if tn.has(lag, n_tiles):
                        stage(tn)

            turns(dve, RINGS, step, n_tiles + 1, RINGS, n_tiles)


def kernel(**inputs):
    import numpy as np
    import concourse.bacc as bacc
    from concourse.bass_utils import run_bass_kernel_spmd

    nc = bacc.Bacc("TRN2", target_bir_lowering=False, num_devices=1)
    arrays, t = {}, {}
    inputs = {n: np.asarray(a) for n, a in inputs.items()}
    b_in = inputs.pop("L0_attn_b_in")
    inputs["b_in_ch"], inputs["b_in_dt"] = b_in[:6 * P], b_in[6 * P:]
    inputs["conv_rows"] = inputs["L0_attn_conv_w"].T.reshape(1, 4 * 4 * P)
    inputs["c"] = np.concatenate([inputs.pop("L0_c").T, inputs.pop("L1_c").T], axis=1)
    inputs["L0_attn_D"] = np.repeat(inputs["L0_attn_D"], HD0)
    inputs["L0_attn_conv_w"] = inputs["L0_attn_conv_w"].reshape(4, P, 4).transpose(1, 0, 2).reshape(P, 16)
    for name in ("L0_attn_conv_b", "L0_attn_norm_w", "L0_attn_D", "b_in_ch"):
        inputs[name] = inputs[name].reshape(-1, P).T
    for name in ("L0_attn_W_in", "L0_attn_W_out", "L1_attn_W_uq", "L1_attn_W_o", "L1_ffn_router_w"):
        inputs[name] = inputs[name].T
    inputs["by_channel"] = np.concatenate([inputs.pop(n) for n in BY_CHANNEL], axis=1)
    inputs["as_row"] = np.concatenate([inputs.pop(n) for n in AS_ROW])[None, :]
    inputs["low_rank"] = np.stack([inputs.pop("L1_attn_" + n) for n in ("W_dq", "W_uq", "W_dkv")], axis=1)
    for name, a in inputs.items():
        if name == "L0_ffn_W1":
            a = a.transpose(1, 0, 2)
        elif name == "L1_ffn_w1":
            a = a.transpose(2, 0, 1)
        elif name == "L0_ffn_W2":
            a = a.reshape(E, FB, P, D).transpose(2, 0, 1, 3)
        elif name == "L1_ffn_w2":
            a = a.transpose(0, 2, 1).reshape(E, FB, P, D).transpose(2, 0, 1, 3)
        elif name in ("L0_ffn_b1", "L1_ffn_b1"):
            a = a.reshape(E * FB, P).T
        elif name in ("L0_ffn_b2", "L1_ffn_b2"):
            a = a.reshape(1, E * D)
        a = np.ascontiguousarray(a)
        arrays[f"in_{name}"] = a
        t[name] = nc.dram_tensor(f"in_{name}", a.shape, mybir.dt.from_np(a.dtype), kind="ExternalInput").ap()
    out = nc.dram_tensor("out_0", (SEQS, SEQ_LEN, D), F32, kind="ExternalOutput").ap()
    build(nc, t, out)
    return run_bass_kernel_spmd(nc, [arrays], core_ids=[0]).results[0]["out_0"]
```
